# Optimizing a Trainium2 kernel written in Bass

```python
import numpy as np
import jax
import jax.numpy as jnp

def _softmax(x, axis=-1):
    return jax.nn.softmax(x, axis=axis)

def _gelu(x):
    return jax.nn.gelu(x, approximate=True)

def _silu(x):
    return jax.nn.silu(x)

def _sigmoid(x):
    return jax.nn.sigmoid(x)

def _layernorm(x, axis=-1, eps=1e-05):
    m = jnp.mean(x, axis=axis, keepdims=True)
    v = jnp.var(x, axis=axis, keepdims=True)
    return (x - m) / jnp.sqrt(v + eps)

def _scatter_add(tgt, idx, src, axis=0):
    return tgt.at[idx].add(src)

def _segment_sum(src, seg, n):
    return jax.ops.segment_sum(src, seg, n)
kernel_name = 'mk_gnn_ffn_d2_gnn_r8_33c9d3'

def setup_inputs(seed: int=0):
    np.random.seed(seed)
    _w = jnp.asarray

    def _rec_inputs():
        import jax
        import jax.numpy as jnp
        _gk = jax.random.key(seed)
        x = -0.0003713 + 1 * jax.random.normal(jax.random.fold_in(_gk, 1), (6250, 256), jnp.float32)
        _s = jax.random.randint(jax.random.fold_in(_gk, 2), (50000,), 0, 6250, jnp.int32)
        _d = jax.random.randint(jax.random.fold_in(_gk, 3), (50000,), 0, 6250, jnp.int32)
        _loop = jnp.arange(6250, dtype=jnp.int32)
        src = jnp.concatenate([_s, _d, _loop])
        dst = jnp.concatenate([_d, _s, _loop])
        _o = jnp.argsort(dst, stable=True)
        src = src[_o]
        dst = dst[_o]
        return (x, src, dst)
    x, src, dst = _rec_inputs()

    def _L0_gnn_setup():
        import jax, jax.numpy as jnp
        import numpy as np
        N_NODES = 6250
        N_HYPEREDGES = 6250
        E = 40000
        D = 256

        def _prelu(x, a):
            return jnp.where(x >= 0, x, a * x)

        def _hypergraph_conv(x, hei, W, b, num_nodes, num_edges):
            src = hei[0]
            he = hei[1]
            xw = x @ W.T
            ones = jnp.ones((hei.shape[1],), x.dtype)
            deg_n = jax.ops.segment_sum(ones, src, num_segments=num_nodes)
            deg_e = jax.ops.segment_sum(ones, he, num_segments=num_edges)
            d_inv = jnp.where(deg_n > 0, 1.0 / deg_n, 0.0)
            b_inv = jnp.where(deg_e > 0, 1.0 / deg_e, 0.0)
            edge_feat = b_inv[:, None] * jax.ops.segment_sum(xw[src], he, num_segments=num_edges)
            out = d_inv[:, None] * jax.ops.segment_sum(edge_feat[he], src, num_segments=num_nodes)
            return out + b
        key = jax.random.key(seed)
        ks = jax.random.split(key, 6)
        std = np.sqrt(2.0 / D)
        x = jax.random.normal(ks[0], (N_NODES, D), dtype=jnp.float32)
        hyper_edge_index = jax.random.randint(ks[1], (2, E), 0, N_HYPEREDGES, dtype=jnp.int64)
        W1 = jax.random.normal(ks[2], (D, D), dtype=jnp.float32) * std
        b1 = jnp.zeros((D,), jnp.float32)
        W2 = jax.random.normal(ks[3], (D, D), dtype=jnp.float32) * std
        b2 = jnp.zeros((D,), jnp.float32)
        prelu_a = jnp.asarray(0.25, jnp.float32)
        return {'x': x, 'W1': W1, 'b1': b1, 'W2': W2, 'b2': b2, 'prelu_a': prelu_a, 'hyper_edge_index': hyper_edge_index}
    _L0_gnn_all = _L0_gnn_setup()
    _L0_gnn_in = {k: v for k, v in _L0_gnn_all.items() if k in ('W1', 'b1', 'W2', 'b2', 'prelu_a')}
    del _L0_gnn_all

    def _L0_ffn_setup():
        import jax, jax.numpy as jnp
        import numpy as np
        B, T, D, H, L = (16, 512, 256, 256, 2)

        def _lstm(x, W_ih, W_hh, b_ih, b_hh):
            x_proj = jnp.einsum('btd,gd->btg', x, W_ih) + b_ih + b_hh
            h0 = jnp.zeros((x.shape[0], W_hh.shape[1]), x.dtype)
            c0 = jnp.zeros_like(h0)

            def step(carry, xp):
                h, c = carry
                gates = xp + h @ W_hh.T
                i, f, g, o = jnp.split(gates, 4, axis=-1)
                c = jax.nn.sigmoid(f) * c + jax.nn.sigmoid(i) * jnp.tanh(g)
                h = jax.nn.sigmoid(o) * jnp.tanh(c)
                return ((h, c), h)
            _, hs = jax.lax.scan(step, (h0, c0), jnp.swapaxes(x_proj, 0, 1))
            return jnp.swapaxes(hs, 0, 1)
        key = jax.random.key(seed)
        ks = jax.random.split(key, 9)
        s = 1.0 / np.sqrt(H)
        u = lambda k, shape: jax.random.uniform(k, shape, jnp.float32, -s, s)
        return {'x': jax.random.normal(ks[0], (B, T, D), jnp.float32), 'W_ih': u(ks[1], (4 * H, D)), 'W_hh': u(ks[2], (4 * H, H)), 'b_ih': u(ks[3], (4 * H,)), 'b_hh': u(ks[4], (4 * H,)), 'W_lin': u(ks[5], (L, H)), 'b_lin': u(ks[6], (L,)), 'fw_att': jnp.full((1, H), 0.001, jnp.float32), 'bw_att': jnp.full((1, H), 0.001, jnp.float32)}
    _L0_ffn_all = _L0_ffn_setup()
    _L0_ffn_in = {k: v for k, v in _L0_ffn_all.items() if k in ('W_ih', 'W_hh', 'b_ih', 'b_hh', 'W_lin', 'b_lin', 'fw_att', 'bw_att')}
    del _L0_ffn_all

    def _L1_gnn_setup():
        import jax, jax.numpy as jnp
        import numpy as np
        NEG_SLOPE = 0.2
        EPS = 1e-16

        def _one_head(x, e0, e1, W_h, a_h, n):
            d = W_h.shape[1]
            h = x @ W_h
            s_dst = h @ a_h[:d]
            s_src = h @ a_h[d:]
            logits = jax.nn.leaky_relu(s_dst[e0] + s_src[e1], NEG_SLOPE)
            m = jax.ops.segment_max(logits, e0, num_segments=n)
            ex = jnp.exp(logits - m[e0])
            denom = jax.ops.segment_sum(ex, e0, num_segments=n) + EPS
            alpha = ex / denom[e0]
            return jax.ops.segment_sum(alpha[:, None] * h[e1], e0, num_segments=n)
        key = jax.random.key(seed)
        k1, k2, k3, k4 = jax.random.split(key, 4)
        N, F_IN, HEADS, D = (12500, 256, 8, 32)
        E = 200000
        x = jax.random.normal(k1, (N, F_IN), dtype=jnp.float32)
        adj = jax.random.randint(k2, (2, E), 0, N, dtype=jnp.int32)
        W = jax.random.normal(k3, (HEADS, F_IN, D), dtype=jnp.float32) / np.sqrt(F_IN)
        a = jax.random.normal(k4, (HEADS, 2 * D), dtype=jnp.float32) / np.sqrt(2 * D)
        return {'input': x, 'adj': adj, 'W': W, 'a': a}
    _L1_gnn_all = _L1_gnn_setup()
    _L1_gnn_in = {k: v for k, v in _L1_gnn_all.items() if k in ('W', 'a')}
    del _L1_gnn_all

    def _L1_ffn_setup():
        import jax, jax.numpy as jnp
        import numpy as np
        E, D, H, TOP_K = (6, 256, 256, 2)
        ROUTER_H = D // 2
        key = jax.random.key(seed)
        ks = jax.random.split(key, 12)
        s = 1.0 / np.sqrt(D)
        sh = 1.0 / np.sqrt(H)
        sr = 1.0 / np.sqrt(ROUTER_H)
        return {'features': jax.random.normal(ks[0], (8, 512, D), dtype=jnp.float32), 'router_w1': jax.random.uniform(ks[1], (D, ROUTER_H), jnp.float32, -s, s), 'router_b1': jnp.zeros((ROUTER_H,), jnp.float32), 'router_w2': jax.random.uniform(ks[2], (ROUTER_H, E), jnp.float32, -sr, sr), 'router_b2': jnp.zeros((E,), jnp.float32), 'expert_w1': jax.random.uniform(ks[3], (E, D, H), jnp.float32, -s, s), 'expert_b1': jnp.zeros((E, H), jnp.float32), 'expert_w2': jax.random.uniform(ks[4], (E, H, H), jnp.float32, -sh, sh), 'expert_b2': jnp.zeros((E, H), jnp.float32), 'expert_w3': jax.random.uniform(ks[5], (E, H, D), jnp.float32, -sh, sh), 'expert_b3': jnp.zeros((E, D), jnp.float32)}
    _L1_ffn_all = _L1_ffn_setup()
    _L1_ffn_in = {k: v for k, v in _L1_ffn_all.items() if k in ('router_w1', 'router_b1', 'router_w2', 'router_b2', 'expert_w1', 'expert_b1', 'expert_w2', 'expert_b2', 'expert_w3', 'expert_b3')}
    del _L1_ffn_all
    return {'x': x, 'src': src, 'dst': dst, 'L0_gnn_W1': _L0_gnn_in['W1'], 'L0_gnn_b1': _L0_gnn_in['b1'], 'L0_gnn_W2': _L0_gnn_in['W2'], 'L0_gnn_b2': _L0_gnn_in['b2'], 'L0_gnn_prelu_a': _L0_gnn_in['prelu_a'], 'L0_ffn_W_ih': _L0_ffn_in['W_ih'], 'L0_ffn_W_hh': _L0_ffn_in['W_hh'], 'L0_ffn_b_ih': _L0_ffn_in['b_ih'], 'L0_ffn_b_hh': _L0_ffn_in['b_hh'], 'L0_ffn_W_lin': _L0_ffn_in['W_lin'], 'L0_ffn_b_lin': _L0_ffn_in['b_lin'], 'L0_ffn_fw_att': _L0_ffn_in['fw_att'], 'L0_ffn_bw_att': _L0_ffn_in['bw_att'], 'L1_gnn_W': _L1_gnn_in['W'], 'L1_gnn_a': _L1_gnn_in['a'], 'L1_ffn_router_w1': _L1_ffn_in['router_w1'], 'L1_ffn_router_b1': _L1_ffn_in['router_b1'], 'L1_ffn_router_w2': _L1_ffn_in['router_w2'], 'L1_ffn_router_b2': _L1_ffn_in['router_b2'], 'L1_ffn_expert_w1': _L1_ffn_in['expert_w1'], 'L1_ffn_expert_b1': _L1_ffn_in['expert_b1'], 'L1_ffn_expert_w2': _L1_ffn_in['expert_w2'], 'L1_ffn_expert_b2': _L1_ffn_in['expert_b2'], 'L1_ffn_expert_w3': _L1_ffn_in['expert_w3'], 'L1_ffn_expert_b3': _L1_ffn_in['expert_b3']}

def reference(x, src, dst, L0_gnn_W1, L0_gnn_b1, L0_gnn_W2, L0_gnn_b2, L0_gnn_prelu_a, L0_ffn_W_ih, L0_ffn_W_hh, L0_ffn_b_ih, L0_ffn_b_hh, L0_ffn_W_lin, L0_ffn_b_lin, L0_ffn_fw_att, L0_ffn_bw_att, L1_gnn_W, L1_gnn_a, L1_ffn_router_w1, L1_ffn_router_b1, L1_ffn_router_w2, L1_ffn_router_b2, L1_ffn_expert_w1, L1_ffn_expert_b1, L1_ffn_expert_w2, L1_ffn_expert_b2, L1_ffn_expert_w3, L1_ffn_expert_b3):
    import jax
    import jax.numpy as jnp

    def _L0_gnn_ref(x, W1, b1, W2, b2, prelu_a, hyper_edge_index):
        import jax, jax.numpy as jnp
        import numpy as np
        N_NODES = 6250
        N_HYPEREDGES = 6250
        E = 40000
        D = 256

        def _prelu(x, a):
            return jnp.where(x >= 0, x, a * x)

        def _hypergraph_conv(x, hei, W, b, num_nodes, num_edges):
            src = hei[0]
            he = hei[1]
            xw = x @ W.T
            ones = jnp.ones((hei.shape[1],), x.dtype)
            deg_n = jax.ops.segment_sum(ones, src, num_segments=num_nodes)
            deg_e = jax.ops.segment_sum(ones, he, num_segments=num_edges)
            d_inv = jnp.where(deg_n > 0, 1.0 / deg_n, 0.0)
            b_inv = jnp.where(deg_e > 0, 1.0 / deg_e, 0.0)
            edge_feat = b_inv[:, None] * jax.ops.segment_sum(xw[src], he, num_segments=num_edges)
            out = d_inv[:, None] * jax.ops.segment_sum(edge_feat[he], src, num_segments=num_nodes)
            return out + b
        out = _hypergraph_conv(x, hyper_edge_index, W1, b1, N_NODES, N_HYPEREDGES)
        out = _prelu(out, prelu_a)
        out = _hypergraph_conv(out, hyper_edge_index, W2, b2, N_NODES, N_HYPEREDGES)
        out = out + x
        out = _prelu(out, prelu_a)
        return out

    def _L0_ffn_ref(x, W_ih, W_hh, b_ih, b_hh, W_lin, b_lin, fw_att, bw_att):
        import jax, jax.numpy as jnp
        import numpy as np
        B, T, D, H, L = (16, 512, 256, 256, 2)

        def _lstm(x, W_ih, W_hh, b_ih, b_hh):
            x_proj = jnp.einsum('btd,gd->btg', x, W_ih) + b_ih + b_hh
            h0 = jnp.zeros((x.shape[0], W_hh.shape[1]), x.dtype)
            c0 = jnp.zeros_like(h0)

            def step(carry, xp):
                h, c = carry
                gates = xp + h @ W_hh.T
                i, f, g, o = jnp.split(gates, 4, axis=-1)
                c = jax.nn.sigmoid(f) * c + jax.nn.sigmoid(i) * jnp.tanh(g)
                h = jax.nn.sigmoid(o) * jnp.tanh(c)
                return ((h, c), h)
            _, hs = jax.lax.scan(step, (h0, c0), jnp.swapaxes(x_proj, 0, 1))
            return jnp.swapaxes(hs, 0, 1)
        lstm_out = _lstm(x, W_ih, W_hh, b_ih, b_hh)
        logits = jnp.einsum('bth,lh->btl', lstm_out, W_lin) + b_lin
        g = jax.lax.stop_gradient(jnp.argmax(logits, axis=-1).astype(lstm_out.dtype))[..., None]
        w = g * lstm_out
        inc = jnp.cumsum(w, axis=1)
        prefix = inc - w
        suffix = inc[:, -1:, :] - inc
        return 2.0 * lstm_out + prefix * fw_att + suffix * bw_att

    def _L1_gnn_ref(input, adj, W, a):
        import jax, jax.numpy as jnp
        import numpy as np
        NEG_SLOPE = 0.2
        EPS = 1e-16

        def _one_head(x, e0, e1, W_h, a_h, n):
            d = W_h.shape[1]
            h = x @ W_h
            s_dst = h @ a_h[:d]
            s_src = h @ a_h[d:]
            logits = jax.nn.leaky_relu(s_dst[e0] + s_src[e1], NEG_SLOPE)
            m = jax.ops.segment_max(logits, e0, num_segments=n)
            ex = jnp.exp(logits - m[e0])
            denom = jax.ops.segment_sum(ex, e0, num_segments=n) + EPS
            alpha = ex / denom[e0]
            return jax.ops.segment_sum(alpha[:, None] * h[e1], e0, num_segments=n)
        n = input.shape[0]
        e0, e1 = (adj[0], adj[1])
        heads = W.shape[0]
        outs = [_one_head(input, e0, e1, W[h], a[h], n) for h in range(heads)]
        return jnp.concatenate(outs, axis=1)

    def _L1_ffn_ref(features, router_w1, router_b1, router_w2, router_b2, expert_w1, expert_b1, expert_w2, expert_b2, expert_w3, expert_b3):
        import jax, jax.numpy as jnp
        import numpy as np
        E, D, H, TOP_K = (6, 256, 256, 2)
        ROUTER_H = D // 2
        rh = jax.nn.relu(features @ router_w1 + router_b1)
        expert_logits = jax.nn.softmax(rh @ router_w2 + router_b2, axis=-1)
        top_w, top_i = jax.lax.top_k(expert_logits, TOP_K)
        routing_weights = jax.nn.softmax(top_w, axis=-1)
        h1 = jax.nn.relu(jnp.einsum('bsd,edh->bseh', features, expert_w1) + expert_b1)
        h2 = jax.nn.relu(jnp.einsum('bseh,ehf->bsef', h1, expert_w2) + expert_b2)
        expert_out = jnp.einsum('bsef,efo->bseo', h2, expert_w3) + expert_b3
        sel = jnp.take_along_axis(expert_out, top_i[:, :, :, None], axis=2)
        combined = jnp.sum(sel * routing_weights[..., None], axis=2)
        return combined
    edge_index = jnp.stack([src, dst])
    x = x + _L0_gnn_ref(_layernorm(x, axis=-1), L0_gnn_W1, L0_gnn_b1, L0_gnn_W2, L0_gnn_b2, L0_gnn_prelu_a, edge_index)
    x = x + _L0_ffn_ref(_layernorm(x, axis=-1)[None], L0_ffn_W_ih, L0_ffn_W_hh, L0_ffn_b_ih, L0_ffn_b_hh, L0_ffn_W_lin, L0_ffn_b_lin, L0_ffn_fw_att, L0_ffn_bw_att)[0]
    x = x + _L1_gnn_ref(_layernorm(x, axis=-1), edge_index, L1_gnn_W, L1_gnn_a)
    x = x + _L1_ffn_ref(_layernorm(x, axis=-1)[None], L1_ffn_router_w1, L1_ffn_router_b1, L1_ffn_router_w2, L1_ffn_router_b2, L1_ffn_expert_w1, L1_ffn_expert_b1, L1_ffn_expert_w2, L1_ffn_expert_b2, L1_ffn_expert_w3, L1_ffn_expert_b3)[0]
    return x

_drawn_inputs = setup_inputs


def setup_inputs(seed=0):
    import zlib

    import numpy as np

    out = dict(_drawn_inputs(seed))
    spreads = {'L0_gnn_b1': (0.0, 0.1),
     'L0_gnn_b2': (0.0, 0.1),
     'L0_ffn_fw_att': (0.0010000000474974513, 0.6),
     'L0_ffn_bw_att': (0.0010000000474974513, 0.6),
     'L1_ffn_router_b1': (0.0, 0.273),
     'L1_ffn_router_b2': (0.0, 0.324),
     'L1_ffn_expert_b1': (0.0, 0.8),
     'L1_ffn_expert_b2': (0.0, 0.503),
     'L1_ffn_expert_b3': (0.0, 0.1)}
    factors = {'L0_gnn_W1': 4.247, 'L0_ffn_W_lin': 3.534, 'L0_ffn_b_lin': 2.753}
    for name, (base, spread) in spreads.items():
        noise = np.random.default_rng([zlib.crc32(name.encode()), seed]).standard_normal(out[name].shape)
        drawn = base * np.exp(spread * noise) if base else spread * noise
        out[name] = jnp.asarray(drawn.astype(out[name].dtype))
    for name, factor in factors.items():
        out[name] = (out[name] * factor).astype(out[name].dtype)
    return out
```

```python
from contextlib import ExitStack

import concourse.bass as bass
from concourse import mybir

F32 = mybir.dt.float32
I32 = mybir.dt.int32
ALU = mybir.AluOpType
ACT = mybir.ActivationFunctionType
AX = mybir.AxisListType

P = 128
N = 6250
D = 256
NB = 49
NP_ = NB * P
BG = 7
NG = NB // BG
BC = BG * P
E = 106250
TIT = 16
NIT = 52
NT = NIT * TIT
EP = NT * P
W = 264
H8 = 8
C = 125
L = 50
BIG = 1.0e30
SETTLED = 1.0e-6
NEXP = 6
HC = BC // 2


class Mem:

    semaphores = []

    def __init__(self, nc, ctx):
        self.nc, self.ctx = nc, ctx

    def sb(self, name, shape, dt=F32):
        return self.ctx.enter_context(self.nc.sbuf_tensor(name, shape, dt))

    def ps(self, name, shape, dt=F32):
        return self.ctx.enter_context(self.nc.psum_tensor(name, shape, dt))

    def sem(self, name):
        Mem.semaphores.append(self.nc.alloc_semaphore(name=name))
        return Mem.semaphores[-1]


def renew_semaphores(nc):
    nc.clear_and_free_semaphores(Mem.semaphores)
    nc.all_engine_barrier()
    Mem.semaphores = []


def blocks_of(t):
    return t.rearrange("(g b p) c -> g p b c", b=BG, p=P)


def stage_constants(nc, cst, io):
    with ExitStack() as ctx:
        m = Mem(nc, ctx)
        ii = m.sb("c_iota_i", [P, 256], I32)
        dst_f = m.sb("c_dst_f", [P, NT])
        base_i = m.sb("c_base_i", [1, NT], I32)
        base_f = m.sb("c_base_f", [1, NT])
        dst_i = m.sb("c_dst_i", [P, NT], I32)
        ps = m.ps("c_ps", [P, 2, 512])
        loaded, iota_ok, zeroed, ident_ok = m.sem("c_loaded"), m.sem("c_iota"), m.sem("c_zeroed"), m.sem("c_ident")
        v, bc = m.sem("c_v"), m.sem("c_bc")
        block = ctx.enter_context(nc.Block())

        @block.sync
        def _(sp):
            sp.dma_start(dst_i[:], io["dstT"]).then_inc(loaded, 16)
            for name, view in cst["loads"]:
                sp.dma_start(cst[name][:], view).then_inc(loaded, 16)
            sp.wait_ge(loaded, 16 * (1 + len(cst["loads"])))

        @block.gpsimd
        def _(pool):
            pool.iota(ii[:], [[1, 256]], base=0, channel_multiplier=0).then_inc(iota_ok, 1)
            pool.memset(cst["ident"][:], 0.0).then_inc(zeroed, 1)
            pool.wait_ge(zeroed, 1)
            pool.affine_select(out=cst["ident"][:], in_=cst["ident"][:], compare_op=ALU.not_equal, fill=1.0,
                               base=0, pattern=[[-1, P]], channel_multiplier=1).then_inc(ident_ok, 1)

        @block.vector
        def _(dve):
            dve.memset(cst["ones"][:], 1.0).then_inc(v, 1)
            dve.memset(cst["rel"][:, NT:NT + 2], 0.0).then_inc(v, 1)
            dve.wait_ge(iota_ok, 1)
            dve.tensor_copy(cst["iota"][:], ii[:]).then_inc(v, 1)
            dve.wait_ge(loaded, 16 * (1 + len(cst["loads"])))
            dve.tensor_copy(dst_f[:], dst_i[:]).then_inc(v, 1)
            dve.tensor_scalar(cst["blk"][:], dst_i[0:1, :], 7, None, ALU.arith_shift_right).then_inc(v, 1)
            dve.tensor_scalar(base_i[:], dst_i[0:1, :], -P, None, ALU.bitwise_and).then_inc(v, 1)
            dve.wait_ge(v, 6)
            dve.tensor_copy(base_f[:], base_i[:]).then_inc(v, 1)
            dve.wait_ge(bc, 2)
            for h in range(2):
                w = NT // 2
                dve.tensor_tensor(cst["rel"][:, h * w:(h + 1) * w], dst_f[:, h * w:(h + 1) * w], ps[:, h, 0:w],
                                  ALU.subtract).then_inc(v, 1)

        @block.tensor
        def _(pe):
            pe.wait_ge(v, 7)
            for h in range(2):
                w = NT // 2
                pe.matmul(ps[:, h, 0:w], cst["ones"][:], base_f[:, h * w:(h + 1) * w], start=True,
                          stop=True).then_inc(bc, 1)


def stage_gather_sum(nc, cst, name, table, idx, acc, ex=None):
    G4 = 4
    LA = 2
    OH = 4
    width = W if ex is None else D
    with ExitStack() as ctx:
        m = Mem(nc, ctx)
        rows = m.sb(f"{name}_rows", [P, TIT, W])
        ids = [m.sb(f"{name}_ids{i}", [P, TIT // 2], I32) for i in range(2)]
        onehot = [m.sb(f"{name}_onehot{i}", [P, 2 * P]) for i in range(OH)]
        part = [m.ps(f"{name}_part{i}", [P, 2, 512]) for i in range(4)]
        ids_in = [m.sem(f"{name}_ids_in{i}") for i in range(2)]
        rows_in = [m.sem(f"{name}_rows_in{i}") for i in range(G4)]
        onehot_ready = m.sem(f"{name}_onehot_ready")
        summed = m.sem(f"{name}_summed")
        added = m.sem(f"{name}_added")
        weighted, exput = m.sem(f"{name}_weighted"), m.sem(f"{name}_exput")
        issue = m.sem(f"{name}_issue")
        block = ctx.enter_context(nc.Block())

        @block.sync
        def _(sp):
            for half in range(2):
                sp.dma_start(ids[half][:], idx[0, :, half * 8:half * 8 + 8]).then_inc(ids_in[half], 16)
            with sp.Fori(0, NIT - 1) as i:
                for half in range(2):
                    for g in (2 * half, 2 * half + 1):
                        sp.wait_ge(rows_in[g], 16 * G4 * i + 16 * G4)
                    sp.dma_start(ids[half][:], idx[bass.ds(i + 1, 1), :, half * 8:half * 8 + 8]
                                 .rearrange("a p k -> (a p) k")).then_inc(ids_in[half], 16)

        @block.gpsimd
        def _(pool):
            with pool.Fori(0, NIT) as i:
                for t in range(TIT):
                    if t % 8 == 0:
                        pool.wait_ge(ids_in[t // 8], 16 * i + 16)
                    if t % G4 == 0:
                        pool.wait_ge(summed, TIT * i + t + G4)
                        pool.sem_inc(issue, 1)
                    pool.indirect_dma_start(rows[:, t, 0:width], None, table,
                                            bass.IndirectOffsetOnAxis(ids[t // 8][:, t % 8:t % 8 + 1], 0)
                                            ).then_inc(rows_in[t // G4], 16)

        if ex is not None:
            @block.scalar
            def _(act):
                with act.Fori(0, NIT) as i:
                    for t in range(TIT):
                        if t % G4 == 0:
                            act.wait_ge(summed, TIT * i + t + G4)
                        act.activation(rows[:, t, D:W],
                                       ex[:, bass.ds(TIT * i + t, 1), :].rearrange("p a h -> p (a h)"),
                                       ACT.Copy).then_inc(exput, 1)

        @block.vector
        def _(dve):
            dve.memset(acc[:], 0.0).then_inc(added, 4)

            def make_onehot(col, buf):
                dve.wait_ge(summed, col + TIT - OH + 1)
                dve.tensor_scalar(onehot[buf][:], cst["iota"][:], cst["rel"][:, bass.ds(col, 1)], None,
                                  ALU.is_equal).then_inc(onehot_ready, 1)

            for t in range(LA):
                make_onehot(t, t % OH)
            with dve.Fori(0, NIT) as i:
                for g in range(TIT // G4):
                    if ex is not None:
                        dve.wait_ge(rows_in[g], 16 * G4 * i + 16 * G4)
                        for t in range(g * G4, g * G4 + G4):
                            rv = rows[:, t, 0:D].rearrange("p (h d) -> p h d", h=H8)
                            ev = ex[:, bass.ds(TIT * i + t, 1), :].rearrange("p a h -> p (a h)")
                            dve.tensor_tensor(rv, rv, ev.unsqueeze(2).to_broadcast([P, H8, D // H8]),
                                              ALU.mult).then_inc(weighted, 1)
                    first = [dve.value_load(cst["blk"][0:1, bass.ds(TIT * i + g * G4 + k, 1)], min_val=0,
                                            max_val=NB - 1) for k in range(G4)]
                    for k in range(G4):
                        t = g * G4 + k
                        make_onehot(TIT * i + t + LA, (t + LA) % OH)
                        dve.wait_ge(summed, TIT * i + t + TIT + 1)
                        dve.wait_ge(added, TIT * i + t + 4)
                        a = acc[:, bass.ds(first[k], 2), :]
                        dve.tensor_tensor(a, a, part[t % 4][:, :, 0:W], ALU.add).then_inc(added, 1)

        @block.tensor
        def _(pe):
            pe.sem_inc(summed, TIT)
            with pe.Fori(0, NIT) as i:
                for t in range(TIT):
                    if ex is not None:
                        pe.wait_ge(weighted, TIT * i + t + 1)
                        pe.wait_ge(exput, TIT * i + t + 1)
                    elif t % G4 == 0:
                        pe.wait_ge(rows_in[t // G4], 16 * G4 * i + 16 * G4)
                    pe.wait_ge(onehot_ready, TIT * i + t + 1)
                    pe.wait_ge(added, TIT * i + t + 1)
                    pe.matmul(part[t % 4][:, 0, 0:W], onehot[t % OH][:, 0:P], rows[:, t, :], start=True, stop=True)
                    pe.matmul(part[t % 4][:, 1, 0:W], onehot[t % OH][:, P:2 * P], rows[:, t, :], start=True,
                              stop=True).then_inc(summed, 1)


def stage_edge_rows(nc, cst, acc, table, name):
    with ExitStack() as ctx:
        m = Mem(nc, ctx)
        rdeg = m.sb(f"{name}_rdeg", [P, NB])
        v, stored = m.sem(f"{name}_v"), m.sem(f"{name}_stored")
        block = ctx.enter_context(nc.Block())

        @block.vector
        def _(dve):
            dve.tensor_scalar(rdeg[:], acc[:, 0:NB, D], 1.0, None, ALU.max).then_inc(v, 1)
            dve.wait_ge(v, 1)
            dve.reciprocal(rdeg[:], rdeg[:]).then_inc(v, 1)
            dve.memset(acc[:, 0:NB, D:W], 1.0)
            dve.wait_ge(v, 2)
            with dve.Fori(0, NG) as g:
                a = acc[:, bass.ds(g * BG, BG), 0:D]
                dve.tensor_tensor(a, a, rdeg[:, bass.ds(g * BG, BG)].unsqueeze(2).to_broadcast([P, BG, D]),
                                  ALU.mult).then_inc(v, 1)

        @block.sync
        def _(sp):
            with sp.Fori(0, NG) as g:
                sp.wait_ge(v, g + 3)
                sp.dma_start(blocks_of(table)[bass.ds(g, 1)].rearrange("a p b c -> (a p) b c"),
                             acc[:, bass.ds(g * BG, BG), :]).then_inc(stored, 16)
            sp.wait_ge(stored, 16 * NG)


def batch(t, g):
    return blocks_of(t)[bass.ds(g, 1)].rearrange("a p b c -> (a p) b c")


def stage_nodes(nc, cst, name, make, steps, loads=(), norm=True, keep=None, keep_row=False, hT=None, proj=None,
                outs=(), xT=None):
    with ExitStack() as ctx:
        m = Mem(nc, ctx)
        bufs = [m.sb(f"{name}_in{i}", [P, BG, D]) for i in range(len(loads))]
        pre = m.sb(f"{name}_pre", [P, BG, D])
        row = m.sb(f"{name}_row", [P, BG, D]) if norm else pre
        tmp = m.sb(f"{name}_tmp", [P, BG, D])
        st, mv, std = m.sb(f"{name}_st", [P, BG, 6]), m.sb(f"{name}_mv", [P, BG, 2]), m.sb(f"{name}_std", [P, BG])
        rstd, var = m.sb(f"{name}_rstd", [P, BG]), m.sb(f"{name}_var", [P, BG])
        psT = [m.ps(f"{name}_psT{i}", [P, 512]) for i in range(2)]
        width = proj.shape[2] if proj is not None else 0
        if proj is not None:
            turned = [m.sb(f"{name}_turned{i}", [P, 2, P]) for i in range(2)]
            psY = [m.ps(f"{name}_psY{i}", [P, 512]) for i in range(2)]
            y = m.sb(f"{name}_y", [P, BG, max(W, width)])
        psH = None
        if hT is not None:
            hfix = m.sb(f"{name}_hfix", [P, 2, BC])
            psH = m.ps(f"{name}_psH", [P, 4, 512])
        loaded = m.sem(f"{name}_loaded")
        v = m.sem(f"{name}_v")
        kept = m.sem(f"{name}_kept")
        turn = m.sem(f"{name}_turn")
        turn_out = m.sem(f"{name}_turn_out")
        prod = m.sem(f"{name}_prod")
        prod_out = m.sem(f"{name}_prod_out")
        stored = m.sem(f"{name}_stored")
        std_ready = m.sem(f"{name}_std_ready")
        hfixed = m.sem(f"{name}_hfixed")
        hturned = m.sem(f"{name}_hturned")
        ones_set = m.sem(f"{name}_ones_set")
        stats_in = m.sem(f"{name}_stats_in")
        block = ctx.enter_context(nc.Block())
        nv = steps + (5 if norm else 0)
        no = len(outs)

        @block.sync
        def _(sp):
            sp.sem_inc(kept, 16)
            sp.sem_inc(stored, 16)
            with sp.Fori(0, NG) as g:
                if loads:
                    sp.wait_ge(v, nv * g + 1)
                for i, src in enumerate(loads):
                    sp.dma_start(bufs[i][:], batch(src, g)).then_inc(loaded, 16)
                if keep is not None:
                    sp.wait_ge(v, nv * g + 1 + (nv if keep_row else steps))
                    sp.dma_start(batch(keep, g), (row if keep_row else pre)[:]).then_inc(kept, 16)
                if proj is not None:
                    sp.wait_ge(prod_out, BG * g + BG + 1)
                    for dram, a, b in outs:
                        sp.dma_start(batch(dram, g), y[:, :, a:b]).then_inc(stored, 16)
            if keep is not None:
                sp.wait_ge(kept, 16 * NG + 16)
            if proj is not None:
                sp.wait_ge(stored, 16 * no * NG + 16)

        @block.vector
        def _(dve):
            dve.sem_inc(v, 1)
            if proj is not None and W > width:
                dve.memset(y[:, :, width:W], 1.0).then_inc(ones_set, 1)
            with dve.Fori(0, NG) as g:
                n = [0]

                def link(ins, count=True):
                    n[0] += 1
                    ins.then_inc(v, 1)
                    dve.wait_ge(v, nv * g + n[0] + 1)

                if loads:
                    dve.wait_ge(loaded, 16 * len(loads) * g + 16 * len(loads))
                if hT is not None:
                    dve.wait_ge(hturned, g + 2)
                dve.wait_ge(turn, BG * g + 1)
                if keep is not None:
                    dve.wait_ge(kept, 16 * g + 16)
                make(dve, link, g, bufs, pre, tmp, psH)
                if norm:
                    for b in range(BG):
                        ins = dve.bn_stats(st[:, b, :], pre[:, b, :])
                    link(ins)
                    dve.sem_inc(stats_in, 1)
                    for b in range(BG):
                        ins = dve.bn_aggr(mv[:, b, :], st[:, b, :])
                    link(ins)
                    link(dve.tensor_scalar(var[:], mv[:, :, 1], 1e-5, None, ALU.add))
                    dve.wait_ge(std_ready, g + 1)
                    link(dve.reciprocal(rstd[:], std[:]))
                    for b in range(BG):
                        ins = dve.tensor_scalar(row[:, b, :], pre[:, b, :], mv[:, b, 0:1], rstd[:, b:b + 1],
                                                ALU.subtract, ALU.mult)
                    link(ins)

        @block.scalar
        def _(act):
            act.sem_inc(turn_out, 1)
            act.sem_inc(prod_out, 1)
            if proj is not None and W > width:
                act.wait_ge(ones_set, 1)
            with act.Fori(0, NG) as g:
                if hT is not None:
                    act.wait_ge(hturned, g + 1)
                    act.activation(hfix[:], hT[:, :, bass.ds(g * BC, BC)], ACT.Copy).then_inc(hfixed, 1)
                if norm:
                    act.wait_ge(v, nv * g + steps + 4)
                    act.activation(std[:], var[:], ACT.Sqrt).then_inc(std_ready, 1)
                for b in range(BG + 1):
                    if b < BG:
                        act.wait_ge(turn, BG * g + b + 2)
                        if proj is not None:
                            act.wait_ge(prod, BG * g + (b if b >= 2 else 1))
                        to = turned[b % 2][:] if xT is None else xT[:, :, bass.ds(g * BC + b * P, P)]
                        act.activation(to, psT[b % 2][:, 0:D].rearrange("p (k n) -> p k n", k=2), ACT.Copy
                                       ).then_inc(turn_out, 1)
                    if b > 0 and proj is not None:
                        act.wait_ge(prod, BG * g + b + 1)
                        if b == 1:
                            act.wait_ge(stored, 16 * no * g + 16)
                        act.activation(y[:, b - 1, 0:width], psY[(b - 1) % 2][:, 0:width], ACT.Copy
                                       ).then_inc(prod_out, 1)

        @block.tensor
        def _(pe):
            pe.sem_inc(turn, 1)
            pe.sem_inc(prod, 1)
            pe.sem_inc(hturned, 1)
            with pe.Fori(0, NG) as g:
                if hT is not None:
                    pe.wait_ge(hfixed, g + 1)
                    pe.wait_ge(v, nv * g + 1)
                    for b in range(BG):
                        for k in range(2):
                            at = (b % 2) * D + k * P
                            ins = pe.transpose(psH[:, b // 2, at:at + P], hfix[:, k, b * P:(b + 1) * P],
                                               cst["ident"][:])
                    ins.then_inc(hturned, 1)
                pe.wait_ge(v, nv * g + nv + 1)
                for b in range(BG + 1):
                    if b < BG:
                        pe.wait_ge(turn_out, BG * g + (b if b >= 2 else 1))
                        for k in range(2):
                            ins = pe.transpose(psT[b % 2][:, k * P:(k + 1) * P], row[:, b, k * P:(k + 1) * P],
                                               cst["ident"][:])
                        ins.then_inc(turn, 1)
                    if b > 0 and proj is not None:
                        pe.wait_ge(turn_out, BG * g + b + 1)
                        pe.wait_ge(prod_out, BG * g + (b - 1 if b > 2 else 1))
                        for k in range(2):
                            ins = pe.matmul(psY[(b - 1) % 2][:, 0:width], turned[(b - 1) % 2][:, k, :],
                                            proj[:, k, :], start=(k == 0), stop=(k == 1))
                        ins.then_inc(prod, 1)


def rows2(w):
    return w.rearrange("(k p) n -> p k n", p=P)


def stage_load(nc, name, pairs):
    with ExitStack() as ctx:
        done = Mem(nc, ctx).sem(f"{name}_done")
        block = ctx.enter_context(nc.Block())

        @block.sync
        def _(sp):
            for to, view in pairs:
                sp.dma_start(to if isinstance(to, bass.AP) else to[:], view).then_inc(done, 16)
            sp.wait_ge(done, 16 * len(pairs))


def make_plain(dve, link, g, bufs, pre, tmp, ps):
    link(dve.tensor_copy(pre[:], bufs[0][:]))


def degree_scale(dve, link, g, acc, pre, tmp):
    r = tmp[:, :, 0]
    link(dve.tensor_scalar(r, acc[:, bass.ds(g * BG, BG), D:D + 1].rearrange("p b a -> p (b a)"), 1.0, None, ALU.max))
    link(dve.reciprocal(tmp[:, :, 1], r))
    link(dve.tensor_tensor(pre[:], acc[:, bass.ds(g * BG, BG), 0:D],
                           tmp[:, :, 1:2].to_broadcast([P, BG, D]), ALU.mult))


def bias_and_prelu(dve, link, pre, tmp, bias, slope, skip=None):
    link(dve.tensor_tensor(pre[:], pre[:], bias[:].unsqueeze(1).to_broadcast([P, BG, D]), ALU.add))
    if skip is not None:
        link(dve.tensor_tensor(pre[:], pre[:], skip[:], ALU.add))
    link(dve.tensor_scalar(tmp[:], pre[:], 0.0, slope[:, 0:1], ALU.min, ALU.mult))
    link(dve.scalar_tensor_tensor(out=pre[:], in0=pre[:], scalar=0.0, in1=tmp[:], op0=ALU.max, op1=ALU.add))


GATES = (0, 1, 3, 2)
Q4 = 4 * C


def stage_lstm_inputs(nc, cst, io, xT, xp):
    with ExitStack() as ctx:
        m = Mem(nc, ctx)
        wih = m.sb("wih", [P, 2, 4 * D])
        bih, bhh, bias = m.sb("bih", [P, 8]), m.sb("bhh", [P, 8]), m.sb("lbias", [P, 8])
        stage = [m.sb(f"xp_stage{u}", [P, 2, Q4]) for u in range(2)]
        ps = [[m.ps(f"xp_ps{u}{k}", [P, 512]) for k in range(2)] for u in range(2)]
        w_in, b_ok = m.sem("xp_w_in"), m.sem("xp_b_ok")
        made, biased = m.sem("xp_made"), m.sem("xp_biased")
        stored = [m.sem(f"xp_stored{u}") for u in range(2)]
        block = ctx.enter_context(nc.Block())

        @block.sync
        def _(sp):
            sp.dma_start(wih[:], rows2(io["WihT"])).then_inc(w_in, 16)
            sp.dma_start(bih[:], io["b_ih"]).then_inc(w_in, 16)
            sp.dma_start(bhh[:], io["b_hh"]).then_inc(w_in, 16)
            for u in range(2):
                sp.sem_inc(stored[u], 16)
            with sp.Fori(0, L // 2) as r:
                for u in range(2):
                    sp.wait_ge(biased, 4 * r + 2 * u + 6)
                    sp.dma_start(xp[bass.ds(2 * r + u, 1)].rearrange("a p q -> (a p) q"),
                                 stage[u][:].rearrange("p k q -> p (k q)")).then_inc(stored[u], 16)
            for u in range(2):
                sp.wait_ge(stored[u], 16 * (L // 2) + 16)

        @block.tensor
        def _(pe):
            pe.wait_ge(w_in, 48)
            xs = xT[:, :, 0:N].rearrange("p k (c s) -> p k s c", s=L)
            with pe.Fori(0, L // 2) as r:
                for u in range(2):
                    for k in range(2):
                        pe.wait_ge(biased, 4 * r + 2 * u + k + 1)
                        for q, gate in enumerate(GATES):
                            col = gate * D + k * P
                            for kk in range(2):
                                ins = pe.matmul(ps[u][k][:, q * C:(q + 1) * C], wih[:, kk, col:col + P],
                                                xs[:, kk, bass.ds(2 * r + u, 1), :].rearrange("p a c -> p (a c)"),
                                                start=(kk == 0), stop=(kk == 1))
                        ins.then_inc(made, 1)

        @block.vector
        def _(dve):
            dve.sem_inc(biased, 4)
            dve.wait_ge(w_in, 48)
            dve.tensor_tensor(bias[:], bih[:], bhh[:], ALU.add).then_inc(b_ok, 1)
            dve.wait_ge(b_ok, 1)
            with dve.Fori(0, L // 2) as r:
                for u in range(2):
                    for k in range(2):
                        if k == 0:
                            dve.wait_ge(stored[u], 16 * r + 16)
                        dve.wait_ge(made, 4 * r + 2 * u + k + 1)
                        dve.tensor_tensor(stage[u][:, k, :].rearrange("p (q c) -> p q c", q=4),
                                          ps[u][k][:, 0:Q4].rearrange("p (q c) -> p q c", q=4),
                                          bias[:, 4 * k:4 * k + 4].unsqueeze(2).to_broadcast([P, 4, C]),
                                          ALU.add).then_inc(biased, 1)


def stage_sweeps(nc, cst, mem, xp, name, sweeps, unless=None):
    whh, h, qc, gs, nxt, start, hist = (mem[k] for k in ("whh", "h", "qc", "gs", "nxt", "start", "hist"))
    with ExitStack() as ctx:
        m = Mem(nc, ctx)
        xin = [m.sb(f"{name}_xin{u}", [P, 2, Q4]) for u in range(2)]
        z = [m.sb(f"{name}_z{k}", [P, Q4]) for k in range(2)]
        pr = [m.sb(f"{name}_pr{k}", [P, 2 * C]) for k in range(2)]
        tc = [m.sb(f"{name}_tc{k}", [P, C]) for k in range(2)]
        dif = m.sb(f"{name}_dif", [P, 4, C])
        far = m.sb(f"{name}_far", [P, 4])
        ps = [[m.ps(f"{name}_ps{u}{k}", [P, 512]) for k in range(2)] for u in range(2)]
        ps_far = m.ps(f"{name}_ps_far", [1, P])
        x_in = [m.sem(f"{name}_x_in{u}") for u in range(2)]
        gates = [m.sem(f"{name}_gates{k}") for k in range(2)]
        z_ready = [m.sem(f"{name}_z_ready{k}") for k in range(2)]
        acted = [m.sem(f"{name}_acted{k}") for k in range(2)]
        mixed = [m.sem(f"{name}_mixed{k}") for k in range(2)]
        c_ready = [m.sem(f"{name}_c_ready{k}") for k in range(2)]
        tc_ready = [m.sem(f"{name}_tc_ready{k}") for k in range(2)]
        h_ready = [m.sem(f"{name}_h_ready{k}") for k in range(2)]
        noted = [m.sem(f"{name}_noted{k}") for k in range(2)]
        shifted = m.sem(f"{name}_shifted")
        loaded = m.sem(f"{name}_loaded")
        judged, far_turned = m.sem(f"{name}_judged"), m.sem(f"{name}_far_turned")
        block = ctx.enter_context(nc.Block())

        def only_if_needed(eng, program):
            if unless is None:
                return program()
            done = eng.value_load(unless[0:1, 0:1], min_val=0, max_val=1)
            with eng.If(done < 1):
                program()

        @block.sync
        def _(sp):
            def program():
                with sp.Fori(0, sweeps) as w:
                    with sp.Fori(0, L // 2) as r:
                        for u in range(2):
                            sp.wait_ge(z_ready[1], w * L + 2 * r + u + 1)
                            sp.dma_start(xin[u][:].rearrange("p k q -> p (k q)"),
                                         xp[bass.ds(2 * r + u, 1)].rearrange("a p q -> (a p) q")
                                         ).then_inc(x_in[u], 16)
            only_if_needed(sp, program)

        @block.tensor
        def _(pe):
            def program():
                with pe.Fori(0, sweeps) as w:
                    with pe.Fori(0, L // 2) as r:
                        for u in range(2):
                            pe.wait_ge(h_ready[0], w * (L + 1) + 2 * r + u + 1)
                            for half in range(2):
                                for q, gate in enumerate(GATES):
                                    col = gate * D + half * P
                                    pe.matmul(ps[u][half][:, q * C:(q + 1) * C], whh[:, 0, col:col + P], h[:, 0, :],
                                              start=(q == 0), stop=False, skip_group_check=True)
                            pe.wait_ge(h_ready[1], w * (L + 1) + 2 * r + u + 1)
                            for half in range(2):
                                for q, gate in enumerate(GATES):
                                    col = gate * D + half * P
                                    ins = pe.matmul(ps[u][half][:, q * C:(q + 1) * C], whh[:, 1, col:col + P],
                                                    h[:, 1, :], start=False, stop=(q == 3), skip_group_check=True)
                                ins.then_inc(gates[half], 1)
                pe.wait_ge(judged, 2)
                pe.transpose(ps_far[0:1, :], far[:, 0:1], cst["ident"][:]).then_inc(far_turned, 1)
            only_if_needed(pe, program)

        @block.scalar
        def _(act):
            def program():
                with act.Fori(0, sweeps) as w:
                    with act.Fori(0, L // 2) as r:
                        for u in range(2):
                            s = w * L + 2 * r + u
                            for k in range(2):
                                act.wait_ge(z_ready[k], s + 3)
                                act.activation(gs[:, k, 0:3 * C], z[k][:, 0:3 * C], ACT.Sigmoid).then_inc(acted[k], 1)
                                act.activation(qc[:, k, 0:C], z[k][:, 3 * C:Q4], ACT.Tanh).then_inc(acted[k], 1)
                            for k in range(2):
                                act.wait_ge(c_ready[k], s + 1)
                                act.activation(tc[k][:], qc[:, k, C:2 * C], ACT.Tanh).then_inc(tc_ready[k], 1)
            only_if_needed(act, program)

        @block.gpsimd
        def _(pool):
            def program():
                hs = hist[:, :, 0:N].rearrange("p k (c s) -> p k s c", s=L)
                for k in range(2):
                    pool.sem_inc(noted[k], 1)
                with pool.Fori(0, sweeps) as w:
                    with pool.Fori(0, L) as s:
                        for k in range(2):
                            pool.wait_ge(h_ready[k], w * (L + 1) + s + 2)
                            pool.tensor_copy(hs[:, k, bass.ds(s, 1), :].rearrange("p a c -> p (a c)"), h[:, k, :]
                                             ).then_inc(noted[k], 1)
            only_if_needed(pool, program)

        @block.vector
        def _(dve):
            def program():
                for k in range(2):
                    dve.sem_inc(z_ready[k], 2)
                with dve.Fori(0, sweeps) as w:
                    dve.tensor_copy(start[:], nxt[:]).then_inc(loaded, 1)
                    dve.tensor_copy(qc[:, :, C:2 * C], nxt[:, 2:4, :]).then_inc(loaded, 1)
                    for k in range(2):
                        dve.wait_ge(noted[k], w * L + 1)
                        dve.tensor_copy(h[:, k, :], nxt[:, k, :]).then_inc(h_ready[k], 1)
                    with dve.Fori(0, L // 2) as r:
                        for u in range(2):
                            s = w * L + 2 * r + u
                            for k in range(2):
                                if k == 0:
                                    dve.wait_ge(x_in[u], 16 * (w * (L // 2) + r) + 16)
                                dve.wait_ge(gates[k], s + 1)
                                dve.tensor_tensor(z[k][:], ps[u][k][:, 0:Q4], xin[u][:, k, :], ALU.add
                                                  ).then_inc(z_ready[k], 1)
                            for k in range(2):
                                dve.wait_ge(acted[k], 2 * s + 2)
                                dve.tensor_tensor(pr[k][:], gs[:, k, 0:2 * C], qc[:, k, :], ALU.mult
                                                  ).then_inc(mixed[k], 1)
                                dve.wait_ge(mixed[k], s + 1)
                                dve.tensor_tensor(qc[:, k, C:2 * C], pr[k][:, 0:C], pr[k][:, C:2 * C], ALU.add
                                                  ).then_inc(c_ready[k], 1)
                            for k in range(2):
                                dve.wait_ge(tc_ready[k], s + 1)
                                dve.wait_ge(noted[k], s + 1)
                                dve.tensor_tensor(h[:, k, :], gs[:, k, 2 * C:3 * C], tc[k][:], ALU.mult
                                                  ).then_inc(h_ready[k], 1)
                    for k in range(2):
                        dve.wait_ge(h_ready[k], w * (L + 1) + L + 1)
                        dve.wait_ge(c_ready[k], w * L + L)
                    for k in range(2):
                        dve.tensor_copy(nxt[:, k, 1:C], h[:, k, 0:C - 1]).then_inc(shifted, 1)
                        dve.tensor_copy(nxt[:, 2 + k, 1:C], qc[:, k, C:2 * C - 1]).then_inc(shifted, 1)
                    dve.wait_ge(shifted, 4 * w + 4)
                dve.tensor_tensor(dif[:], nxt[:], start[:], ALU.subtract).then_inc(loaded, 1)
                dve.wait_ge(loaded, 2 * sweeps + 1)
                dve.tensor_tensor(dif[:], dif[:], dif[:], ALU.mult).then_inc(judged, 1)
                dve.wait_ge(judged, 1)
                dve.tensor_reduce(far[:, 0:1], dif[:].rearrange("p k c -> p (k c)"), AX.X, ALU.max).then_inc(judged, 1)
                dve.wait_ge(far_turned, 1)
                dve.tensor_reduce(far[0:1, 1:2], ps_far[0:1, :], AX.X, ALU.max).then_inc(judged, 1)
                dve.wait_ge(judged, 3)
                dve.tensor_scalar(mem["settled"][:], far[0:1, 1:2], SETTLED * SETTLED, None, ALU.is_le
                                  ).then_inc(judged, 1)
            only_if_needed(dve, program)


def stage_gated_sums(nc, cst, io, hist):
    TC = 500
    NC_ = 13
    with ExitStack() as ctx:
        m = Mem(nc, ctx)
        wl, wlb = m.sb("wl", [P, 2, 2]), m.sb("wlb", [P, 2, 2, P])
        bl = m.sb("bl", [P, 2])
        fw, bw, nbw = m.sb("fw", [P, 2]), m.sb("bw", [P, 2]), m.sb("nbw", [P, 2])
        w, inc = m.sb("gw", [P, 2, NP_]), m.sb("inc", [P, 2, NP_])
        one = m.sb("one_row", [P, TC])
        l1 = m.sb("l1", [P, TC])
        gate = m.sb("gate", [P, TC])
        ps = [[m.ps(f"gs_ps{u}{l}", [P, 512]) for l in range(2)] for u in range(2)]
        w_in, v, logits = m.sem("gs_w_in"), m.sem("gs_v"), m.sem("gs_logits")
        spread = m.sem("gs_spread")
        block = ctx.enter_context(nc.Block())
        cols = [(i * TC, min(N, (i + 1) * TC)) for i in range(NC_)]

        @block.sync
        def _(sp):
            for to, frm in ((wl, io["W_lin"]), (bl, io["b_lin"].to_broadcast([P, 2])), (fw, io["fw"]), (bw, io["bw"])):
                sp.dma_start(to[:], frm).then_inc(w_in, 16)

        @block.tensor
        def _(pe):
            pe.wait_ge(spread, 5)
            for i, (a, b) in enumerate(cols):
                if i >= 2:
                    pe.wait_ge(v, 5 * (i - 2) + 2)
                for l in range(2):
                    for k in range(2):
                        ins = pe.matmul(ps[i % 2][l][:, 0:b - a], wlb[:, k, l, :], hist[:, k, a:b], start=(k == 0),
                                        stop=(k == 1))
                ins.then_inc(logits, 1)

        @block.vector
        def _(dve):
            dve.wait_ge(w_in, 64)
            for k in range(2):
                for l in range(2):
                    dve.tensor_copy(wlb[:, k, l, :], wl[:, k, l:l + 1].to_broadcast([P, P])).then_inc(spread, 1)
            dve.tensor_scalar(nbw[:], bw[:], -1.0, None, ALU.mult).then_inc(spread, 1)
            dve.memset(one[:], 1.0).then_inc(spread, 1)
            dve.wait_ge(spread, 6)
            for i, (a, b) in enumerate(cols):
                n = b - a
                dve.wait_ge(logits, i + 1)
                dve.tensor_scalar(l1[:, 0:n], ps[i % 2][1][:, 0:n], bl[:, 1:2], None, ALU.add).then_inc(v, 1)
                dve.wait_ge(v, 5 * i + 1)
                dve.scalar_tensor_tensor(out=gate[:, 0:n], in0=ps[i % 2][0][:, 0:n], scalar=bl[:, 0:1],
                                         in1=l1[:, 0:n], op0=ALU.add, op1=ALU.is_lt).then_inc(v, 1)
                dve.wait_ge(v, 5 * i + 2)
                dve.tensor_tensor(w[:, :, a:b], hist[:, :, a:b], gate[:, 0:n].unsqueeze(1).to_broadcast([P, 2, n]),
                                  ALU.mult).then_inc(v, 1)
                dve.wait_ge(v, 5 * i + 3)
                for k in range(2):
                    first = 0.0 if i == 0 else inc[:, k, a - 1:a]
                    dve.tensor_tensor_scan(inc[:, k, a:b], one[:, 0:n], w[:, k, a:b], first, ALU.mult, ALU.add
                                           ).then_inc(v, 1)
                dve.wait_ge(v, 5 * i + 5)
            at = [5 * NC_]

            def link(ins):
                at[0] += 1
                ins.then_inc(v, 1)
                dve.wait_ge(v, at[0])

            link(dve.tensor_tensor(w[:, :, 0:N], inc[:, :, 0:N], w[:, :, 0:N], ALU.subtract))
            for k in range(2):
                total = one[:, k:k + 1]
                link(dve.tensor_copy(total, inc[:, k, N - 1:N]))
                link(dve.tensor_scalar(inc[:, k, 0:N], inc[:, k, 0:N], total, nbw[:, k:k + 1], ALU.subtract, ALU.mult))
                link(dve.scalar_tensor_tensor(out=w[:, k, 0:N], in0=w[:, k, 0:N], scalar=fw[:, k:k + 1],
                                              in1=inc[:, k, 0:N], op0=ALU.mult, op1=ALU.add))
                link(dve.scalar_tensor_tensor(out=hist[:, k, 0:N], in0=hist[:, k, 0:N], scalar=2.0, in1=w[:, k, 0:N],
                                              op0=ALU.mult, op1=ALU.add))


def stage_clear(nc, name, views):
    with ExitStack() as ctx:
        done = Mem(nc, ctx).sem(f"{name}_done")
        block = ctx.enter_context(nc.Block())

        @block.vector
        def _(dve):
            for view in views:
                dve.memset(view, 0.0).then_inc(done, 1)
            dve.wait_ge(done, len(views))


CE = NIT * P


def stage_head_scores(nc, cst, io, proj):
    with ExitStack() as ctx:
        m = Mem(nc, ctx)
        wt, at = m.sb("hs_wt", [D // H8, H8, D]), m.sb("hs_at", [D // H8, 2, H8])
        ps = m.ps("hs_ps", [P, 2, 2 * H8])
        loaded, made, copied = m.sem("hs_loaded"), m.sem("hs_made"), m.sem("hs_copied")
        block = ctx.enter_context(nc.Block())

        @block.sync
        def _(sp):
            sp.dma_start(wt[:], io["headWT"]).then_inc(loaded, 16)
            sp.dma_start(at[:], io["headA"]).then_inc(loaded, 16)
            sp.dma_start(proj[:, :, 0:D], rows2(io["headW"])).then_inc(loaded, 16)
            sp.wait_ge(loaded, 48)

        @block.tensor
        def _(pe):
            pe.wait_ge(loaded, 48)
            for k in range(2):
                for s in range(2):
                    for hd in range(H8):
                        ins = pe.matmul(ps[:, k, s * H8 + hd:s * H8 + hd + 1], wt[:, hd, k * P:(k + 1) * P],
                                        at[:, s, hd:hd + 1], start=True, stop=True)
            ins.then_inc(made, 1)

        @block.vector
        def _(dve):
            dve.wait_ge(made, 1)
            dve.tensor_copy(proj[:, :, D:D + 2 * H8], ps[:]).then_inc(copied, 1)
            dve.wait_ge(copied, 1)


def stage_edge_weights(nc, cst, io, s_seg, s_oth, ex):
    with ExitStack() as ctx:
        m = Mem(nc, ctx)
        ga = [m.sb(f"ew_ga{u}", [P, TIT, H8]) for u in range(2)]
        gb = [m.sb(f"ew_gb{u}", [P, TIT, H8]) for u in range(2)]
        ia = [m.sb(f"ew_ia{u}", [P, TIT], I32) for u in range(2)]
        ib = [m.sb(f"ew_ib{u}", [P, TIT], I32) for u in range(2)]
        zz = m.sb("ew_z", [P, CE])
        node = m.sb("ew_node", [P, CE + 2], I32)
        cut = m.sb("ew_cut", [P, CE])
        top = m.sb("ew_top", [P, CE])
        ends = m.sb("ew_ends", [P, 2])
        line = m.sb("ew_line", [1, 2, P])
        run, carry = m.sb("ew_run", [1, P]), m.sb("ew_carry", [1, P])
        init = m.sb("ew_init", [P, 2])
        slot = [m.sb(f"ew_slot{u}", [P, P]) for u in range(2)]
        ps = [m.ps(f"ew_ps{u}", [P, 512]) for u in range(2)]
        ps_line = [m.ps(f"ew_psl{r}", [1, 2, P]) for r in range(2)]
        ps_init = m.ps("ew_psi", [P, 512])
        ids_in = [m.sem(f"ew_ids_in{u}") for u in range(2)]
        rows_in = [m.sem(f"ew_rows_in{u}") for u in range(2)]
        summed, copied = m.sem("ew_summed"), m.sem("ew_copied")
        node_in, v, turned = m.sem("ew_node_in"), m.sem("ew_v"), m.sem("ew_turned")
        exped, back_out, issue = m.sem("ew_exped"), m.sem("ew_back_out"), m.sem("ew_issue")
        eturned = m.sem("ew_eturned")
        block = ctx.enter_context(nc.Block())
        PER = 16 * 2 * TIT
        END = [0]

        @block.sync
        def _(sp):
            for j in range(TIT):
                sp.dma_start(node[j * H8:(j + 1) * H8, :], io["dst_pieces"][j:j + 1, :].to_broadcast([H8, CE + 2])
                             ).then_inc(node_in, 16)
            for u in range(2):
                sp.dma_start(ia[u][:], io["dst_cols"][u]).then_inc(ids_in[u], 16)
                sp.dma_start(ib[u][:], io["src_cols"][u]).then_inc(ids_in[u], 16)
            with sp.Fori(0, NIT // 2 - 1) as r:
                for u in range(2):
                    sp.wait_ge(rows_in[u], PER * r + PER)
                    for to, frm in ((ia[u], io["dst_cols"]), (ib[u], io["src_cols"])):
                        sp.dma_start(to[:], frm[bass.ds(2 * r + 2 + u, 1)].rearrange("a p k -> (a p) k")
                                     ).then_inc(ids_in[u], 16)
            sp.wait_ge(node_in, 16 * TIT)

        @block.gpsimd
        def _(pool):
            with pool.Fori(0, NIT // 2) as r:
                for u in range(2):
                    pool.wait_ge(ids_in[u], 32 * r + 32)
                    pool.wait_ge(summed, 2 * r + u + 1)
                    pool.sem_inc(issue, 1)
                    for table, g, ids in ((s_seg, ga[u], ia[u]), (s_oth, gb[u], ib[u])):
                        for j in range(TIT):
                            pool.indirect_dma_start(g[:, j, :], None, table,
                                                    bass.IndirectOffsetOnAxis(ids[:, j:j + 1], 0)
                                                    ).then_inc(rows_in[u], 16)

        @block.tensor
        def _(pe):
            pe.sem_inc(summed, 2)
            with pe.Fori(0, NIT // 2) as r:
                for u in range(2):
                    pe.wait_ge(rows_in[u], PER * r + PER)
                    pe.wait_ge(copied, 2 * r + u + 1)
                    pe.matmul(ps[u][:, 0:P], ga[u][:].rearrange("p j h -> p (j h)"), cst["ident"][:], start=True,
                              stop=False)
                    pe.matmul(ps[u][:, 0:P], gb[u][:].rearrange("p j h -> p (j h)"), cst["ident"][:], start=False,
                              stop=True).then_inc(summed, 1)
            for rd, base in ((0, FORTH1), (1, BACK1)):
                pe.wait_ge(v, base)
                for c in range(2):
                    ins = pe.transpose(ps_line[rd][0:1, c, :], ends[:, c:c + 1], cst["ident"][:])
                ins.then_inc(turned, 1)
                pe.wait_ge(v, base + CARRIED)
                pe.matmul(ps_init[:, rd:rd + 1], carry[0:1, :], cst["ones"][0:1, 0:1], start=True, stop=True
                          ).then_inc(turned, 1)
            with pe.Fori(0, NIT // 2) as r:
                for u in range(2):
                    pe.wait_ge(exped, 2 * r + u + 3)
                    pe.wait_ge(back_out, 2 * r + u + 1)
                    pe.transpose(ps[u][:, 0:P], slot[u][:], cst["ident"][:]).then_inc(eturned, 1)

        @block.scalar
        def _(act):
            act.sem_inc(copied, 2)
            act.sem_inc(exped, 2)
            with act.Fori(0, NIT // 2) as r:
                for u in range(2):
                    act.wait_ge(summed, 2 * r + u + 3)
                    act.activation(zz[:, bass.ds((2 * r + u) * P, P)], ps[u][:, 0:P], ACT.Copy).then_inc(copied, 1)
            act.wait_ge(v, LAST)
            with act.Fori(0, NIT // 2) as r:
                for u in range(2):
                    act.wait_ge(back_out, 2 * r + u + 1)
                    act.activation(slot[u][:], zz[:, bass.ds((2 * r + u) * P, P)], ACT.Exp).then_inc(exped, 1)

        @block.vector
        def _(dve):
            at = [0]

            def link(ins):
                at[0] += 1
                ins.then_inc(v, 1)
                dve.wait_ge(v, at[0])

            def carry_over(rd):
                dve.wait_ge(turned, 2 * rd + 1)
                link(dve.tensor_copy(line[:].rearrange("a c (h j) -> a c h j", h=H8),
                                     ps_line[rd][:].rearrange("a c (j h) -> a c h j", h=H8)))
                first = line[0:1, 1, :].rearrange("a (h j) -> a h j", j=TIT)
                edge = slice(0, 1) if rd == 0 else slice(TIT - 1, TIT)
                link(dve.memset(first[:, :, edge], -BIG))
                a, b = line[0:1, 1, :], line[0:1, 0, :]
                o = run[0:1, :]
                if rd:
                    a, b, o = a[:, ::-1], b[:, ::-1], o[:, ::-1]
                link(dve.tensor_tensor_scan(o, a, b, -BIG, ALU.add, ALU.max))
                link(dve.memset(carry[:], -BIG))
                cv = carry[:].rearrange("a (j h) -> a h j", j=TIT)
                rv = run[:].rearrange("a (h j) -> a h j", j=TIT)
                if rd == 0:
                    link(dve.tensor_copy(cv[:, :, 1:TIT], rv[:, :, 0:TIT - 1]))
                else:
                    link(dve.tensor_copy(cv[:, :, 0:TIT - 1], rv[:, :, 1:TIT]))
                dve.wait_ge(turned, 2 * rd + 2)
                link(dve.tensor_copy(init[:, rd:rd + 1], ps_init[:, rd:rd + 1]))

            dve.sem_inc(back_out, 2)
            dve.wait_ge(node_in, 16 * TIT)
            dve.wait_ge(copied, NIT + 2)
            link(dve.scalar_tensor_tensor(out=zz[:], in0=zz[:], scalar=0.2, in1=zz[:], op0=ALU.mult, op1=ALU.max))
            link(dve.tensor_tensor(cut[:], node[:, 1:CE + 1], node[:, 0:CE], ALU.not_equal))
            link(dve.tensor_scalar(cut[:], cut[:], -BIG, None, ALU.mult))
            link(dve.tensor_tensor_scan(top[:], cut[:], zz[:], -BIG, ALU.add, ALU.max))
            link(dve.tensor_copy(ends[:, 0:1], top[:, CE - 1:CE]))
            link(dve.tensor_reduce(ends[:, 1:2], cut[:], AX.X, ALU.min))
            assert at[0] == FORTH1
            carry_over(0)
            link(dve.tensor_tensor_scan(top[:], cut[:], zz[:], init[:, 0:1], ALU.add, ALU.max))
            link(dve.tensor_tensor(cut[:], node[:, 1:CE + 1], node[:, 2:CE + 2], ALU.not_equal))
            link(dve.tensor_scalar(cut[:], cut[:], -BIG, None, ALU.mult))
            link(dve.tensor_tensor_scan(top[:, ::-1], cut[:, ::-1], top[:, ::-1], -BIG, ALU.add, ALU.max))
            link(dve.tensor_copy(ends[:, 0:1], top[:, 0:1]))
            link(dve.tensor_reduce(ends[:, 1:2], cut[:], AX.X, ALU.min))
            assert at[0] == BACK1, at[0]
            carry_over(1)
            link(dve.tensor_tensor_scan(top[:, ::-1], cut[:, ::-1], top[:, ::-1], init[:, 1:2], ALU.add, ALU.max))
            link(dve.tensor_tensor(zz[:], zz[:], top[:], ALU.subtract))
            assert at[0] == LAST, at[0]
            ev = ex[:].rearrange("p (j i) h -> p i j h", i=NIT)
            with dve.Fori(0, NIT // 2) as r:
                for u in range(2):
                    dve.wait_ge(eturned, 2 * r + u + 1)
                    dve.tensor_copy(ev[:, bass.ds(2 * r + u, 1), :, :].rearrange("p a j h -> p (a j) h"),
                                    ps[u][:, 0:P].rearrange("p (j h) -> p j h", h=H8)).then_inc(back_out, 1)


CARRIED = 5
FORTH1 = 6
BACK1 = FORTH1 + 6 + 6
LAST = BACK1 + 6 + 2


def stage_experts(nc, cst, io, xT, x3, out):
    with ExitStack() as ctx:
        m = Mem(nc, ctx)
        w1, w2, w3 = (m.sb(f"ew{i}", [P, NEXP, 2, D]) for i in (1, 2, 3))
        b1, b2 = m.sb("eb1", [P, NEXP, 2]), m.sb("eb2", [P, NEXP, 2])
        b3 = m.sb("eb3", [1, NEXP, D])
        rw1, rb1, rw2, rb2 = m.sb("rw1", [P, 2, P]), m.sb("rb1", [P, 1]), m.sb("rw2", [P, NEXP]), m.sb("rb2", [1, NEXP])
        x = m.sb("ex_x", [P, 2, BC])
        rh = m.sb("ex_rh", [P, BC])
        h1, h2 = m.sb("ex_h1", [P, 2, BC]), m.sb("ex_h2", [P, 2, BC])
        tot = m.sb("ex_tot", [P, BG, D])
        lg, pr, oh1, oh2, key, wt = (m.sb(f"ex_{n}", [P, BG, NEXP]) for n in ("lg", "pr", "oh1", "oh2", "key", "wt"))
        s = [m.sb(f"ex_s{i}", [P, BG, 1]) for i in range(8)]
        psh = m.ps("ex_psh", [P, 4, 512])
        psy = [m.ps(f"ex_psy{i}", [P, 512]) for i in range(3)]
        psl = m.ps("ex_psl", [P, 512])
        w_in, x_in, stored = m.sem("ex_w_in"), m.sem("ex_x_in"), m.sem("ex_stored")
        fixed = m.sem("ex_fixed")
        up = m.sem("ex_up")
        act_up = m.sem("ex_act_up")
        lgs, v, ydone, yadd = m.sem("ex_lgs"), m.sem("ex_v"), m.sem("ex_ydone"), m.sem("ex_yadd")
        expd, mixed = m.sem("ex_expd"), m.sem("ex_mixed")
        block = ctx.enter_context(nc.Block())
        UP = 2 + NEXP * 8
        NV = 24
        NY = NEXP * BG

        @block.sync
        def _(sp):
            sp.sem_inc(stored, 16)
            for to, frm in ((w1[:], io["ew1"]), (w2[:], io["ew2"]), (w3[:], io["ew3"]), (b1[:], io["eb1"]),
                            (b2[:], io["eb2"]), (b3[:], io["eb3"]), (rw1[:], rows2(io["rw1"])), (rb1[:], io["rb1"]),
                            (rw2[:], io["rw2"]), (rb2[:], io["rb2"])):
                sp.dma_start(to, frm).then_inc(w_in, 16)
            with sp.Fori(0, NG) as g:
                sp.wait_ge(stored, 16 * g + 16)
                sp.dma_start(tot[:], batch(x3, g)).then_inc(x_in, 16)
                sp.wait_ge(yadd, NY * g + NY + 3)
                sp.dma_start(batch(out, g), tot[:]).then_inc(stored, 16)
            sp.wait_ge(stored, 16 * NG + 16)

        @block.tensor
        def _(pe):
            pe.wait_ge(w_in, 160)
            pe.sem_inc(up, 1)
            with pe.Fori(0, NG) as g:
                n = [0]

                def pair(lhs, src, need):
                    for c in range(2):
                        bank = n[0] % 4
                        pe.wait_ge(act_up, UP * g + max(n[0] - 3, 0) + 4 - 3 * (n[0] < 4))
                        for k in range(2):
                            ins = pe.matmul(psh[:, bank, 0:HC], lhs[k], src[:, k, c * HC:(c + 1) * HC],
                                            start=(k == 0), stop=(k == 1))
                        ins.then_inc(up, 1)
                        n[0] += 1

                pe.wait_ge(fixed, g + 1)
                pair([rw1[:, k, :] for k in range(2)], x, None)
                pe.wait_ge(act_up, UP * g + 2 + 1)
                pe.wait_ge(v, NV * g + 1)
                for b in range(BG):
                    pe.matmul(psl[:, b * NEXP:(b + 1) * NEXP], rh[:, b * P:(b + 1) * P], rw2[:], start=True,
                              stop=False)
                    ins = pe.matmul(psl[:, b * NEXP:(b + 1) * NEXP], cst["ones"][:], rb2[:], start=False, stop=True)
                ins.then_inc(lgs, 1)
                for e in range(NEXP):
                    for mm in range(2):
                        pair([w1[:, e, k, mm * P:(mm + 1) * P] for k in range(2)], x, None)
                    pe.wait_ge(act_up, UP * g + n[0] + 1)
                    for mm in range(2):
                        pair([w2[:, e, k, mm * P:(mm + 1) * P] for k in range(2)], h1, None)
                    pe.wait_ge(act_up, UP * g + n[0] + 1)
                    for b in range(BG):
                        y = e * BG + b
                        pe.wait_ge(yadd, NY * g + y + 1)
                        for k in range(2):
                            pe.matmul(psy[y % 3][:, 0:D], h2[:, k, b * P:(b + 1) * P], w3[:, e, k, :],
                                      start=(k == 0), stop=False)
                        pe.matmul(psy[y % 3][:, 0:D], cst["ones"][:], b3[0:1, e, :], start=False, stop=True
                                  ).then_inc(ydone, 1)

        @block.scalar
        def _(act):
            act.wait_ge(w_in, 160)
            act.sem_inc(act_up, 1)
            with act.Fori(0, NG) as g:
                n = [0]

                def relu(to, bias, free=None):
                    for c in range(2):
                        act.wait_ge(up, UP * g + n[0] + 2)
                        if free is not None:
                            act.wait_ge(*free)
                        act.activation(to[:, c * HC:(c + 1) * HC], psh[:, n[0] % 4, 0:HC], ACT.Relu, bias=bias
                                       ).then_inc(act_up, 1)
                        n[0] += 1

                act.wait_ge(up, UP * g + 1)
                act.activation(x[:], xT[:, :, bass.ds(g * BC, BC)], ACT.Copy).then_inc(fixed, 1)
                relu(rh[:], rb1[:, 0:1])
                for e in range(NEXP):
                    for mm in range(2):
                        relu(h1[:, mm, :], b1[:, e, mm:mm + 1])
                    if e == 0:
                        act.wait_ge(v, NV * g + 4)
                        act.activation(pr[:], lg[:], ACT.Exp).then_inc(expd, 1)
                        act.wait_ge(v, NV * g + 17)
                        act.activation(s[5][:], s[4][:], ACT.Exp).then_inc(expd, 1)
                    for mm in range(2):
                        relu(h2[:, mm, :], b2[:, e, mm:mm + 1],
                             free=(ydone, NY * g + BG * e) if e else (yadd, NY * g + 1))

        @block.vector
        def _(dve):
            dve.wait_ge(w_in, 160)
            dve.sem_inc(yadd, 3)
            dve.sem_inc(v, 1)
            with dve.Fori(0, NG) as g:
                at = [0]

                def link(ins):
                    at[0] += 1
                    ins.then_inc(v, 1)
                    dve.wait_ge(v, NV * g + at[0] + 1)

                def wide(t):
                    return t[:].to_broadcast([P, BG, NEXP])

                iota = cst["iota"][:, 0:NEXP].unsqueeze(1).to_broadcast([P, BG, NEXP])

                def pick(first, val, oh):
                    link(dve.tensor_tensor(key[:], pr[:], wide(val), ALU.not_equal))
                    link(dve.tensor_scalar(key[:], key[:], 64.0, None, ALU.mult))
                    link(dve.tensor_tensor(key[:], key[:], iota, ALU.add))
                    link(dve.tensor_reduce(first[:], key[:], AX.X, ALU.min))
                    link(dve.tensor_tensor(oh[:], iota, wide(first), ALU.is_equal))

                dve.wait_ge(lgs, g + 1)
                lv = psl[:, 0:BG * NEXP].rearrange("p (b e) -> p b e", b=BG)
                link(dve.tensor_copy(lg[:], lv))
                link(dve.tensor_reduce(s[0][:], lg[:], AX.X, ALU.max))
                link(dve.tensor_tensor(lg[:], lg[:], wide(s[0]), ALU.subtract))
                dve.wait_ge(expd, 2 * g + 1)
                link(dve.tensor_reduce(s[1][:], pr[:], AX.X, ALU.add))
                link(dve.reciprocal(s[1][:], s[1][:]))
                link(dve.tensor_tensor(pr[:], pr[:], wide(s[1]), ALU.mult))
                link(dve.tensor_reduce(s[2][:], pr[:], AX.X, ALU.max))
                pick(s[3], s[2], oh1)
                link(dve.scalar_tensor_tensor(out=pr[:], in0=oh1[:], scalar=-4.0, in1=pr[:], op0=ALU.mult,
                                              op1=ALU.add))
                link(dve.tensor_reduce(s[6][:], pr[:], AX.X, ALU.max))
                link(dve.tensor_tensor(s[4][:], s[6][:], s[2][:], ALU.subtract))
                link(dve.tensor_copy(s[7][:], s[2][:]))
                dve.wait_ge(expd, 2 * g + 2)
                pick(s[3], s[6], oh2)
                link(dve.tensor_scalar(s[0][:], s[5][:], 1.0, None, ALU.add))
                link(dve.reciprocal(s[0][:], s[0][:]))
                link(dve.tensor_tensor(oh2[:], oh2[:], wide(s[5]), ALU.mult))
                assert at[0] == NV
                dve.tensor_tensor(oh1[:], oh1[:], oh2[:], ALU.add).then_inc(mixed, 1)
                dve.wait_ge(mixed, 2 * g + 1)
                dve.tensor_tensor(wt[:], oh1[:], wide(s[0]), ALU.mult).then_inc(mixed, 1)
                dve.wait_ge(mixed, 2 * g + 2)
                dve.wait_ge(x_in, 16 * g + 16)
                for e in range(NEXP):
                    for b in range(BG):
                        y = e * BG + b
                        dve.wait_ge(ydone, NY * g + y + 1)
                        if e:
                            dve.wait_ge(yadd, NY * g + y - BG + 1 + 3)
                        dve.scalar_tensor_tensor(out=tot[:, b, :], in0=psy[y % 3][:, 0:D], scalar=wt[:, b, e:e + 1],
                                                 in1=tot[:, b, :], op0=ALU.mult, op1=ALU.add).then_inc(yadd, 1)


def build(nc, io, out):
    def dram(name, shape, dt=F32):
        return nc.dram_tensor(name, shape, dt, kind="Internal").ap()

    Mem.semaphores = []
    with ExitStack() as ctx:
        m = Mem(nc, ctx)
        cst = {
            "ident": m.sb("ident", [P, P]), "iota": m.sb("iota", [P, 256]), "ones": m.sb("ones", [1, P]),
            "rel": m.sb("rel", [P, NT + 2]), "blk": m.sb("blk", [1, NT], I32),
            "slope": m.sb("slope", [P, 1]),
        }
        cst["loads"] = [("slope", io["prelu_a"].to_broadcast([P, 1]))]
        stage_constants(nc, cst, io)
        tables = [dram(f"table{i}", (NP_, W)) for i in range(2)]
        xn_d, x1_d, x2_d, x3_d = (dram(n, (NP_, D)) for n in ("xn_d", "x1_d", "x2_d", "x3_d"))
        xp = dram("xp_d", (L, P, 2 * Q4))

        with ExitStack() as lctx:
            hist = Mem(nc, lctx).sb("hist", [P, 2, NP_])
            with ExitStack() as gctx:
                gm = Mem(nc, gctx)
                w1, w2 = gm.sb("w1", [P, 2, D]), gm.sb("w2", [P, 2, D])
                b1, b2 = gm.sb("b1", [P, D]), gm.sb("b2", [P, D])
                stage_load(nc, "gw", [(w1, rows2(io["W1T"])), (w2, rows2(io["W2T"])),
                                      (b1, io["b1"].to_broadcast([P, D])), (b2, io["b2"].to_broadcast([P, D]))])
                acc = gm.sb("acc", [P, NB + 1, W])
                stage_nodes(nc, cst, "n1", make_plain, 1, loads=[io["x"]], keep=xn_d, keep_row=True, proj=w1,
                            outs=[(tables[0], 0, W)])
                stage_gather_sum(nc, cst, "s1", tables[0], io["idx"], acc)
                stage_edge_rows(nc, cst, acc, tables[1], "e1")
                stage_gather_sum(nc, cst, "s2", tables[1], io["idx"], acc)

                def make_mid(dve, link, g, bufs, pre, tmp, ps):
                    degree_scale(dve, link, g, acc, pre, tmp)
                    bias_and_prelu(dve, link, pre, tmp, b1, cst["slope"])

                stage_nodes(nc, cst, "n2", make_mid, 6, norm=False, proj=w2, outs=[(tables[0], 0, W)])
                stage_gather_sum(nc, cst, "s3", tables[0], io["idx"], acc)
                stage_edge_rows(nc, cst, acc, tables[1], "e2")
                stage_gather_sum(nc, cst, "s4", tables[1], io["idx"], acc)

                def make_x1(dve, link, g, bufs, pre, tmp, ps):
                    degree_scale(dve, link, g, acc, pre, tmp)
                    bias_and_prelu(dve, link, pre, tmp, b2, cst["slope"], skip=bufs[1])
                    link(dve.tensor_tensor(pre[:], pre[:], bufs[0][:], ALU.add))

                stage_nodes(nc, cst, "n3", make_x1, 8, loads=[io["x"], xn_d], keep=x1_d, xT=hist)
            stage_lstm_inputs(nc, cst, io, hist, xp)
            with ExitStack() as sctx:
                sm = Mem(nc, sctx)
                mem = {"whh": sm.sb("whh", [P, 2, 4 * D]), "h": sm.sb("h", [P, 2, C]), "qc": sm.sb("qc", [P, 2, 2 * C]),
                       "gs": sm.sb("gs", [P, 2, 3 * C]), "nxt": sm.sb("nxt", [P, 4, C]),
                       "start": sm.sb("start", [P, 4, C]), "settled": sm.sb("settled", [1, 1], I32), "hist": hist}
                stage_clear(nc, "lz", [mem["nxt"][:], hist[:, :, N:NP_]])
                stage_load(nc, "lw", [(mem["whh"], rows2(io["WhhT"]))])
                stage_sweeps(nc, cst, mem, xp, "sw", 2)
                stage_sweeps(nc, cst, mem, xp, "sx", C - 2 + 1, unless=mem["settled"])
            renew_semaphores(nc)
            stage_gated_sums(nc, cst, io, hist)
            with ExitStack() as actx:
                am = Mem(nc, actx)
                proj = am.sb("head_proj", [P, 2, D + 2 * H8])
                stage_head_scores(nc, cst, io, proj)
                h_t, s_seg, s_oth = dram("h_t", (NP_, D)), dram("s_seg", (NP_, H8)), dram("s_oth", (NP_, H8))

                def make_x2(dve, link, g, bufs, pre, tmp, psH):
                    link(dve.tensor_tensor(pre[:], psH[:].rearrange("p a (b d) -> p (a b) d", b=2)[:, 0:BG, :],
                                           bufs[0][:], ALU.add))

                stage_nodes(nc, cst, "n4", make_x2, 1, loads=[x1_d], keep=x2_d, hT=hist, proj=proj,
                            outs=[(h_t, 0, D), (s_seg, D, D + H8), (s_oth, D + H8, D + 2 * H8)])
        with ExitStack() as mctx:
            x3T = Mem(nc, mctx).sb("x3T", [P, 2, NP_])
            with ExitStack() as ectx:
                em = Mem(nc, ectx)
                ex = em.sb("ex", [P, NT, H8])
                stage_edge_weights(nc, cst, io, s_seg, s_oth, ex)
                acc = em.sb("acc_att", [P, NB + 1, W])
                stage_gather_sum(nc, cst, "s5", h_t, io["idx"], acc, ex=ex)

                def make_x3(dve, link, g, bufs, pre, tmp, ps):
                    link(dve.tensor_scalar(tmp[:, :, 0:H8], acc[:, bass.ds(g * BG, BG), D:W], 1e-16, None, ALU.add))
                    link(dve.reciprocal(tmp[:, :, H8:2 * H8], tmp[:, :, 0:H8]))
                    for b in range(BG):
                        ins = dve.tensor_tensor(pre[:, b, :].rearrange("p (h d) -> p h d", h=H8),
                                                acc[:, bass.ds(g * BG + b, 1), 0:D]
                                                .rearrange("p a (h d) -> p (a h) d", h=H8),
                                                tmp[:, b, H8:2 * H8].unsqueeze(2).to_broadcast([P, H8, D // H8]),
                                                ALU.mult)
                    link(ins)
                    link(dve.tensor_tensor(pre[:], pre[:], bufs[0][:], ALU.add))

                stage_nodes(nc, cst, "n5", make_x3, 4, loads=[x2_d], keep=x3_d, xT=x3T)
            stage_experts(nc, cst, io, x3T, x3_d, out)


def layout(z):
    import numpy as np
    a = {k: np.asarray(v) for k, v in z.items()}
    src = np.concatenate([a["src"], np.zeros(EP - E, np.int32)]).reshape(NT, P)
    dst = np.concatenate([a["dst"], np.full(EP - E, NP_ - 1, np.int32)]).reshape(NT, P)
    tiles = lambda t: np.ascontiguousarray(t.reshape(NIT, TIT, P).transpose(0, 2, 1))
    cols = lambda t: np.ascontiguousarray(t.reshape(TIT, NIT, P).transpose(1, 2, 0))
    row = lambda v: np.ascontiguousarray(v.reshape(1, -1))
    gate_cols = lambda v: np.ascontiguousarray(v.reshape(4, 2, P)[list(GATES)].transpose(2, 1, 0).reshape(P, 8))
    half_cols = lambda v: np.ascontiguousarray(v.reshape(-1, P).T)
    flat = dst.reshape(-1)
    ringed = np.concatenate([[-1], flat, [-1]]).astype(np.int32)
    piece = EP // TIT
    pieces = np.stack([ringed[j * piece:j * piece + piece + 2] for j in range(TIT)])
    halves = lambda w: np.ascontiguousarray(w.reshape(NEXP, 2, P, D).transpose(2, 0, 1, 3))
    cols2 = lambda b: np.ascontiguousarray(b.reshape(NEXP, 2, P).transpose(2, 0, 1))
    return {
        "x": np.concatenate([a["x"], np.zeros((NP_ - N, D), np.float32)]),
        "idx": tiles(src), "src_cols": cols(src), "dst_cols": cols(dst),
        "dstT": np.ascontiguousarray(dst.T), "dst": row(dst),
        "prelu_a": a["L0_gnn_prelu_a"].reshape(1, 1),
        "W1T": np.ascontiguousarray(a["L0_gnn_W1"].T), "W2T": np.ascontiguousarray(a["L0_gnn_W2"].T),
        "WihT": np.ascontiguousarray(a["L0_ffn_W_ih"].T), "WhhT": np.ascontiguousarray(a["L0_ffn_W_hh"].T),
        "b_ih": gate_cols(a["L0_ffn_b_ih"]), "b_hh": gate_cols(a["L0_ffn_b_hh"]),
        "W_lin": np.ascontiguousarray(a["L0_ffn_W_lin"].reshape(2, 2, P).transpose(2, 1, 0)),
        "b_lin": row(a["L0_ffn_b_lin"]), "fw": half_cols(a["L0_ffn_fw_att"]), "bw": half_cols(a["L0_ffn_bw_att"]),
        "dst_pieces": pieces, "headW": np.ascontiguousarray(a["L1_gnn_W"].transpose(1, 0, 2).reshape(D, D)),
        "headWT": np.ascontiguousarray(a["L1_gnn_W"].transpose(2, 0, 1)),
        "headA": np.ascontiguousarray(a["L1_gnn_a"].reshape(H8, 2, D // H8).transpose(2, 1, 0)),
        "ew1": halves(a["L1_ffn_expert_w1"]), "ew2": halves(a["L1_ffn_expert_w2"]),
        "ew3": halves(a["L1_ffn_expert_w3"]), "eb1": cols2(a["L1_ffn_expert_b1"]), "eb2": cols2(a["L1_ffn_expert_b2"]),
        "eb3": np.ascontiguousarray(a["L1_ffn_expert_b3"][None]), "rw1": a["L1_ffn_router_w1"],
        "rb1": a["L1_ffn_router_b1"].reshape(P, 1), "rw2": a["L1_ffn_router_w2"], "rb2": row(a["L1_ffn_router_b2"]),
        "b1": row(a["L0_gnn_b1"]), "b2": row(a["L0_gnn_b2"]),
    }


def kernel(**inputs):
    import numpy as np
    import concourse.bacc as bacc
    from concourse.bass_utils import run_bass_kernel_spmd

    nc = bacc.Bacc("TRN2", target_bir_lowering=False, num_devices=1)
    arrays = layout(inputs)
    io = {k: nc.dram_tensor(f"in_{k}", a.shape, mybir.dt.from_np(a.dtype), kind="ExternalInput").ap()
          for k, a in arrays.items()}
    out = nc.dram_tensor("out", (NP_, D), F32, kind="ExternalOutput").ap()
    build(nc, io, out)
    r = run_bass_kernel_spmd(nc, [{f"in_{k}": a for k, a in arrays.items()}], core_ids=[0])
    return r.results[0]["out"][0:N]
```

```python
from contextlib import ExitStack

import concourse.bass as bass
from concourse import mybir

F32 = mybir.dt.float32
I32 = mybir.dt.int32
ALU = mybir.AluOpType
ACT = mybir.ActivationFunctionType
AX = mybir.AxisListType

P = 128
N = 6250
D = 256
NB = 49
NP_ = NB * P
BG = 7
NG = NB // BG
BC = BG * P
E = 106250
TIT = 16
JT = 4
NIT = 52
NT = NIT * TIT
EP = NT * P
H8 = 8
C = 125
L = 50
BIG = 1.0e30
SETTLED = 4.0e-6
NEXP = 6
HC = BC // 2


class Mem:

    semaphores = []

    def __init__(self, nc, ctx):
        self.nc, self.ctx = nc, ctx

    def sb(self, name, shape, dt=F32):
        return self.ctx.enter_context(self.nc.sbuf_tensor(name, shape, dt))

    def ps(self, name, shape, dt=F32):
        return self.ctx.enter_context(self.nc.psum_tensor(name, shape, dt))

    def sem(self, name):
        Mem.semaphores.append(self.nc.alloc_semaphore(name=name))
        return Mem.semaphores[-1]


def renew_semaphores(nc):
    nc.clear_and_free_semaphores(Mem.semaphores)
    nc.all_engine_barrier()
    Mem.semaphores = []


def blocks_of(t):
    return t.rearrange("(g b p) c -> g p b c", b=BG, p=P)


def stage_constants(nc, cst, io):
    with ExitStack() as ctx:
        m = Mem(nc, ctx)
        ii = m.sb("c_iota_i", [P, P], I32)
        dst_f = m.sb("c_dst_f", [P, NT])
        dst_i = m.sb("c_dst_i", [P, NT], I32)
        span = m.sb("c_span", [1, NT // JT + 1])
        ps = m.ps("c_ps", [P, 3, 512])
        loaded, iota_ok, zeroed, ident_ok = m.sem("c_loaded"), m.sem("c_iota"), m.sem("c_zeroed"), m.sem("c_ident")
        v, bc = m.sem("c_v"), m.sem("c_bc")
        block = ctx.enter_context(nc.Block())
        half = NT // 2
        NJ = NT // JT
        heads = dst_f[0:1, :].rearrange("p (g k) -> p g k", k=JT)[:, :, 0:1].rearrange("p g k -> p (g k)")

        @block.sync
        def _(sp):
            sp.dma_start(dst_i[:], io["dstT"]).then_inc(loaded, 16)
            for name, view in cst["loads"]:
                sp.dma_start(cst[name][:], view).then_inc(loaded, 16)
            sp.wait_ge(loaded, 16 * (1 + len(cst["loads"])))

        @block.gpsimd
        def _(pool):
            pool.iota(ii[:], [[1, P]], base=0, channel_multiplier=0).then_inc(iota_ok, 1)
            pool.memset(cst["ident"][:], 0.0).then_inc(zeroed, 1)
            pool.wait_ge(zeroed, 1)
            pool.affine_select(out=cst["ident"][:], in_=cst["ident"][:], compare_op=ALU.not_equal, fill=1.0,
                               base=0, pattern=[[-1, P]], channel_multiplier=1).then_inc(ident_ok, 1)

        @block.vector
        def _(dve):
            dve.memset(cst["ones"][:], 1.0).then_inc(v, 1)
            dve.memset(cst["rel"][:, :, NT:NT + 2], 0.0).then_inc(v, 1)
            dve.wait_ge(iota_ok, 1)
            dve.tensor_copy(cst["iota"][:], ii[:]).then_inc(v, 1)
            dve.wait_ge(loaded, 16 * (1 + len(cst["loads"])))
            dve.tensor_copy(cst["first"][:, 0, :], dst_i[0:1, :]).then_inc(v, 1)
            dve.tensor_copy(cst["first"][:, 1, 0:NJ], dst_i[0:1, :].rearrange("p (g k) -> p g k", k=JT)[:, :, 0:1]
                            .rearrange("p g k -> p (g k)")).then_inc(v, 1)
            dve.tensor_copy(dst_f[:], dst_i[:]).then_inc(v, 1)
            dve.wait_ge(bc, 3)
            for h in range(2):
                dve.tensor_tensor(cst["rel"][:, 0, h * half:(h + 1) * half], dst_f[:, h * half:(h + 1) * half],
                                  ps[:, h, 0:half], ALU.subtract).then_inc(v, 1)
            dve.tensor_tensor(cst["rel"][:, 1, 0:NT].rearrange("p (g k) -> p g k", k=JT),
                              dst_f[:].rearrange("p (g k) -> p g k", k=JT),
                              ps[:, 2, 0:NJ].unsqueeze(2).to_broadcast([P, NJ, JT]), ALU.subtract).then_inc(v, 1)
            dve.tensor_tensor(span[:, 0:NJ - 1], heads[:, 1:NJ], heads[:, 0:NJ - 1], ALU.subtract).then_inc(v, 1)
            dve.tensor_scalar(span[:, NJ - 1:NJ], heads[:, NJ - 1:NJ], -1.0, float(NP_ - 1), ALU.mult, ALU.add
                              ).then_inc(v, 1)
            dve.wait_ge(v, 11)
            dve.tensor_reduce(span[:, NJ:NJ + 1], span[:, 0:NJ], AX.X, ALU.max).then_inc(v, 1)
            dve.wait_ge(v, 12)
            dve.tensor_scalar(cst["wide"][:, 0:1], span[:, NJ:NJ + 1], float(P), None, ALU.is_ge).then_inc(v, 1)
            dve.tensor_scalar(cst["wide"][:, 1:2], span[:, NJ:NJ + 1], float(P), None, ALU.is_lt).then_inc(v, 1)

        @block.tensor
        def _(pe):
            pe.wait_ge(v, 6)
            for h in range(2):
                pe.matmul(ps[:, h, 0:half], cst["ones"][0:1, :], dst_f[0:1, h * half:(h + 1) * half], start=True,
                          stop=True).then_inc(bc, 1)
            pe.matmul(ps[:, 2, 0:NJ], cst["ones"][0:1, :], heads, start=True, stop=True).then_inc(bc, 1)


def stage_gather_sum(nc, cst, name, table, idx, acc, parts=2, ex=None):
    G4 = 4
    LA = 2
    OH = 4
    with ExitStack() as ctx:
        m = Mem(nc, ctx)
        rows = m.sb(f"{name}_rows", [P, TIT, D])
        ids = [m.sb(f"{name}_ids{i}", [P, TIT // 2], I32) for i in range(2)]
        onehot = [m.sb(f"{name}_onehot{i}", [P, P]) for i in range(OH)]
        part = [m.ps(f"{name}_part{i}", [P, 3, 512]) for i in range(2)]
        ids_in = [m.sem(f"{name}_ids_in{i}") for i in range(2)]
        rows_in = [m.sem(f"{name}_rows_in{i}") for i in range(G4)]
        onehot_ready = m.sem(f"{name}_onehot_ready")
        summed = m.sem(f"{name}_summed")
        added = m.sem(f"{name}_added")
        issue = m.sem(f"{name}_issue")
        if ex is not None:
            spread = m.sb(f"{name}_spread", [P, 4, H8, P // H8])
            weighted, exput = m.sem(f"{name}_weighted"), m.sem(f"{name}_exput")
        block = ctx.enter_context(nc.Block())

        def narrow_or_wide(eng, program):
            for flag, joint in ((0, JT), (1, 1)):
                other_case = eng.value_load(cst["wide"][0:1, flag:flag + 1], min_val=0, max_val=1)
                with eng.If(other_case < 1):
                    program(joint)

        @block.sync
        def _(sp):
            for half in range(2):
                sp.dma_start(ids[half][:], idx[0, :, half * 8:half * 8 + 8]).then_inc(ids_in[half], 16)
            with sp.Fori(0, NIT - 1) as i:
                for half in range(2):
                    for g in (2 * half, 2 * half + 1):
                        sp.wait_ge(rows_in[g], 16 * G4 * i + 16 * G4)
                    sp.dma_start(ids[half][:], idx[bass.ds(i + 1, 1), :, half * 8:half * 8 + 8]
                                 .rearrange("a p k -> (a p) k")).then_inc(ids_in[half], 16)

        @block.gpsimd
        def _(pool):
            with pool.Fori(0, NIT) as i:
                for t in range(TIT):
                    if t % 8 == 0:
                        pool.wait_ge(ids_in[t // 8], 16 * i + 16)
                    if t % G4 == 0:
                        pool.wait_ge(summed, TIT * i + t + G4)
                        pool.sem_inc(issue, 1)
                    pool.indirect_dma_start(rows[:, t, :], None, table,
                                            bass.IndirectOffsetOnAxis(ids[t // 8][:, t % 8:t % 8 + 1], 0)
                                            ).then_inc(rows_in[t // G4], 16)

        if ex is not None:
            @block.scalar
            def _(act):
                with act.Fori(0, NIT) as i:
                    for t in range(TIT):
                        act.wait_ge(summed, TIT * i + t + TIT - 3)
                        act.sem_inc(issue, 1)
                        act.activation(spread[:, t % 4], ex[:, bass.ds(TIT * i + t, 1), :]
                                       .rearrange("p a h -> p (a h)").unsqueeze(2).to_broadcast([P, H8, P // H8]),
                                       ACT.Copy).then_inc(exput, 1)

        @block.vector
        def _(dve):
            dve.memset(acc[:, 0:parts, :], 0.0).then_inc(added, 2)

            def make_onehot(col, buf, joint):
                dve.wait_ge(summed, col + TIT - OH + 1)
                rel = cst["rel"][:, int(joint > 1), :]
                dve.tensor_scalar(onehot[buf][:], cst["iota"][:], rel[:, bass.ds(col, 1)], None,
                                  ALU.is_equal).then_inc(onehot_ready, 1)

            def weigh(i, t):
                if t % G4 == 0:
                    dve.wait_ge(rows_in[t // G4], 16 * G4 * i + 16 * G4)
                rv = rows[:, t, :].rearrange("p (h d) -> p h d", h=H8)
                ev = ex[:, bass.ds(TIT * i + t, 1), :].rearrange("p a h -> p (a h)")
                dve.tensor_tensor(rv, rv, ev.unsqueeze(2).to_broadcast([P, H8, D // H8]), ALU.mult
                                  ).then_inc(weighted, 1)

            def program(joint):
                for t in range(LA):
                    if ex is not None:
                        weigh(0, t)
                    make_onehot(t, t % OH, joint)

                def tiles(i, last):
                    for t in range(TIT):
                        if t % (4 * joint) == 0:
                            group = (TIT // joint) * i + t // joint
                            firsts = cst["first"][0:1, 0, bass.ds(group, 4)] if joint == 1 else \
                                cst["first"][0:1, 1, bass.ds(group, 4)]
                            _, first = nc.values_load_multi_w_load_instructions(
                                firsts, engines=[mybir.EngineType.DVE], min_val=0, max_val=NP_ - 1)
                        if ex is not None and not (last and t + LA >= TIT):
                            weigh(i + (t + LA) // TIT, (t + LA) % TIT)
                        make_onehot(TIT * i + t + LA, (t + LA) % OH, joint)
                        if t % joint == joint - 1:
                            g = t // joint
                            dve.wait_ge(summed, TIT * i + t + TIT + 1)
                            dve.wait_ge(added, (TIT // joint) * i + g + 2)
                            a = acc[:, 0:parts, bass.ds(first[g % 4], P)]
                            dve.tensor_tensor(a, a, part[g % 2][:, 0:parts, 0:P], ALU.add).then_inc(added, 1)

                with dve.Fori(0, NIT - 1) as i:
                    tiles(i, False)
                tiles(NIT - 1, True)

            narrow_or_wide(dve, program)

        @block.tensor
        def _(pe):
            def program(joint):
                with pe.Fori(0, NIT) as i:
                    for t in range(TIT):
                        g = t // joint
                        if ex is not None:
                            pe.wait_ge(weighted, TIT * i + t + 1)
                            pe.wait_ge(exput, TIT * i + t + 1)
                        elif t % G4 == 0:
                            pe.wait_ge(rows_in[t // G4], 16 * G4 * i + 16 * G4)
                        pe.wait_ge(onehot_ready, TIT * i + t + 1)
                        if t % joint == 0:
                            pe.wait_ge(added, (TIT // joint) * i + g + 1)
                        for k in range(parts):
                            if k < 2:
                                lhs = rows[:, t, k * P:(k + 1) * P]
                            elif ex is None:
                                lhs = cst["ones"][:]
                            else:
                                lhs = spread[:, t % 4].rearrange("p h r -> p (h r)")
                            ins = pe.matmul(part[g % 2][:, k, 0:P], lhs, onehot[t % OH][:], start=(t % joint == 0),
                                            stop=(t % joint == joint - 1))
                        ins.then_inc(summed, 1)

            pe.sem_inc(summed, TIT)
            narrow_or_wide(pe, program)


def stage_run_starts(nc, cst, acc):
    start, runs = cst["start"], cst["runs"]
    with ExitStack() as ctx:
        m = Mem(nc, ctx)
        zero, upto = m.sb("rs_zero", [1, NP_]), m.sb("rs_upto", [1, NP_])
        start_f = m.sb("rs_start_f", [P, NB])
        fill = m.sb("rs_fill", [P, NT * H8])
        ps = m.ps("rs_ps", [P, 512])
        v, made, filled, stored = m.sem("rs_v"), m.sem("rs_made"), m.sem("rs_filled"), m.sem("rs_stored")
        block = ctx.enter_context(nc.Block())

        @block.sync
        def _(sp):
            sp.wait_ge(filled, 1)
            sp.dma_start(runs.rearrange("(p t) h -> p (t h)", p=P), fill[:]).then_inc(stored, 16)
            sp.wait_ge(stored, 16)

        @block.gpsimd
        def _(pool):
            pool.memset(fill[:], -BIG).then_inc(filled, 1)

        @block.vector
        def _(dve):
            deg = acc[0:1, 2, 0:NP_]
            dve.memset(zero[:], 0.0).then_inc(v, 1)
            dve.wait_ge(v, 1)
            dve.tensor_tensor_scan(upto[:], zero[:], deg, 0.0, ALU.add, ALU.add).then_inc(v, 1)
            dve.wait_ge(v, 2)
            dve.tensor_tensor(upto[:], upto[:], deg, ALU.subtract).then_inc(v, 1)
            dve.tensor_scalar(zero[:], deg, 0.0, float(EP), ALU.is_equal, ALU.mult).then_inc(v, 1)
            dve.wait_ge(v, 4)
            dve.tensor_tensor(upto[:], upto[:], zero[:], ALU.add).then_inc(v, 1)
            dve.wait_ge(made, 1)
            dve.tensor_copy(start[:], ps[:, 0:NB]).then_inc(v, 1)

        @block.tensor
        def _(pe):
            pe.wait_ge(v, 5)
            for b in range(NB):
                ins = pe.matmul(ps[:, b:b + 1], upto[0:1, b * P:(b + 1) * P], cst["ones"][0:1, 0:1], start=True,
                                stop=True)
            ins.then_inc(made, 1)


def stage_scatter_scores(nc, cst, s_seg):
    with ExitStack() as ctx:
        m = Mem(nc, ctx)
        scores = m.sb("sc_scores", [P, NB, H8])
        loaded, scattered = m.sem("sc_loaded"), m.sem("sc_scattered")
        block = ctx.enter_context(nc.Block())

        @block.sync
        def _(sp):
            sp.dma_start(scores[:], s_seg.rearrange("(b p) h -> p b h", p=P)).then_inc(loaded, 16)

        @block.gpsimd
        def _(pool):
            pool.wait_ge(loaded, 16)
            for b in range(NB):
                pool.indirect_dma_start(cst["runs"], bass.IndirectOffsetOnAxis(cst["start"][:, b:b + 1], 0),
                                        scores[:, b, :], None, bounds_check=EP - 1, oob_is_err=False
                                        ).then_inc(scattered, 16)
            pool.wait_ge(scattered, 16 * NB)


def stage_over_degree(nc, cst, name, acc, new):
    with ExitStack() as ctx:
        v = Mem(nc, ctx).sem(f"{name}_v")
        block = ctx.enter_context(nc.Block())

        @block.vector
        def _(dve):
            if new:
                dve.tensor_scalar(acc[:, 2, :], acc[:, 2, :], 1.0, None, ALU.max).then_inc(v, 1)
                dve.wait_ge(v, 1)
                dve.reciprocal(acc[:, 2, :], acc[:, 2, :]).then_inc(v, 1)
                dve.wait_ge(v, 2)
            dve.tensor_tensor(acc[:, 0:2, :], acc[:, 0:2, :],
                              acc[:, 2:3, :].to_broadcast([P, 2, NP_ + P]), ALU.mult).then_inc(v, 1)


def stage_over_sums(nc, cst, io, acc):
    with ExitStack() as ctx:
        m = Mem(nc, ctx)
        sel = m.sb("os_sel", [P, D])
        ps = [m.ps(f"os_ps{u}", [P, 2, 512]) for u in range(2)]
        sel_in, v, made = m.sem("os_sel_in"), m.sem("os_v"), m.sem("os_made")
        block = ctx.enter_context(nc.Block())
        n = NP_ // HC

        @block.sync
        def _(sp):
            sp.dma_start(sel[:], io["head_sel"]).then_inc(sel_in, 16)
            sp.wait_ge(sel_in, 16)

        @block.tensor
        def _(pe):
            pe.wait_ge(sel_in, 16)
            pe.wait_ge(v, 2)
            for i in range(n):
                if i >= 2:
                    pe.wait_ge(v, i + 1)
                for k in range(2):
                    ins = pe.matmul(ps[i % 2][:, k, 0:HC], sel[:, k * P:(k + 1) * P], acc[:, 2, i * HC:(i + 1) * HC],
                                    start=True, stop=True)
                ins.then_inc(made, 1)

        @block.vector
        def _(dve):
            dve.tensor_scalar(acc[:, 2, :], acc[:, 2, :], 1e-16, None, ALU.add).then_inc(v, 1)
            dve.wait_ge(v, 1)
            dve.reciprocal(acc[:, 2, :], acc[:, 2, :]).then_inc(v, 1)
            for i in range(n):
                dve.wait_ge(made, i + 1)
                a = acc[:, 0:2, i * HC:(i + 1) * HC]
                dve.tensor_tensor(a, a, ps[i % 2][:, :, 0:HC], ALU.mult).then_inc(v, 1)


def batch(t, g):
    return blocks_of(t)[bass.ds(g, 1)].rearrange("a p b c -> (a p) b c")


def each_batch(eng, body):
    with eng.Fori(0, NG // 2) as r:
        for u in range(2):
            body(2 * r + u, u, r)
    body(NG - 1, (NG - 1) % 2, NG // 2)


def stage_nodes(nc, cst, name, make, steps, loads=(), norm=True, keep=None, keep_row=False, hT=None, proj=None,
                outs=(), xT=None):
    turns = proj is not None or xT is not None
    with ExitStack() as ctx:
        m = Mem(nc, ctx)
        bufs = [[m.sb(f"{name}_in{i}{u}", [P, BG, D]) for i in range(len(loads))] for u in range(2)]
        pre = [m.sb(f"{name}_pre{u}", [P, BG, D]) for u in range(2)]
        row = [m.sb(f"{name}_row{u}", [P, BG, D]) for u in range(2)] if norm else pre
        tmp = m.sb(f"{name}_tmp", [P, BG, D])
        st, mv, std = m.sb(f"{name}_st", [P, BG, 6]), m.sb(f"{name}_mv", [P, BG, 2]), m.sb(f"{name}_std", [P, BG])
        rstd, var = m.sb(f"{name}_rstd", [P, BG]), m.sb(f"{name}_var", [P, BG])
        psT = [m.ps(f"{name}_psT{i}", [P, 512]) for i in range(2)]
        width = proj.shape[2] if proj is not None else 0
        if proj is not None:
            turned = [m.sb(f"{name}_turned{i}", [P, 2, P]) for i in range(2)]
            psY = [m.ps(f"{name}_psY{i}", [P, 512]) for i in range(2)]
            y = [m.sb(f"{name}_y{u}", [P, BG, width]) for u in range(2)]
        psH = None
        if hT is not None:
            hfix = [m.sb(f"{name}_hfix{u}", [P, 2, BC]) for u in range(2)]
            psH = m.ps(f"{name}_psH", [P, 4, 512])
            hfixed = m.sem(f"{name}_hfixed")
            hturned = m.sem(f"{name}_hturned")
        loaded = [m.sem(f"{name}_loaded{u}") for u in range(2)]
        nv = steps + (5 if norm else 0)
        v = m.sem(f"{name}_v")
        kept = [m.sem(f"{name}_kept{u}") for u in range(2)]
        turn = m.sem(f"{name}_turn")
        turn_out = m.sem(f"{name}_turn_out")
        prod = m.sem(f"{name}_prod")
        prod_out = m.sem(f"{name}_prod_out")
        no = len(outs)
        stored = [m.sem(f"{name}_stored{u}") for u in range(2)]
        std_ready = m.sem(f"{name}_std_ready")
        stats_in, loading = m.sem(f"{name}_stats_in"), m.sem(f"{name}_loading")
        placing = m.sem(f"{name}_placing")
        block = ctx.enter_context(nc.Block())
        V0 = 2 * nv

        @block.sync
        def _(sp):
            for u in range(2):
                sp.sem_inc(kept[u], 16)
                sp.sem_inc(stored[u], 16)

            def body(g, u, n):
                store_keep(g, u, n)
                if proj is not None:
                    sp.wait_ge(prod_out, BG * g + BG + 1)
                    for dram, a, b in outs:
                        sp.dma_start(batch(dram, g), y[u][:, :, a:b]).then_inc(stored[u], 16)

            def store_keep(g, u, n):
                if keep is not None:
                    sp.wait_ge(v, V0 + nv * g + (nv if keep_row else steps))
                    sp.dma_start(batch(keep, g), (row if keep_row else pre)[u][:]).then_inc(kept[u], 16)

            if keep is not None or proj is not None:
                each_batch(sp, body)
            for u, count in ((0, NG - NG // 2), (1, NG // 2)):
                if keep is not None:
                    sp.wait_ge(kept[u], 16 * count + 16)
                if proj is not None:
                    sp.wait_ge(stored[u], 16 * no * count + 16)

        @block.gpsimd
        def _(pool):
            def body(g, u, n):
                pool.wait_ge(v, nv * g + nv)
                pool.sem_inc(loading, 1)
                for i, src in enumerate(loads):
                    pool.dma_start(bufs[u][i][:], batch(src, g)).then_inc(loaded[u], 16)

            if loads:
                each_batch(pool, body)

        @block.vector
        def _(dve):
            dve.sem_inc(v, V0)

            def body(g, u, n):
                at = [0]

                def link(ins):
                    at[0] += 1
                    ins.then_inc(v, 1)
                    dve.wait_ge(v, V0 + nv * g + at[0])

                if loads:
                    dve.wait_ge(loaded[u], 16 * len(loads) * n + 16 * len(loads))
                if hT is not None:
                    dve.wait_ge(hturned, g + 3)
                if turns:
                    dve.wait_ge(turn, BG * g + 1)
                if keep is not None:
                    dve.wait_ge(kept[u], 16 * n + 16)
                make(dve, link, g, bufs[u], pre[u], tmp, psH)
                if norm:
                    for b in range(BG):
                        ins = dve.bn_stats(st[:, b, :], pre[u][:, b, :])
                    link(ins)
                    dve.sem_inc(stats_in, 1)
                    for b in range(BG):
                        ins = dve.bn_aggr(mv[:, b, :], st[:, b, :])
                    link(ins)
                    link(dve.tensor_scalar(var[:], mv[:, :, 1], 1e-5, None, ALU.add))
                    dve.wait_ge(std_ready, g + 1)
                    link(dve.reciprocal(rstd[:], std[:]))
                    for b in range(BG):
                        ins = dve.tensor_scalar(row[u][:, b, :], pre[u][:, b, :], mv[:, b, 0:1], rstd[:, b:b + 1],
                                                ALU.subtract, ALU.mult)
                    link(ins)

            each_batch(dve, body)

        @block.scalar
        def _(act):
            act.sem_inc(turn_out, 1)
            act.sem_inc(prod_out, 1)

            def fix(g, u):
                act.wait_ge(hturned, g + 1)
                act.activation(hfix[u][:], hT[:, 0:2, bass.ds(g * BC, BC)], ACT.Copy).then_inc(hfixed, 1)

            if hT is not None:
                fix(0, 0)

            def body(g, u, n):
                if hT is not None and not (isinstance(g, int) and g == NG - 1):
                    fix(g + 1, 1 - u)
                if norm:
                    act.wait_ge(v, V0 + nv * g + steps + 3)
                    act.activation(std[:], var[:], ACT.Sqrt).then_inc(std_ready, 1)
                for b in range(BG + 1 if turns else 0):
                    if b < BG:
                        act.wait_ge(turn, BG * g + b + 2 * BG + 1)
                        if proj is not None:
                            act.wait_ge(prod, BG * g + (b if b >= 2 else 1))
                        if xT is not None:
                            act.sem_inc(placing, 1)
                        to = turned[b % 2][:] if xT is None else xT[:, :, bass.ds(g * BC + b * P, P)]
                        act.activation(to, psT[b % 2][:, 0:D].rearrange("p (k n) -> p k n", k=2), ACT.Copy
                                       ).then_inc(turn_out, 1)
                    if b > 0 and proj is not None:
                        act.wait_ge(prod, BG * g + b + 1)
                        if b == 1:
                            act.wait_ge(stored[u], 16 * no * n + 16)
                        act.activation(y[u][:, b - 1, :], psY[(b - 1) % 2][:, 0:width], ACT.Copy
                                       ).then_inc(prod_out, 1)

            each_batch(act, body)

        @block.tensor
        def _(pe):
            pe.sem_inc(turn, 2 * BG)
            pe.sem_inc(prod, 1)
            if hT is not None:
                pe.sem_inc(hturned, 2)

            def turn_back(g, u):
                pe.wait_ge(hfixed, g + 1)
                pe.wait_ge(v, V0 + nv * g + 1 - nv)
                for b in range(BG):
                    for k in range(2):
                        at = (b % 2) * D + k * P
                        ins = pe.transpose(psH[:, b // 2, at:at + P], hfix[u][:, k, b * P:(b + 1) * P],
                                           cst["ident"][:])
                ins.then_inc(hturned, 1)

            if hT is not None:
                turn_back(0, 0)

            def body(g, u, n):
                if hT is not None and not (isinstance(g, int) and g == NG - 1):
                    turn_back(g + 1, 1 - u)
                if turns:
                    pe.wait_ge(v, V0 + nv * g + nv)
                for b in range(BG + 1 if turns else 0):
                    if b < BG:
                        pe.wait_ge(turn_out, BG * g + (b if b >= 2 else 1))
                        for k in range(2):
                            ins = pe.transpose(psT[b % 2][:, k * P:(k + 1) * P], row[u][:, b, k * P:(k + 1) * P],
                                               cst["ident"][:])
                        ins.then_inc(turn, 1)
                    if b > 0 and proj is not None:
                        pe.wait_ge(turn_out, BG * g + b + 1)
                        pe.wait_ge(prod_out, BG * g + (b - 1 if b > 2 else 1))
                        for k in range(2):
                            ins = pe.matmul(psY[(b - 1) % 2][:, 0:width], turned[(b - 1) % 2][:, k, :],
                                            proj[:, k, :], start=(k == 0), stop=(k == 1))
                        ins.then_inc(prod, 1)

            each_batch(pe, body)


def rows2(w):
    return w.rearrange("(k p) n -> p k n", p=P)


def stage_load(nc, name, pairs):
    with ExitStack() as ctx:
        done = Mem(nc, ctx).sem(f"{name}_done")
        block = ctx.enter_context(nc.Block())

        @block.sync
        def _(sp):
            for to, view in pairs:
                sp.dma_start(to if isinstance(to, bass.AP) else to[:], view).then_inc(done, 16)
            sp.wait_ge(done, 16 * len(pairs))


def make_plain(dve, link, g, bufs, pre, tmp, ps):
    link(dve.tensor_copy(pre[:], bufs[0][:]))


def turned_back(psH):
    return psH[:].rearrange("p a (b d) -> p (a b) d", b=2)[:, 0:BG, :]


def bias_and_prelu(dve, link, psH, pre, tmp, bias, slope, skip=None):
    link(dve.tensor_tensor(pre[:], turned_back(psH), bias[:].unsqueeze(1).to_broadcast([P, BG, D]), ALU.add))
    if skip is not None:
        link(dve.tensor_tensor(pre[:], pre[:], skip[:], ALU.add))
    link(dve.tensor_scalar(tmp[:], pre[:], 0.0, slope[:, 0:1], ALU.min, ALU.mult))
    link(dve.scalar_tensor_tensor(out=pre[:], in0=pre[:], scalar=0.0, in1=tmp[:], op0=ALU.max, op1=ALU.add))


GATES = (0, 1, 3, 2)
Q4 = 4 * C


def stage_lstm_inputs(nc, cst, io, xT, xp):
    with ExitStack() as ctx:
        m = Mem(nc, ctx)
        wih = m.sb("wih", [P, 2, 4 * D])
        bih, bhh, bias = m.sb("bih", [P, 8]), m.sb("bhh", [P, 8]), m.sb("lbias", [P, 8])
        stage = [m.sb(f"xp_stage{u}", [P, 2, Q4]) for u in range(2)]
        ps = [[m.ps(f"xp_ps{u}{k}", [P, 512]) for k in range(2)] for u in range(2)]
        w_in, b_ok = m.sem("xp_w_in"), m.sem("xp_b_ok")
        made, biased = m.sem("xp_made"), m.sem("xp_biased")
        stored = [m.sem(f"xp_stored{u}") for u in range(2)]
        block = ctx.enter_context(nc.Block())

        @block.sync
        def _(sp):
            sp.dma_start(wih[:], rows2(io["WihT"])).then_inc(w_in, 16)
            sp.dma_start(bih[:], io["b_ih"]).then_inc(w_in, 16)
            sp.dma_start(bhh[:], io["b_hh"]).then_inc(w_in, 16)
            for u in range(2):
                sp.sem_inc(stored[u], 16)
            with sp.Fori(0, L // 2) as r:
                for u in range(2):
                    sp.wait_ge(biased, 4 * r + 2 * u + 6)
                    sp.dma_start(xp[bass.ds(2 * r + u, 1)].rearrange("a p q -> (a p) q"),
                                 stage[u][:].rearrange("p k q -> p (k q)")).then_inc(stored[u], 16)
            for u in range(2):
                sp.wait_ge(stored[u], 16 * (L // 2) + 16)

        @block.tensor
        def _(pe):
            pe.wait_ge(w_in, 48)
            xs = xT[:, :, 0:N].rearrange("p k (c s) -> p k s c", s=L)
            with pe.Fori(0, L // 2) as r:
                for u in range(2):
                    for k in range(2):
                        pe.wait_ge(biased, 4 * r + 2 * u + k + 1)
                        for q, gate in enumerate(GATES):
                            col = gate * D + k * P
                            for kk in range(2):
                                ins = pe.matmul(ps[u][k][:, q * C:(q + 1) * C], wih[:, kk, col:col + P],
                                                xs[:, kk, bass.ds(2 * r + u, 1), :].rearrange("p a c -> p (a c)"),
                                                start=(kk == 0), stop=(kk == 1))
                        ins.then_inc(made, 1)

        @block.vector
        def _(dve):
            dve.sem_inc(biased, 4)
            dve.wait_ge(w_in, 48)
            dve.tensor_tensor(bias[:], bih[:], bhh[:], ALU.add).then_inc(b_ok, 1)
            dve.wait_ge(b_ok, 1)
            with dve.Fori(0, L // 2) as r:
                for u in range(2):
                    for k in range(2):
                        if k == 0:
                            dve.wait_ge(stored[u], 16 * r + 16)
                        dve.wait_ge(made, 4 * r + 2 * u + k + 1)
                        dve.tensor_tensor(stage[u][:, k, :].rearrange("p (q c) -> p q c", q=4),
                                          ps[u][k][:, 0:Q4].rearrange("p (q c) -> p q c", q=4),
                                          bias[:, 4 * k:4 * k + 4].unsqueeze(2).to_broadcast([P, 4, C]),
                                          ALU.add).then_inc(biased, 1)


def stage_sweeps(nc, cst, mem, xp, name, sweeps, skip=0, unless=None):
    R0, LS = skip // 2, L - skip
    whh, h, qc, gs, nxt, start, hist = (mem[k] for k in ("whh", "h", "qc", "gs", "nxt", "start", "hist"))
    with ExitStack() as ctx:
        m = Mem(nc, ctx)
        xin = [m.sb(f"{name}_xin{u}", [P, 2, Q4]) for u in range(2)]
        pr = [m.sb(f"{name}_pr{k}", [P, 2 * C]) for k in range(2)]
        tc = [m.sb(f"{name}_tc{k}", [P, C]) for k in range(2)]
        dif = m.sb(f"{name}_dif", [P, 4, C])
        far = m.sb(f"{name}_far", [P, 4])
        ps = [[m.ps(f"{name}_ps{u}{k}", [P, 512]) for k in range(2)] for u in range(2)]
        ps_far = m.ps(f"{name}_ps_far", [1, P])
        x_in = [m.sem(f"{name}_x_in{u}") for u in range(2)]
        gates = [m.sem(f"{name}_gates{k}") for k in range(2)]
        x_used = m.sem(f"{name}_x_used")
        acted = [m.sem(f"{name}_acted{k}") for k in range(2)]
        mixed = [m.sem(f"{name}_mixed{k}") for k in range(2)]
        c_ready = [m.sem(f"{name}_c_ready{k}") for k in range(2)]
        tc_ready = [m.sem(f"{name}_tc_ready{k}") for k in range(2)]
        h_ready = [m.sem(f"{name}_h_ready{k}") for k in range(2)]
        noted = [m.sem(f"{name}_noted{k}") for k in range(2)]
        shifted = m.sem(f"{name}_shifted")
        loaded = m.sem(f"{name}_loaded")
        judged, far_turned = m.sem(f"{name}_judged"), m.sem(f"{name}_far_turned")
        block = ctx.enter_context(nc.Block())

        def only_if_needed(eng, program):
            if unless is None:
                return program()
            done = eng.value_load(unless[0:1, 0:1], min_val=0, max_val=1)
            with eng.If(done < 1):
                program()

        @block.sync
        def _(sp):
            def program():
                with sp.Fori(0, sweeps) as w:
                    with sp.Fori(0, LS // 2) as r:
                        for u in range(2):
                            sp.wait_ge(x_used, w * LS + 2 * r + u + 1)
                            sp.dma_start(xin[u][:].rearrange("p k q -> p (k q)"),
                                         xp[bass.ds(2 * (r + R0) + u, 1)].rearrange("a p q -> (a p) q")
                                         ).then_inc(x_in[u], 16)
            only_if_needed(sp, program)

        @block.tensor
        def _(pe):
            def program():
                pe.sem_inc(x_used, 2)
                with pe.Fori(0, sweeps) as w:
                    with pe.Fori(0, LS // 2) as r:
                        for u in range(2):
                            pe.wait_ge(x_in[u], 16 * (w * (LS // 2) + r) + 16)
                            for half in range(2):
                                ins = pe.matmul(ps[u][half][:, 0:Q4], cst["ident"][:], xin[u][:, half, :],
                                                start=True, stop=False, skip_group_check=True)
                            ins.then_inc(x_used, 1)
                            pe.wait_ge(h_ready[0], w * (LS + 1) + 2 * r + u + 1)
                            for half in range(2):
                                for q, gate in enumerate(GATES):
                                    col = gate * D + half * P
                                    pe.matmul(ps[u][half][:, q * C:(q + 1) * C], whh[:, 0, col:col + P], h[:, 0, :],
                                              start=False, stop=False, skip_group_check=True)
                            pe.wait_ge(h_ready[1], w * (LS + 1) + 2 * r + u + 1)
                            for half in range(2):
                                for q, gate in enumerate(GATES):
                                    col = gate * D + half * P
                                    ins = pe.matmul(ps[u][half][:, q * C:(q + 1) * C], whh[:, 1, col:col + P],
                                                    h[:, 1, :], start=False, stop=(q == 3), skip_group_check=True)
                                ins.then_inc(gates[half], 1)
                pe.wait_ge(judged, 2)
                pe.transpose(ps_far[0:1, :], far[:, 0:1], cst["ident"][:]).then_inc(far_turned, 1)
            only_if_needed(pe, program)

        @block.scalar
        def _(act):
            def program():
                with act.Fori(0, sweeps) as w:
                    with act.Fori(0, LS // 2) as r:
                        for u in range(2):
                            s = w * LS + 2 * r + u
                            for k in range(2):
                                act.wait_ge(gates[k], s + 1)
                                act.activation(gs[:, k, 0:3 * C], ps[u][k][:, 0:3 * C], ACT.Sigmoid
                                               ).then_inc(acted[k], 1)
                                act.activation(qc[:, k, 0:C], ps[u][k][:, 3 * C:Q4], ACT.Tanh).then_inc(acted[k], 1)
                            for k in range(2):
                                act.wait_ge(c_ready[k], s + 1)
                                act.activation(tc[k][:], qc[:, k, C:2 * C], ACT.Tanh).then_inc(tc_ready[k], 1)
            only_if_needed(act, program)

        @block.gpsimd
        def _(pool):
            def program():
                hs = hist[:, :, 0:N].rearrange("p k (c s) -> p k s c", s=L)
                for k in range(2):
                    pool.sem_inc(noted[k], 1)
                with pool.Fori(0, sweeps) as w:
                    with pool.Fori(0, LS) as s:
                        for k in range(2):
                            pool.wait_ge(h_ready[k], w * (LS + 1) + s + 2)
                            pool.tensor_copy(hs[:, k, bass.ds(s + skip, 1), :].rearrange("p a c -> p (a c)"), h[:, k, :]
                                             ).then_inc(noted[k], 1)
            only_if_needed(pool, program)

        @block.vector
        def _(dve):
            def program():
                with dve.Fori(0, sweeps) as w:
                    dve.tensor_copy(start[:], nxt[:]).then_inc(loaded, 1)
                    dve.tensor_copy(qc[:, :, C:2 * C], nxt[:, 2:4, :]).then_inc(loaded, 1)
                    for k in range(2):
                        dve.wait_ge(noted[k], w * LS + 1)
                        dve.tensor_copy(h[:, k, :], nxt[:, k, :]).then_inc(h_ready[k], 1)
                    with dve.Fori(0, LS // 2) as r:
                        for u in range(2):
                            s = w * LS + 2 * r + u
                            for k in range(2):
                                dve.wait_ge(acted[k], 2 * s + 2)
                                dve.tensor_tensor(pr[k][:], gs[:, k, 0:2 * C], qc[:, k, :], ALU.mult
                                                  ).then_inc(mixed[k], 1)
                                dve.wait_ge(mixed[k], s + 1)
                                dve.tensor_tensor(qc[:, k, C:2 * C], pr[k][:, 0:C], pr[k][:, C:2 * C], ALU.add
                                                  ).then_inc(c_ready[k], 1)
                            for k in range(2):
                                dve.wait_ge(tc_ready[k], s + 1)
                                dve.wait_ge(noted[k], s + 1)
                                dve.tensor_tensor(h[:, k, :], gs[:, k, 2 * C:3 * C], tc[k][:], ALU.mult
                                                  ).then_inc(h_ready[k], 1)
                    for k in range(2):
                        dve.wait_ge(h_ready[k], w * (LS + 1) + LS + 1)
                        dve.wait_ge(c_ready[k], w * LS + LS)
                    for k in range(2):
                        dve.tensor_copy(nxt[:, k, 1:C], h[:, k, 0:C - 1]).then_inc(shifted, 1)
                        dve.tensor_copy(nxt[:, 2 + k, 1:C], qc[:, k, C:2 * C - 1]).then_inc(shifted, 1)
                    dve.wait_ge(shifted, 4 * w + 4)
                dve.tensor_tensor(dif[:], nxt[:], start[:], ALU.subtract).then_inc(loaded, 1)
                dve.wait_ge(loaded, 2 * sweeps + 1)
                dve.tensor_tensor(dif[:], dif[:], dif[:], ALU.mult).then_inc(judged, 1)
                dve.wait_ge(judged, 1)
                dve.tensor_reduce(far[:, 0:1], dif[:].rearrange("p k c -> p (k c)"), AX.X, ALU.max).then_inc(judged, 1)
                dve.wait_ge(far_turned, 1)
                dve.tensor_reduce(far[0:1, 1:2], ps_far[0:1, :], AX.X, ALU.max).then_inc(judged, 1)
                dve.wait_ge(judged, 3)
                dve.tensor_scalar(mem["settled"][:], far[0:1, 1:2], SETTLED * SETTLED, None, ALU.is_le
                                  ).then_inc(judged, 1)
            only_if_needed(dve, program)


def stage_gated_sums(nc, cst, io, hist):
    TC = 500
    NC_ = 13
    with ExitStack() as ctx:
        m = Mem(nc, ctx)
        wl, wlb = m.sb("wl", [P, 2, 2]), m.sb("wlb", [P, 2, 2, P])
        bl = m.sb("bl", [P, 2])
        fw, bw, nbw = m.sb("fw", [P, 2]), m.sb("bw", [P, 2]), m.sb("nbw", [P, 2])
        w, inc = m.sb("gw", [P, 2, NP_]), m.sb("inc", [P, 2, NP_])
        one = m.sb("one_row", [P, TC])
        l1 = m.sb("l1", [P, TC])
        gate = m.sb("gate", [P, TC])
        ps = [[m.ps(f"gs_ps{u}{l}", [P, 512]) for l in range(2)] for u in range(2)]
        w_in, v, logits = m.sem("gs_w_in"), m.sem("gs_v"), m.sem("gs_logits")
        spread = m.sem("gs_spread")
        block = ctx.enter_context(nc.Block())
        cols = [(i * TC, min(N, (i + 1) * TC)) for i in range(NC_)]

        @block.sync
        def _(sp):
            for to, frm in ((wl, io["W_lin"]), (bl, io["b_lin"].to_broadcast([P, 2])), (fw, io["fw"]), (bw, io["bw"])):
                sp.dma_start(to[:], frm).then_inc(w_in, 16)

        @block.tensor
        def _(pe):
            pe.wait_ge(spread, 5)
            for i, (a, b) in enumerate(cols):
                if i >= 2:
                    pe.wait_ge(v, 5 * (i - 2) + 2)
                for l in range(2):
                    for k in range(2):
                        ins = pe.matmul(ps[i % 2][l][:, 0:b - a], wlb[:, k, l, :], hist[:, k, a:b], start=(k == 0),
                                        stop=(k == 1))
                ins.then_inc(logits, 1)

        @block.vector
        def _(dve):
            dve.wait_ge(w_in, 64)
            for k in range(2):
                for l in range(2):
                    dve.tensor_copy(wlb[:, k, l, :], wl[:, k, l:l + 1].to_broadcast([P, P])).then_inc(spread, 1)
            dve.tensor_scalar(nbw[:], bw[:], -1.0, None, ALU.mult).then_inc(spread, 1)
            dve.memset(one[:], 1.0).then_inc(spread, 1)
            dve.wait_ge(spread, 6)
            for i, (a, b) in enumerate(cols):
                n = b - a
                dve.wait_ge(logits, i + 1)
                dve.tensor_scalar(l1[:, 0:n], ps[i % 2][1][:, 0:n], bl[:, 1:2], None, ALU.add).then_inc(v, 1)
                dve.wait_ge(v, 5 * i + 1)
                dve.scalar_tensor_tensor(out=gate[:, 0:n], in0=ps[i % 2][0][:, 0:n], scalar=bl[:, 0:1],
                                         in1=l1[:, 0:n], op0=ALU.add, op1=ALU.is_lt).then_inc(v, 1)
                dve.wait_ge(v, 5 * i + 2)
                dve.tensor_tensor(w[:, :, a:b], hist[:, :, a:b], gate[:, 0:n].unsqueeze(1).to_broadcast([P, 2, n]),
                                  ALU.mult).then_inc(v, 1)
                dve.wait_ge(v, 5 * i + 3)
                for k in range(2):
                    first = 0.0 if i == 0 else inc[:, k, a - 1:a]
                    dve.tensor_tensor_scan(inc[:, k, a:b], one[:, 0:n], w[:, k, a:b], first, ALU.mult, ALU.add
                                           ).then_inc(v, 1)
                dve.wait_ge(v, 5 * i + 5)
            at = [5 * NC_]

            def link(ins):
                at[0] += 1
                ins.then_inc(v, 1)
                dve.wait_ge(v, at[0])

            link(dve.tensor_tensor(w[:, :, 0:N], inc[:, :, 0:N], w[:, :, 0:N], ALU.subtract))
            for k in range(2):
                total = one[:, k:k + 1]
                link(dve.tensor_copy(total, inc[:, k, N - 1:N]))
                link(dve.tensor_scalar(inc[:, k, 0:N], inc[:, k, 0:N], total, nbw[:, k:k + 1], ALU.subtract, ALU.mult))
                link(dve.scalar_tensor_tensor(out=w[:, k, 0:N], in0=w[:, k, 0:N], scalar=fw[:, k:k + 1],
                                              in1=inc[:, k, 0:N], op0=ALU.mult, op1=ALU.add))
                link(dve.scalar_tensor_tensor(out=hist[:, k, 0:N], in0=hist[:, k, 0:N], scalar=2.0, in1=w[:, k, 0:N],
                                              op0=ALU.mult, op1=ALU.add))


def stage_clear(nc, name, views):
    with ExitStack() as ctx:
        done = Mem(nc, ctx).sem(f"{name}_done")
        block = ctx.enter_context(nc.Block())

        @block.vector
        def _(dve):
            for view in views:
                dve.memset(view, 0.0).then_inc(done, 1)
            dve.wait_ge(done, len(views))


CE = NIT * P


def stage_head_scores(nc, cst, io, proj):
    with ExitStack() as ctx:
        m = Mem(nc, ctx)
        wt, at = m.sb("hs_wt", [D // H8, H8, D]), m.sb("hs_at", [D // H8, 2, H8])
        ps = m.ps("hs_ps", [P, 2, 2 * H8])
        loaded, made, copied = m.sem("hs_loaded"), m.sem("hs_made"), m.sem("hs_copied")
        block = ctx.enter_context(nc.Block())

        @block.sync
        def _(sp):
            sp.dma_start(wt[:], io["headWT"]).then_inc(loaded, 16)
            sp.dma_start(at[:], io["headA"]).then_inc(loaded, 16)
            sp.dma_start(proj[:, :, 0:D], rows2(io["headW"])).then_inc(loaded, 16)
            sp.wait_ge(loaded, 48)

        @block.tensor
        def _(pe):
            pe.wait_ge(loaded, 48)
            for k in range(2):
                for s in range(2):
                    for hd in range(H8):
                        ins = pe.matmul(ps[:, k, s * H8 + hd:s * H8 + hd + 1], wt[:, hd, k * P:(k + 1) * P],
                                        at[:, s, hd:hd + 1], start=True, stop=True)
            ins.then_inc(made, 1)

        @block.vector
        def _(dve):
            dve.wait_ge(made, 1)
            dve.tensor_copy(proj[:, :, D:D + 2 * H8], ps[:]).then_inc(copied, 1)
            dve.wait_ge(copied, 1)


def stage_edge_weights(nc, cst, io, s_oth, ex):
    with ExitStack() as ctx:
        m = Mem(nc, ctx)
        ga = [m.sb(f"ew_ga{u}", [P, TIT, H8]) for u in range(2)]
        gb = [m.sb(f"ew_gb{u}", [P, TIT, H8]) for u in range(2)]
        ib = [m.sb(f"ew_ib{u}", [P, TIT], I32) for u in range(2)]
        zz, own = m.sb("ew_z", [P, CE]), m.sb("ew_own", [P, CE])
        node = m.sb("ew_node", [P, CE + 2], I32)
        cut = m.sb("ew_cut", [P, CE])
        top = m.sb("ew_top", [P, CE])
        ends = m.sb("ew_ends", [P, 2])
        line = m.sb("ew_line", [1, 2, P])
        run, carry = m.sb("ew_run", [1, P]), m.sb("ew_carry", [1, P])
        init = m.sb("ew_init", [P, 3])
        slot = [m.sb(f"ew_slot{u}", [P, P]) for u in range(2)]
        ps = [m.ps(f"ew_ps{u}", [P, 512]) for u in range(2)]
        ps_line = [m.ps(f"ew_psl{r}", [1, 2, P]) for r in range(3)]
        ps_init = m.ps("ew_psi", [P, 512])
        ids_in = [m.sem(f"ew_ids_in{u}") for u in range(2)]
        rows_in = [m.sem(f"ew_rows_in{u}") for u in range(2)]
        own_in = [m.sem(f"ew_own_in{u}") for u in range(2)]
        summed, copied = m.sem("ew_summed"), m.sem("ew_copied")
        node_in, v, turned = m.sem("ew_node_in"), m.sem("ew_v"), m.sem("ew_turned")
        exped, back_out, issue = m.sem("ew_exped"), m.sem("ew_back_out"), m.sem("ew_issue")
        eturned = m.sem("ew_eturned")
        block = ctx.enter_context(nc.Block())
        PER = 16 * TIT

        @block.sync
        def _(sp):
            for j in range(TIT):
                sp.dma_start(node[j * H8:(j + 1) * H8, :], io["dst_pieces"][j:j + 1, :].to_broadcast([H8, CE + 2])
                             ).then_inc(node_in, 16)
            runs = cst["runs"].rearrange("(j i p) h -> i p j h", j=TIT, p=P)
            for u in range(2):
                sp.dma_start(ib[u][:], io["src_cols"][u]).then_inc(ids_in[u], 16)
                sp.dma_start(ga[u][:], runs[u]).then_inc(own_in[u], 16)
            with sp.Fori(0, NIT // 2 - 1) as r:
                for u in range(2):
                    sp.wait_ge(rows_in[u], PER * r + PER)
                    sp.dma_start(ib[u][:], io["src_cols"][bass.ds(2 * r + 2 + u, 1)].rearrange("a p k -> (a p) k")
                                 ).then_inc(ids_in[u], 16)
                    sp.wait_ge(summed, 2 * r + u + 3)
                    sp.dma_start(ga[u][:], runs[bass.ds(2 * r + 2 + u, 1)].rearrange("a p j h -> (a p) j h")
                                 ).then_inc(own_in[u], 16)
            sp.wait_ge(node_in, 16 * TIT)

        @block.gpsimd
        def _(pool):
            with pool.Fori(0, NIT // 2) as r:
                for u in range(2):
                    pool.wait_ge(ids_in[u], 16 * r + 16)
                    pool.wait_ge(summed, 2 * r + u + 1)
                    pool.sem_inc(issue, 1)
                    for j in range(TIT):
                        pool.indirect_dma_start(gb[u][:, j, :], None, s_oth,
                                                bass.IndirectOffsetOnAxis(ib[u][:, j:j + 1], 0)
                                                ).then_inc(rows_in[u], 16)

        @block.tensor
        def _(pe):
            pe.sem_inc(summed, 2)
            with pe.Fori(0, NIT // 2) as r:
                for u in range(2):
                    pe.wait_ge(rows_in[u], PER * r + PER)
                    pe.wait_ge(copied, 2 * r + u + 1)
                    pe.wait_ge(own_in[u], 16 * r + 16)
                    for c, g in enumerate((ga[u], gb[u])):
                        ins = pe.transpose(ps[u][:, c * P:(c + 1) * P], g[:].rearrange("p j h -> p (j h)"),
                                           cst["ident"][:])
                    ins.then_inc(summed, 1)
            for rd, base in ((0, OWN1), (1, FORTH1), (2, BACK1)):
                pe.wait_ge(v, base)
                for c in range(2):
                    ins = pe.transpose(ps_line[rd][0:1, c, :], ends[:, c:c + 1], cst["ident"][:])
                ins.then_inc(turned, 1)
                pe.wait_ge(v, base + CARRIED)
                pe.matmul(ps_init[:, rd:rd + 1], carry[0:1, :], cst["ones"][0:1, 0:1], start=True, stop=True
                          ).then_inc(turned, 1)
            with pe.Fori(0, NIT // 2) as r:
                for u in range(2):
                    pe.wait_ge(exped, 2 * r + u + 3)
                    pe.wait_ge(back_out, 2 * r + u + 1)
                    pe.transpose(ps[u][:, 0:P], slot[u][:], cst["ident"][:]).then_inc(eturned, 1)

        @block.scalar
        def _(act):
            act.sem_inc(copied, 2)
            act.sem_inc(exped, 2)
            with act.Fori(0, NIT // 2) as r:
                for u in range(2):
                    act.wait_ge(summed, 2 * r + u + 3)
                    act.sem_inc(issue, 1)
                    act.activation(own[:, bass.ds((2 * r + u) * P, P)], ps[u][:, 0:P], ACT.Copy)
                    act.activation(zz[:, bass.ds((2 * r + u) * P, P)], ps[u][:, P:2 * P], ACT.Copy
                                   ).then_inc(copied, 1)
            act.wait_ge(v, LAST)
            with act.Fori(0, NIT // 2) as r:
                for u in range(2):
                    act.wait_ge(back_out, 2 * r + u + 1)
                    act.activation(slot[u][:], zz[:, bass.ds((2 * r + u) * P, P)], ACT.Exp).then_inc(exped, 1)

        @block.vector
        def _(dve):
            at = [0]

            def link(ins):
                at[0] += 1
                ins.then_inc(v, 1)
                dve.wait_ge(v, at[0])

            def carry_over(rd):
                dve.wait_ge(turned, 2 * rd + 1)
                link(dve.tensor_copy(line[:].rearrange("a c (h j) -> a c h j", h=H8),
                                     ps_line[rd][:].rearrange("a c (j h) -> a c h j", h=H8)))
                first = line[0:1, 1, :].rearrange("a (h j) -> a h j", j=TIT)
                edge = slice(0, 1) if rd < 2 else slice(TIT - 1, TIT)
                link(dve.memset(first[:, :, edge], -BIG))
                a, b = line[0:1, 1, :], line[0:1, 0, :]
                o = run[0:1, :]
                if rd == 2:
                    a, b, o = a[:, ::-1], b[:, ::-1], o[:, ::-1]
                link(dve.tensor_tensor_scan(o, a, b, -BIG, ALU.add, ALU.max))
                link(dve.memset(carry[:], -BIG))
                cv = carry[:].rearrange("a (j h) -> a h j", j=TIT)
                rv = run[:].rearrange("a (h j) -> a h j", j=TIT)
                if rd < 2:
                    link(dve.tensor_copy(cv[:, :, 1:TIT], rv[:, :, 0:TIT - 1]))
                else:
                    link(dve.tensor_copy(cv[:, :, 0:TIT - 1], rv[:, :, 1:TIT]))
                dve.wait_ge(turned, 2 * rd + 2)
                link(dve.tensor_copy(init[:, rd:rd + 1], ps_init[:, rd:rd + 1]))

            dve.sem_inc(back_out, 2)
            dve.wait_ge(node_in, 16 * TIT)
            dve.wait_ge(copied, NIT + 2)
            link(dve.tensor_tensor(cut[:], node[:, 1:CE + 1], node[:, 0:CE], ALU.not_equal))
            link(dve.tensor_scalar(cut[:], cut[:], -BIG, None, ALU.mult))
            link(dve.tensor_tensor_scan(top[:], cut[:], own[:], -BIG, ALU.add, ALU.max))
            link(dve.tensor_copy(ends[:, 0:1], top[:, CE - 1:CE]))
            link(dve.tensor_reduce(ends[:, 1:2], cut[:], AX.X, ALU.min))
            assert at[0] == OWN1
            carry_over(0)
            link(dve.tensor_tensor_scan(top[:], cut[:], own[:], init[:, 0:1], ALU.add, ALU.max))
            link(dve.tensor_tensor(zz[:], zz[:], top[:], ALU.add))
            link(dve.scalar_tensor_tensor(out=zz[:], in0=zz[:], scalar=0.2, in1=zz[:], op0=ALU.mult, op1=ALU.max))
            link(dve.tensor_tensor_scan(top[:], cut[:], zz[:], -BIG, ALU.add, ALU.max))
            link(dve.tensor_copy(ends[:, 0:1], top[:, CE - 1:CE]))
            assert at[0] == FORTH1, at[0]
            carry_over(1)
            link(dve.tensor_tensor_scan(top[:], cut[:], zz[:], init[:, 1:2], ALU.add, ALU.max))
            link(dve.tensor_tensor(cut[:], node[:, 1:CE + 1], node[:, 2:CE + 2], ALU.not_equal))
            link(dve.tensor_scalar(cut[:], cut[:], -BIG, None, ALU.mult))
            link(dve.tensor_tensor_scan(top[:, ::-1], cut[:, ::-1], top[:, ::-1], -BIG, ALU.add, ALU.max))
            link(dve.tensor_copy(ends[:, 0:1], top[:, 0:1]))
            link(dve.tensor_reduce(ends[:, 1:2], cut[:], AX.X, ALU.min))
            assert at[0] == BACK1, at[0]
            carry_over(2)
            link(dve.tensor_tensor_scan(top[:, ::-1], cut[:, ::-1], top[:, ::-1], init[:, 2:3], ALU.add, ALU.max))
            link(dve.tensor_tensor(zz[:], zz[:], top[:], ALU.subtract))
            assert at[0] == LAST, at[0]
            ev = ex[:].rearrange("p (j i) h -> p i j h", i=NIT)
            with dve.Fori(0, NIT // 2) as r:
                for u in range(2):
                    dve.wait_ge(eturned, 2 * r + u + 1)
                    dve.tensor_copy(ev[:, bass.ds(2 * r + u, 1), :, :].rearrange("p a j h -> p (a j) h"),
                                    ps[u][:, 0:P].rearrange("p (j h) -> p j h", h=H8)).then_inc(back_out, 1)


CARRIED = 5
OWN1 = 5
FORTH1 = OWN1 + 6 + 5
BACK1 = FORTH1 + 6 + 6
LAST = BACK1 + 6 + 2


def stage_experts(nc, cst, io, xT, x3, out):
    with ExitStack() as ctx:
        m = Mem(nc, ctx)
        w1, w2, w3 = (m.sb(f"ew{i}", [P, NEXP, 2, D]) for i in (1, 2, 3))
        b1, b2 = m.sb("eb1", [P, NEXP, 2]), m.sb("eb2", [P, NEXP, 2])
        b3 = m.sb("eb3", [1, NEXP, D])
        rw1, rb1, rw2, rb2 = m.sb("rw1", [P, 2, P]), m.sb("rb1", [P, 1]), m.sb("rw2", [P, NEXP]), m.sb("rb2", [1, NEXP])
        x = m.sb("ex_x", [P, 2, BC])
        rh = m.sb("ex_rh", [P, BC])
        h1, h2 = m.sb("ex_h1", [P, 2, BC]), m.sb("ex_h2", [P, 2, BC])
        tot = m.sb("ex_tot", [P, BG, D])
        lg, pr, oh1, oh2, key, wt = (m.sb(f"ex_{n}", [P, BG, NEXP]) for n in ("lg", "pr", "oh1", "oh2", "key", "wt"))
        s = [m.sb(f"ex_s{i}", [P, BG, 1]) for i in range(8)]
        psh = m.ps("ex_psh", [P, 4, 512])
        psy = [m.ps(f"ex_psy{i}", [P, 512]) for i in range(3)]
        psl = m.ps("ex_psl", [P, 512])
        w_in, x_in, stored = m.sem("ex_w_in"), m.sem("ex_x_in"), m.sem("ex_stored")
        fixed = m.sem("ex_fixed")
        up = m.sem("ex_up")
        act_up = m.sem("ex_act_up")
        lgs, v, ydone, yadd = m.sem("ex_lgs"), m.sem("ex_v"), m.sem("ex_ydone"), m.sem("ex_yadd")
        expd, mixed = m.sem("ex_expd"), m.sem("ex_mixed")
        block = ctx.enter_context(nc.Block())
        UP = 2 + NEXP * 8
        NV = 24
        NY = NEXP * BG

        @block.sync
        def _(sp):
            sp.sem_inc(stored, 16)
            for to, frm in ((w1[:], io["ew1"]), (w2[:], io["ew2"]), (w3[:], io["ew3"]), (b1[:], io["eb1"]),
                            (b2[:], io["eb2"]), (b3[:], io["eb3"]), (rw1[:], rows2(io["rw1"])), (rb1[:], io["rb1"]),
                            (rw2[:], io["rw2"]), (rb2[:], io["rb2"])):
                sp.dma_start(to, frm).then_inc(w_in, 16)
            with sp.Fori(0, NG) as g:
                sp.wait_ge(stored, 16 * g + 16)
                sp.dma_start(tot[:], batch(x3, g)).then_inc(x_in, 16)
                sp.wait_ge(yadd, NY * g + NY + 3)
                sp.dma_start(batch(out, g), tot[:]).then_inc(stored, 16)
            sp.wait_ge(stored, 16 * NG + 16)

        @block.tensor
        def _(pe):
            pe.wait_ge(w_in, 160)
            pe.sem_inc(up, 1)
            with pe.Fori(0, NG) as g:
                n = [0]

                def pair(lhs, src, need):
                    for c in range(2):
                        bank = n[0] % 4
                        pe.wait_ge(act_up, UP * g + max(n[0] - 2, 1))
                        for k in range(2):
                            ins = pe.matmul(psh[:, bank, 0:HC], lhs[k], src[:, k, c * HC:(c + 1) * HC],
                                            start=(k == 0), stop=(k == 1))
                        ins.then_inc(up, 1)
                        n[0] += 1

                pe.wait_ge(fixed, g + 1)
                pair([rw1[:, k, :] for k in range(2)], x, None)
                pe.wait_ge(act_up, UP * g + 2 + 1)
                pe.wait_ge(v, NV * g + 1)
                for b in range(BG):
                    pe.matmul(psl[:, b * NEXP:(b + 1) * NEXP], rh[:, b * P:(b + 1) * P], rw2[:], start=True,
                              stop=False)
                    ins = pe.matmul(psl[:, b * NEXP:(b + 1) * NEXP], cst["ones"][0:1, :], rb2[:], start=False, stop=True)
                ins.then_inc(lgs, 1)
                for e in range(NEXP):
                    for mm in range(2):
                        pair([w1[:, e, k, mm * P:(mm + 1) * P] for k in range(2)], x, None)
                    pe.wait_ge(act_up, UP * g + n[0] + 1)
                    for mm in range(2):
                        pair([w2[:, e, k, mm * P:(mm + 1) * P] for k in range(2)], h1, None)
                    pe.wait_ge(act_up, UP * g + n[0] + 1)
                    for b in range(BG):
                        y = e * BG + b
                        pe.wait_ge(yadd, NY * g + y + 1)
                        for k in range(2):
                            pe.matmul(psy[y % 3][:, 0:D], h2[:, k, b * P:(b + 1) * P], w3[:, e, k, :],
                                      start=(k == 0), stop=False)
                        pe.matmul(psy[y % 3][:, 0:D], cst["ones"][0:1, :], b3[0:1, e, :], start=False, stop=True
                                  ).then_inc(ydone, 1)

        @block.scalar
        def _(act):
            act.wait_ge(w_in, 160)
            act.sem_inc(act_up, 1)
            with act.Fori(0, NG) as g:
                n = [0]

                def relu(to, bias, free=None):
                    for c in range(2):
                        act.wait_ge(up, UP * g + n[0] + 2)
                        if free is not None:
                            act.wait_ge(*free)
                        act.activation(to[:, c * HC:(c + 1) * HC], psh[:, n[0] % 4, 0:HC], ACT.Relu, bias=bias
                                       ).then_inc(act_up, 1)
                        n[0] += 1

                act.wait_ge(up, UP * g + 1)
                act.activation(x[:], xT[:, :, bass.ds(g * BC, BC)], ACT.Copy).then_inc(fixed, 1)
                relu(rh[:], rb1[:, 0:1])
                for e in range(NEXP):
                    for mm in range(2):
                        relu(h1[:, mm, :], b1[:, e, mm:mm + 1])
                    if e == 0:
                        act.wait_ge(v, NV * g + 4)
                        act.activation(pr[:], lg[:], ACT.Exp).then_inc(expd, 1)
                        act.wait_ge(v, NV * g + 17)
                        act.activation(s[5][:], s[4][:], ACT.Exp).then_inc(expd, 1)
                    for mm in range(2):
                        relu(h2[:, mm, :], b2[:, e, mm:mm + 1],
                             free=(ydone, NY * g + BG * e) if e else (yadd, NY * g + 1))

        @block.vector
        def _(dve):
            dve.wait_ge(w_in, 160)
            dve.sem_inc(yadd, 3)
            dve.sem_inc(v, 1)
            with dve.Fori(0, NG) as g:
                at = [0]

                def link(ins):
                    at[0] += 1
                    ins.then_inc(v, 1)
                    dve.wait_ge(v, NV * g + at[0] + 1)

                def wide(t):
                    return t[:].to_broadcast([P, BG, NEXP])

                iota = cst["iota"][:, 0:NEXP].unsqueeze(1).to_broadcast([P, BG, NEXP])

                def pick(first, val, oh):
                    link(dve.tensor_tensor(key[:], pr[:], wide(val), ALU.not_equal))
                    link(dve.tensor_scalar(key[:], key[:], 64.0, None, ALU.mult))
                    link(dve.tensor_tensor(key[:], key[:], iota, ALU.add))
                    link(dve.tensor_reduce(first[:], key[:], AX.X, ALU.min))
                    link(dve.tensor_tensor(oh[:], iota, wide(first), ALU.is_equal))

                dve.wait_ge(lgs, g + 1)
                lv = psl[:, 0:BG * NEXP].rearrange("p (b e) -> p b e", b=BG)
                link(dve.tensor_copy(lg[:], lv))
                link(dve.tensor_reduce(s[0][:], lg[:], AX.X, ALU.max))
                link(dve.tensor_tensor(lg[:], lg[:], wide(s[0]), ALU.subtract))
                dve.wait_ge(expd, 2 * g + 1)
                link(dve.tensor_reduce(s[1][:], pr[:], AX.X, ALU.add))
                link(dve.reciprocal(s[1][:], s[1][:]))
                link(dve.tensor_tensor(pr[:], pr[:], wide(s[1]), ALU.mult))
                link(dve.tensor_reduce(s[2][:], pr[:], AX.X, ALU.max))
                pick(s[3], s[2], oh1)
                link(dve.scalar_tensor_tensor(out=pr[:], in0=oh1[:], scalar=-4.0, in1=pr[:], op0=ALU.mult,
                                              op1=ALU.add))
                link(dve.tensor_reduce(s[6][:], pr[:], AX.X, ALU.max))
                link(dve.tensor_tensor(s[4][:], s[6][:], s[2][:], ALU.subtract))
                link(dve.tensor_copy(s[7][:], s[2][:]))
                dve.wait_ge(expd, 2 * g + 2)
                pick(s[3], s[6], oh2)
                link(dve.tensor_scalar(s[0][:], s[5][:], 1.0, None, ALU.add))
                link(dve.reciprocal(s[0][:], s[0][:]))
                link(dve.tensor_tensor(oh2[:], oh2[:], wide(s[5]), ALU.mult))
                assert at[0] == NV
                dve.tensor_tensor(oh1[:], oh1[:], oh2[:], ALU.add).then_inc(mixed, 1)
                dve.wait_ge(mixed, 2 * g + 1)
                dve.tensor_tensor(wt[:], oh1[:], wide(s[0]), ALU.mult).then_inc(mixed, 1)
                dve.wait_ge(mixed, 2 * g + 2)
                dve.wait_ge(x_in, 16 * g + 16)
                for e in range(NEXP):
                    for b in range(BG):
                        y = e * BG + b
                        dve.wait_ge(ydone, NY * g + y + 1)
                        if e:
                            dve.wait_ge(yadd, NY * g + y - BG + 1 + 3)
                        dve.scalar_tensor_tensor(out=tot[:, b, :], in0=psy[y % 3][:, 0:D], scalar=wt[:, b, e:e + 1],
                                                 in1=tot[:, b, :], op0=ALU.mult, op1=ALU.add).then_inc(yadd, 1)


def make_edge_rows(dve, link, g, bufs, pre, tmp, psH):
    link(dve.tensor_copy(pre[:], turned_back(psH)))


def build(nc, io, out):
    def dram(name, shape, dt=F32):
        return nc.dram_tensor(name, shape, dt, kind="Internal").ap()

    Mem.semaphores = []
    with ExitStack() as ctx:
        m = Mem(nc, ctx)
        cst = {
            "ident": m.sb("ident", [P, P]), "iota": m.sb("iota", [P, P]), "ones": m.sb("ones", [P, P]),
            "rel": m.sb("rel", [P, 2, NT + 2]), "first": m.sb("first", [1, 2, NT], I32),
            "wide": m.sb("wide", [1, 2], I32),
            "slope": m.sb("slope", [P, 1]), "start": m.sb("run_start", [P, NB], I32), "runs": dram("runs", (EP, H8)),
        }
        cst["loads"] = [("slope", io["prelu_a"].to_broadcast([P, 1]))]
        stage_constants(nc, cst, io)
        tables = [dram(f"table{i}", (NP_, D)) for i in range(2)]
        xn_d, x1_d, x2_d, x3_d = (dram(n, (NP_, D)) for n in ("xn_d", "x1_d", "x2_d", "x3_d"))
        xp = dram("xp_d", (L, P, 2 * Q4))

        with ExitStack() as lctx:
            acc = Mem(nc, lctx).sb("acc", [P, 3, NP_ + P])
            hist = acc[:, 0:2, 0:NP_]
            with ExitStack() as gctx:
                gm = Mem(nc, gctx)
                w1, w2 = gm.sb("w1", [P, 2, D]), gm.sb("w2", [P, 2, D])
                b1, b2 = gm.sb("b1", [P, D]), gm.sb("b2", [P, D])
                stage_load(nc, "gw", [(w1, rows2(io["W1T"])), (w2, rows2(io["W2T"])),
                                      (b1, io["b1"].to_broadcast([P, D])), (b2, io["b2"].to_broadcast([P, D]))])
                stage_nodes(nc, cst, "n1", make_plain, 1, loads=[io["x"]], keep=xn_d, keep_row=True, proj=w1,
                            outs=[(tables[0], 0, D)])
                stage_gather_sum(nc, cst, "s1", tables[0], io["idx"], acc, parts=3)
                stage_run_starts(nc, cst, acc)
                stage_over_degree(nc, cst, "d1", acc, new=True)
                stage_nodes(nc, cst, "e1", make_edge_rows, 1, norm=False, keep=tables[1], hT=acc)
                stage_gather_sum(nc, cst, "s2", tables[1], io["idx"], acc)
                stage_over_degree(nc, cst, "d2", acc, new=False)

                def make_mid(dve, link, g, bufs, pre, tmp, psH):
                    bias_and_prelu(dve, link, psH, pre, tmp, b1, cst["slope"])

                stage_nodes(nc, cst, "n2", make_mid, 3, norm=False, hT=acc, proj=w2, outs=[(tables[0], 0, D)])
                stage_gather_sum(nc, cst, "s3", tables[0], io["idx"], acc)
                stage_over_degree(nc, cst, "d3", acc, new=False)
                stage_nodes(nc, cst, "e2", make_edge_rows, 1, norm=False, keep=tables[1], hT=acc)
                stage_gather_sum(nc, cst, "s4", tables[1], io["idx"], acc)
                stage_over_degree(nc, cst, "d4", acc, new=False)

                def make_x1(dve, link, g, bufs, pre, tmp, psH):
                    bias_and_prelu(dve, link, psH, pre, tmp, b2, cst["slope"], skip=bufs[1])
                    link(dve.tensor_tensor(pre[:], pre[:], bufs[0][:], ALU.add))

                stage_nodes(nc, cst, "n3", make_x1, 5, loads=[io["x"], xn_d], keep=x1_d, hT=acc, xT=hist)
            renew_semaphores(nc)
            stage_lstm_inputs(nc, cst, io, hist, xp)
            with ExitStack() as sctx:
                sm = Mem(nc, sctx)
                mem = {"whh": sm.sb("whh", [P, 2, 4 * D]), "h": sm.sb("h", [P, 2, C]), "qc": sm.sb("qc", [P, 2, 2 * C]),
                       "gs": sm.sb("gs", [P, 2, 3 * C]), "nxt": sm.sb("nxt", [P, 4, C]),
                       "start": sm.sb("start", [P, 4, C]), "settled": sm.sb("settled", [1, 1], I32), "hist": hist}
                stage_clear(nc, "lz", [mem["nxt"][:], hist[:, :, N:NP_]])
                stage_load(nc, "lw", [(mem["whh"], rows2(io["WhhT"]))])
                stage_sweeps(nc, cst, mem, xp, "sg", 1, skip=10)
                stage_sweeps(nc, cst, mem, xp, "sw", 1)
                stage_sweeps(nc, cst, mem, xp, "sx", C - 1, unless=mem["settled"])
            renew_semaphores(nc)
            stage_gated_sums(nc, cst, io, hist)
            with ExitStack() as actx:
                am = Mem(nc, actx)
                proj = am.sb("head_proj", [P, 2, D + 2 * H8])
                stage_head_scores(nc, cst, io, proj)
                h_t, s_seg, s_oth = dram("h_t", (NP_, D)), dram("s_seg", (NP_, H8)), dram("s_oth", (NP_, H8))

                def make_x2(dve, link, g, bufs, pre, tmp, psH):
                    link(dve.tensor_tensor(pre[:], turned_back(psH), bufs[0][:], ALU.add))

                stage_nodes(nc, cst, "n4", make_x2, 1, loads=[x1_d], keep=x2_d, hT=hist, proj=proj,
                            outs=[(h_t, 0, D), (s_seg, D, D + H8), (s_oth, D + H8, D + 2 * H8)])
        with ExitStack() as ectx:
            em = Mem(nc, ectx)
            ex = em.sb("ex", [P, NT, H8])
            stage_scatter_scores(nc, cst, s_seg)
            stage_edge_weights(nc, cst, io, s_oth, ex)
            acc = em.sb("acc_att", [P, 3, NP_ + P])
            x3T = acc[:, 0:2, 0:NP_]
            stage_gather_sum(nc, cst, "s5", h_t, io["idx"], acc, parts=3, ex=ex)
            stage_over_sums(nc, cst, io, acc)
            stage_nodes(nc, cst, "n5", make_x2, 1, loads=[x2_d], keep=x3_d, hT=acc, xT=x3T)
            stage_experts(nc, cst, io, x3T, x3_d, out)


def layout(z):
    import numpy as np
    a = {k: np.asarray(v) for k, v in z.items()}
    src = np.concatenate([a["src"], np.zeros(EP - E, np.int32)]).reshape(NT, P)
    dst = np.concatenate([a["dst"], np.full(EP - E, NP_ - 1, np.int32)]).reshape(NT, P)
    tiles = lambda t: np.ascontiguousarray(t.reshape(NIT, TIT, P).transpose(0, 2, 1))
    cols = lambda t: np.ascontiguousarray(t.reshape(TIT, NIT, P).transpose(1, 2, 0))
    row = lambda v: np.ascontiguousarray(v.reshape(1, -1))
    gate_cols = lambda v: np.ascontiguousarray(v.reshape(4, 2, P)[list(GATES)].transpose(2, 1, 0).reshape(P, 8))
    half_cols = lambda v: np.ascontiguousarray(v.reshape(-1, P).T)
    flat = dst.reshape(-1)
    ringed = np.concatenate([[-1], flat, [-1]]).astype(np.int32)
    piece = EP // TIT
    pieces = np.stack([ringed[j * piece:j * piece + piece + 2] for j in range(TIT)])
    halves = lambda w: np.ascontiguousarray(w.reshape(NEXP, 2, P, D).transpose(2, 0, 1, 3))
    cols2 = lambda b: np.ascontiguousarray(b.reshape(NEXP, 2, P).transpose(2, 0, 1))
    return {
        "x": np.concatenate([a["x"], np.zeros((NP_ - N, D), np.float32)]),
        "idx": tiles(src), "src_cols": cols(src),
        "dstT": np.ascontiguousarray(dst.T),
        "prelu_a": a["L0_gnn_prelu_a"].reshape(1, 1),
        "W1T": np.ascontiguousarray(a["L0_gnn_W1"].T), "W2T": np.ascontiguousarray(a["L0_gnn_W2"].T),
        "WihT": np.ascontiguousarray(a["L0_ffn_W_ih"].T), "WhhT": np.ascontiguousarray(a["L0_ffn_W_hh"].T),
        "b_ih": gate_cols(a["L0_ffn_b_ih"]), "b_hh": gate_cols(a["L0_ffn_b_hh"]),
        "W_lin": np.ascontiguousarray(a["L0_ffn_W_lin"].reshape(2, 2, P).transpose(2, 1, 0)),
        "b_lin": row(a["L0_ffn_b_lin"]), "fw": half_cols(a["L0_ffn_fw_att"]), "bw": half_cols(a["L0_ffn_bw_att"]),
        "dst_pieces": pieces, "headW": np.ascontiguousarray(a["L1_gnn_W"].transpose(1, 0, 2).reshape(D, D)),
        "headWT": np.ascontiguousarray(a["L1_gnn_W"].transpose(2, 0, 1)),
        "headA": np.ascontiguousarray(a["L1_gnn_a"].reshape(H8, 2, D // H8).transpose(2, 1, 0)),
        "ew1": halves(a["L1_ffn_expert_w1"]), "ew2": halves(a["L1_ffn_expert_w2"]),
        "ew3": halves(a["L1_ffn_expert_w3"]), "eb1": cols2(a["L1_ffn_expert_b1"]), "eb2": cols2(a["L1_ffn_expert_b2"]),
        "eb3": np.ascontiguousarray(a["L1_ffn_expert_b3"][None]), "rw1": a["L1_ffn_router_w1"],
        "rb1": a["L1_ffn_router_b1"].reshape(P, 1), "rw2": a["L1_ffn_router_w2"], "rb2": row(a["L1_ffn_router_b2"]),
        "head_sel": (np.arange(P)[:, None] == 16 * (np.arange(D)[None] // 32)).astype(np.float32),
        "b1": row(a["L0_gnn_b1"]), "b2": row(a["L0_gnn_b2"]),
    }


def kernel(**inputs):
    import numpy as np
    import concourse.bacc as bacc
    from concourse.bass_utils import run_bass_kernel_spmd

    nc = bacc.Bacc("TRN2", target_bir_lowering=False, num_devices=1)
    arrays = layout(inputs)
    io = {k: nc.dram_tensor(f"in_{k}", a.shape, mybir.dt.from_np(a.dtype), kind="ExternalInput").ap()
          for k, a in arrays.items()}
    out = nc.dram_tensor("out", (NP_, D), F32, kind="ExternalOutput").ap()
    build(nc, io, out)
    r = run_bass_kernel_spmd(nc, [{f"in_{k}": a for k, a in arrays.items()}], core_ids=[0])
    return r.results[0]["out"][0:N]
```

```python
from contextlib import ExitStack

import concourse.bass as bass
from concourse import mybir

F32 = mybir.dt.float32
I32 = mybir.dt.int32
ALU = mybir.AluOpType
ACT = mybir.ActivationFunctionType
AX = mybir.AxisListType

P = 128
N = 6250
D = 256
NB = 49
NP_ = NB * P
BG = 7
NG = NB // BG
BC = BG * P
E = 106250
TIT = 16
JT = 4
NIT = 52
NT = NIT * TIT
EP = NT * P
H8 = 8
C = 125
L = 50
BIG = 1.0e30
SETTLED = 4.0e-6
NEXP = 6
HC = BC // 2


class Mem:

    semaphores = []

    def __init__(self, nc, ctx):
        self.nc, self.ctx = nc, ctx

    def sb(self, name, shape, dt=F32):
        return self.ctx.enter_context(self.nc.sbuf_tensor(name, shape, dt))

    def ps(self, name, shape, dt=F32):
        return self.ctx.enter_context(self.nc.psum_tensor(name, shape, dt))

    def sem(self, name):
        Mem.semaphores.append(self.nc.alloc_semaphore(name=name))
        return Mem.semaphores[-1]


def renew_semaphores(nc):
    nc.clear_and_free_semaphores(Mem.semaphores)
    nc.all_engine_barrier()
    Mem.semaphores = []


def blocks_of(t):
    return t.rearrange("(g b p) c -> g p b c", b=BG, p=P)


def stage_constants(nc, cst, io):
    with ExitStack() as ctx:
        m = Mem(nc, ctx)
        ii = m.sb("c_iota_i", [P, P], I32)
        dst_f = m.sb("c_dst_f", [P, NT])
        dst_i = m.sb("c_dst_i", [P, NT], I32)
        span = m.sb("c_span", [1, NT // JT + 1])
        ps = m.ps("c_ps", [P, 3, 512])
        loaded, iota_ok, zeroed, ident_ok = m.sem("c_loaded"), m.sem("c_iota"), m.sem("c_zeroed"), m.sem("c_ident")
        v, bc = m.sem("c_v"), m.sem("c_bc")
        block = ctx.enter_context(nc.Block())
        half = NT // 2
        NJ = NT // JT
        heads = dst_f[0:1, :].rearrange("p (g k) -> p g k", k=JT)[:, :, 0:1].rearrange("p g k -> p (g k)")

        @block.sync
        def _(sp):
            sp.dma_start(dst_i[:], io["dstT"]).then_inc(loaded, 16)
            for name, view in cst["loads"]:
                sp.dma_start(cst[name][:], view).then_inc(loaded, 16)
            sp.wait_ge(loaded, 16 * (1 + len(cst["loads"])))

        @block.gpsimd
        def _(pool):
            pool.iota(ii[:], [[1, P]], base=0, channel_multiplier=0).then_inc(iota_ok, 1)
            pool.memset(cst["ident"][:], 0.0).then_inc(zeroed, 1)
            pool.wait_ge(zeroed, 1)
            pool.affine_select(out=cst["ident"][:], in_=cst["ident"][:], compare_op=ALU.not_equal, fill=1.0,
                               base=0, pattern=[[-1, P]], channel_multiplier=1).then_inc(ident_ok, 1)

        @block.vector
        def _(dve):
            dve.memset(cst["ones"][:], 1.0).then_inc(v, 1)
            dve.memset(cst["rel"][:, :, NT:NT + 2], 0.0).then_inc(v, 1)
            dve.wait_ge(iota_ok, 1)
            dve.tensor_copy(cst["iota"][:], ii[:]).then_inc(v, 1)
            dve.wait_ge(loaded, 16 * (1 + len(cst["loads"])))
            dve.tensor_copy(cst["first"][:, 0, :], dst_i[0:1, :]).then_inc(v, 1)
            dve.tensor_copy(cst["first"][:, 1, 0:NJ], dst_i[0:1, :].rearrange("p (g k) -> p g k", k=JT)[:, :, 0:1]
                            .rearrange("p g k -> p (g k)")).then_inc(v, 1)
            dve.tensor_copy(dst_f[:], dst_i[:]).then_inc(v, 1)
            dve.wait_ge(bc, 3)
            for h in range(2):
                dve.tensor_tensor(cst["rel"][:, 0, h * half:(h + 1) * half], dst_f[:, h * half:(h + 1) * half],
                                  ps[:, h, 0:half], ALU.subtract).then_inc(v, 1)
            dve.tensor_tensor(cst["rel"][:, 1, 0:NT].rearrange("p (g k) -> p g k", k=JT),
                              dst_f[:].rearrange("p (g k) -> p g k", k=JT),
                              ps[:, 2, 0:NJ].unsqueeze(2).to_broadcast([P, NJ, JT]), ALU.subtract).then_inc(v, 1)
            dve.tensor_tensor(span[:, 0:NJ - 1], heads[:, 1:NJ], heads[:, 0:NJ - 1], ALU.subtract).then_inc(v, 1)
            dve.tensor_scalar(span[:, NJ - 1:NJ], heads[:, NJ - 1:NJ], -1.0, float(NP_ - 1), ALU.mult, ALU.add
                              ).then_inc(v, 1)
            dve.wait_ge(v, 11)
            dve.tensor_reduce(span[:, NJ:NJ + 1], span[:, 0:NJ], AX.X, ALU.max).then_inc(v, 1)
            dve.wait_ge(v, 12)
            dve.tensor_scalar(cst["wide"][:, 0:1], span[:, NJ:NJ + 1], float(P), None, ALU.is_ge).then_inc(v, 1)
            dve.tensor_scalar(cst["wide"][:, 1:2], span[:, NJ:NJ + 1], float(P), None, ALU.is_lt).then_inc(v, 1)

        @block.tensor
        def _(pe):
            pe.wait_ge(v, 6)
            for h in range(2):
                pe.matmul(ps[:, h, 0:half], cst["ones"][0:1, :], dst_f[0:1, h * half:(h + 1) * half], start=True,
                          stop=True).then_inc(bc, 1)
            pe.matmul(ps[:, 2, 0:NJ], cst["ones"][0:1, :], heads, start=True, stop=True).then_inc(bc, 1)


def narrow_or_wide(cst, eng, program):
    for flag, joint in ((0, JT), (1, 1)):
        other_case = eng.value_load(cst["wide"][0:1, flag:flag + 1], min_val=0, max_val=1)
        with eng.If(other_case < 1):
            program(joint)


def stage_gather_sum(nc, cst, name, table, idx, acc, parts=2):
    G4 = 4
    LA = 2
    OH = 4
    with ExitStack() as ctx:
        m = Mem(nc, ctx)
        rows = m.sb(f"{name}_rows", [P, TIT, D])
        ids = [m.sb(f"{name}_ids{i}", [P, TIT // 2], I32) for i in range(2)]
        onehot = [m.sb(f"{name}_onehot{i}", [P, P]) for i in range(OH)]
        part = [m.ps(f"{name}_part{i}", [P, 3, 512]) for i in range(2)]
        ids_in = [m.sem(f"{name}_ids_in{i}") for i in range(2)]
        rows_in = [m.sem(f"{name}_rows_in{i}") for i in range(G4)]
        onehot_ready = m.sem(f"{name}_onehot_ready")
        summed = m.sem(f"{name}_summed")
        added = m.sem(f"{name}_added")
        issue = m.sem(f"{name}_issue")
        block = ctx.enter_context(nc.Block())

        @block.sync
        def _(sp):
            for half in range(2):
                sp.dma_start(ids[half][:], idx[0, :, half * 8:half * 8 + 8]).then_inc(ids_in[half], 16)
            with sp.Fori(0, NIT - 1) as i:
                for half in range(2):
                    for g in (2 * half, 2 * half + 1):
                        sp.wait_ge(rows_in[g], 16 * G4 * i + 16 * G4)
                    sp.dma_start(ids[half][:], idx[bass.ds(i + 1, 1), :, half * 8:half * 8 + 8]
                                 .rearrange("a p k -> (a p) k")).then_inc(ids_in[half], 16)

        @block.gpsimd
        def _(pool):
            with pool.Fori(0, NIT) as i:
                for t in range(TIT):
                    if t % 8 == 0:
                        pool.wait_ge(ids_in[t // 8], 16 * i + 16)
                    if t % G4 == 0:
                        pool.wait_ge(summed, TIT * i + t + G4)
                        pool.sem_inc(issue, 1)
                    pool.indirect_dma_start(rows[:, t, :], None, table,
                                            bass.IndirectOffsetOnAxis(ids[t // 8][:, t % 8:t % 8 + 1], 0)
                                            ).then_inc(rows_in[t // G4], 16)

        @block.vector
        def _(dve):
            dve.memset(acc[:, 0:parts, :], 0.0).then_inc(added, 2)

            def make_onehot(col, buf, joint):
                dve.wait_ge(summed, col + TIT - OH + 1)
                rel = cst["rel"][:, int(joint > 1), :]
                dve.tensor_scalar(onehot[buf][:], cst["iota"][:], rel[:, bass.ds(col, 1)], None,
                                  ALU.is_equal).then_inc(onehot_ready, 1)

            def program(joint):
                for t in range(LA):
                    make_onehot(t, t % OH, joint)

                with dve.Fori(0, NIT) as i:
                    for t in range(TIT):
                        if t % (4 * joint) == 0:
                            group = (TIT // joint) * i + t // joint
                            firsts = cst["first"][0:1, 0, bass.ds(group, 4)] if joint == 1 else \
                                cst["first"][0:1, 1, bass.ds(group, 4)]
                            _, first = nc.values_load_multi_w_load_instructions(
                                firsts, engines=[mybir.EngineType.DVE], min_val=0, max_val=NP_ - 1)
                        make_onehot(TIT * i + t + LA, (t + LA) % OH, joint)
                        if t % joint == joint - 1:
                            g = t // joint
                            dve.wait_ge(summed, TIT * i + t + TIT + 1)
                            dve.wait_ge(added, (TIT // joint) * i + g + 2)
                            a = acc[:, 0:parts, bass.ds(first[g % 4], P)]
                            dve.tensor_tensor(a, a, part[g % 2][:, 0:parts, 0:P], ALU.add).then_inc(added, 1)

            narrow_or_wide(cst, dve, program)

        @block.tensor
        def _(pe):
            def program(joint):
                with pe.Fori(0, NIT) as i:
                    for t in range(TIT):
                        g = t // joint
                        if t % G4 == 0:
                            pe.wait_ge(rows_in[t // G4], 16 * G4 * i + 16 * G4)
                        pe.wait_ge(onehot_ready, TIT * i + t + 1)
                        if t % joint == 0:
                            pe.wait_ge(added, (TIT // joint) * i + g + 1)
                        for k in range(parts):
                            lhs = rows[:, t, k * P:(k + 1) * P] if k < 2 else cst["ones"][:]
                            ins = pe.matmul(part[g % 2][:, k, 0:P], lhs, onehot[t % OH][:], start=(t % joint == 0),
                                            stop=(t % joint == joint - 1))
                        ins.then_inc(summed, 1)

            pe.sem_inc(summed, TIT)
            narrow_or_wide(cst, pe, program)


def stage_run_starts(nc, cst, acc):
    start, runs = cst["start"], cst["runs"]
    with ExitStack() as ctx:
        m = Mem(nc, ctx)
        zero, upto = m.sb("rs_zero", [1, NP_]), m.sb("rs_upto", [1, NP_])
        start_f = m.sb("rs_start_f", [P, NB])
        fill = m.sb("rs_fill", [P, NT * H8])
        ps = m.ps("rs_ps", [P, 512])
        v, made, filled, stored = m.sem("rs_v"), m.sem("rs_made"), m.sem("rs_filled"), m.sem("rs_stored")
        block = ctx.enter_context(nc.Block())

        @block.sync
        def _(sp):
            sp.wait_ge(filled, 1)
            sp.dma_start(runs.rearrange("(p t) h -> p (t h)", p=P), fill[:]).then_inc(stored, 16)
            sp.wait_ge(stored, 16)

        @block.gpsimd
        def _(pool):
            pool.memset(fill[:], -BIG).then_inc(filled, 1)

        @block.vector
        def _(dve):
            deg = acc[0:1, 2, 0:NP_]
            dve.memset(zero[:], 0.0).then_inc(v, 1)
            dve.wait_ge(v, 1)
            dve.tensor_tensor_scan(upto[:], zero[:], deg, 0.0, ALU.add, ALU.add).then_inc(v, 1)
            dve.wait_ge(v, 2)
            dve.tensor_tensor(upto[:], upto[:], deg, ALU.subtract).then_inc(v, 1)
            dve.tensor_scalar(zero[:], deg, 0.0, float(EP), ALU.is_equal, ALU.mult).then_inc(v, 1)
            dve.wait_ge(v, 4)
            dve.tensor_tensor(upto[:], upto[:], zero[:], ALU.add).then_inc(v, 1)
            dve.wait_ge(made, 1)
            dve.tensor_copy(start[:], ps[:, 0:NB]).then_inc(v, 1)

        @block.tensor
        def _(pe):
            pe.wait_ge(v, 5)
            for b in range(NB):
                ins = pe.matmul(ps[:, b:b + 1], upto[0:1, b * P:(b + 1) * P], cst["ones"][0:1, 0:1], start=True,
                                stop=True)
            ins.then_inc(made, 1)


def stage_over_degree(nc, cst, name, acc, new):
    with ExitStack() as ctx:
        v = Mem(nc, ctx).sem(f"{name}_v")
        block = ctx.enter_context(nc.Block())

        @block.vector
        def _(dve):
            if new:
                dve.tensor_scalar(acc[:, 2, :], acc[:, 2, :], 1.0, None, ALU.max).then_inc(v, 1)
                dve.wait_ge(v, 1)
                dve.reciprocal(acc[:, 2, :], acc[:, 2, :]).then_inc(v, 1)
                dve.wait_ge(v, 2)
            dve.tensor_tensor(acc[:, 0:2, :], acc[:, 0:2, :],
                              acc[:, 2:3, :].to_broadcast([P, 2, NP_ + P]), ALU.mult).then_inc(v, 1)


def stage_over_sums(nc, cst, io, acc):
    with ExitStack() as ctx:
        m = Mem(nc, ctx)
        sel = m.sb("os_sel", [P, D])
        ps = [m.ps(f"os_ps{u}", [P, 2, 512]) for u in range(2)]
        sel_in, v, made = m.sem("os_sel_in"), m.sem("os_v"), m.sem("os_made")
        block = ctx.enter_context(nc.Block())
        n = NP_ // HC

        @block.sync
        def _(sp):
            sp.dma_start(sel[:], io["head_sel"]).then_inc(sel_in, 16)
            sp.wait_ge(sel_in, 16)

        @block.tensor
        def _(pe):
            pe.wait_ge(sel_in, 16)
            pe.wait_ge(v, 2)
            for i in range(n):
                if i >= 2:
                    pe.wait_ge(v, i + 1)
                for k in range(2):
                    ins = pe.matmul(ps[i % 2][:, k, 0:HC], sel[:, k * P:(k + 1) * P], acc[:, 2, i * HC:(i + 1) * HC],
                                    start=True, stop=True)
                ins.then_inc(made, 1)

        @block.vector
        def _(dve):
            dve.tensor_scalar(acc[:, 2, :], acc[:, 2, :], 1e-16, None, ALU.add).then_inc(v, 1)
            dve.wait_ge(v, 1)
            dve.reciprocal(acc[:, 2, :], acc[:, 2, :]).then_inc(v, 1)
            for i in range(n):
                dve.wait_ge(made, i + 1)
                a = acc[:, 0:2, i * HC:(i + 1) * HC]
                dve.tensor_tensor(a, a, ps[i % 2][:, :, 0:HC], ALU.mult).then_inc(v, 1)


def batch(t, g):
    return blocks_of(t)[bass.ds(g, 1)].rearrange("a p b c -> (a p) b c")


def each_batch(eng, body):
    with eng.Fori(0, NG // 2) as r:
        for u in range(2):
            body(2 * r + u, u, r)
    body(NG - 1, (NG - 1) % 2, NG // 2)


def stage_nodes(nc, cst, name, make, steps, loads=(), norm=True, keep=None, keep_row=False, hT=None, proj=None,
                outs=(), xT=None):
    turns = proj is not None or xT is not None
    with ExitStack() as ctx:
        m = Mem(nc, ctx)
        bufs = [[m.sb(f"{name}_in{i}{u}", [P, BG, D]) for i in range(len(loads))] for u in range(2)]
        pre = [m.sb(f"{name}_pre{u}", [P, BG, D]) for u in range(2)]
        row = [m.sb(f"{name}_row{u}", [P, BG, D]) for u in range(2)] if norm else pre
        tmp = m.sb(f"{name}_tmp", [P, BG, D])
        st, mv, std = m.sb(f"{name}_st", [P, BG, 6]), m.sb(f"{name}_mv", [P, BG, 2]), m.sb(f"{name}_std", [P, BG])
        rstd, var = m.sb(f"{name}_rstd", [P, BG]), m.sb(f"{name}_var", [P, BG])
        psT = [m.ps(f"{name}_psT{i}", [P, 512]) for i in range(2)]
        width = proj.shape[2] if proj is not None else 0
        if proj is not None:
            turned = [m.sb(f"{name}_turned{i}", [P, 2, P]) for i in range(2)]
            psY = [m.ps(f"{name}_psY{i}", [P, 512]) for i in range(2)]
            y = [m.sb(f"{name}_y{u}", [P, BG, width]) for u in range(2)]
        psH = None
        if hT is not None:
            hfix = [m.sb(f"{name}_hfix{u}", [P, 2, BC]) for u in range(2)]
            psH = m.ps(f"{name}_psH", [P, 4, 512])
            hfixed = m.sem(f"{name}_hfixed")
            hturned = m.sem(f"{name}_hturned")
        loaded = [m.sem(f"{name}_loaded{u}") for u in range(2)]
        nv = steps + (5 if norm else 0)
        v = m.sem(f"{name}_v")
        kept = [m.sem(f"{name}_kept{u}") for u in range(2)]
        turn = m.sem(f"{name}_turn")
        turn_out = m.sem(f"{name}_turn_out")
        prod = m.sem(f"{name}_prod")
        prod_out = m.sem(f"{name}_prod_out")
        no = len(outs)
        stored = [m.sem(f"{name}_stored{u}") for u in range(2)]
        std_ready = m.sem(f"{name}_std_ready")
        stats_in, loading = m.sem(f"{name}_stats_in"), m.sem(f"{name}_loading")
        placing = m.sem(f"{name}_placing")
        block = ctx.enter_context(nc.Block())
        V0 = 2 * nv

        @block.sync
        def _(sp):
            for u in range(2):
                sp.sem_inc(kept[u], 16)
                sp.sem_inc(stored[u], 16)

            def body(g, u, n):
                store_keep(g, u, n)
                if proj is not None:
                    sp.wait_ge(prod_out, BG * g + BG + 1)
                    for dram, a, b in outs:
                        sp.dma_start(batch(dram, g), y[u][:, :, a:b]).then_inc(stored[u], 16)

            def store_keep(g, u, n):
                if keep is not None:
                    sp.wait_ge(v, V0 + nv * g + (nv if keep_row else steps))
                    sp.dma_start(batch(keep, g), (row if keep_row else pre)[u][:]).then_inc(kept[u], 16)

            if keep is not None or proj is not None:
                each_batch(sp, body)
            for u, count in ((0, NG - NG // 2), (1, NG // 2)):
                if keep is not None:
                    sp.wait_ge(kept[u], 16 * count + 16)
                if proj is not None:
                    sp.wait_ge(stored[u], 16 * no * count + 16)

        @block.gpsimd
        def _(pool):
            def body(g, u, n):
                pool.wait_ge(v, nv * g + nv)
                pool.sem_inc(loading, 1)
                for i, src in enumerate(loads):
                    pool.dma_start(bufs[u][i][:], batch(src, g)).then_inc(loaded[u], 16)

            if loads:
                each_batch(pool, body)

        @block.vector
        def _(dve):
            dve.sem_inc(v, V0)

            def body(g, u, n):
                at = [0]

                def link(ins):
                    at[0] += 1
                    ins.then_inc(v, 1)
                    dve.wait_ge(v, V0 + nv * g + at[0])

                if loads:
                    dve.wait_ge(loaded[u], 16 * len(loads) * n + 16 * len(loads))
                if hT is not None:
                    dve.wait_ge(hturned, g + 3)
                if turns:
                    dve.wait_ge(turn, BG * g + 1)
                if keep is not None:
                    dve.wait_ge(kept[u], 16 * n + 16)
                make(dve, link, g, bufs[u], pre[u], tmp, psH)
                if norm:
                    for b in range(BG):
                        ins = dve.bn_stats(st[:, b, :], pre[u][:, b, :])
                    link(ins)
                    dve.sem_inc(stats_in, 1)
                    for b in range(BG):
                        ins = dve.bn_aggr(mv[:, b, :], st[:, b, :])
                    link(ins)
                    link(dve.tensor_scalar(var[:], mv[:, :, 1], 1e-5, None, ALU.add))
                    dve.wait_ge(std_ready, g + 1)
                    link(dve.reciprocal(rstd[:], std[:]))
                    for b in range(BG):
                        ins = dve.tensor_scalar(row[u][:, b, :], pre[u][:, b, :], mv[:, b, 0:1], rstd[:, b:b + 1],
                                                ALU.subtract, ALU.mult)
                    link(ins)

            each_batch(dve, body)

        @block.scalar
        def _(act):
            act.sem_inc(turn_out, 1)
            act.sem_inc(prod_out, 1)

            def fix(g, u):
                act.wait_ge(hturned, g + 1)
                act.activation(hfix[u][:], hT[:, 0:2, bass.ds(g * BC, BC)], ACT.Copy).then_inc(hfixed, 1)

            if hT is not None:
                fix(0, 0)

            def body(g, u, n):
                if hT is not None and not (isinstance(g, int) and g == NG - 1):
                    fix(g + 1, 1 - u)
                if norm:
                    act.wait_ge(v, V0 + nv * g + steps + 3)
                    act.activation(std[:], var[:], ACT.Sqrt).then_inc(std_ready, 1)
                for b in range(BG + 1 if turns else 0):
                    if b < BG:
                        act.wait_ge(turn, BG * g + b + 2 * BG + 1)
                        if proj is not None:
                            act.wait_ge(prod, BG * g + (b if b >= 2 else 1))
                        if xT is not None:
                            act.sem_inc(placing, 1)
                        to = turned[b % 2][:] if xT is None else xT[:, :, bass.ds(g * BC + b * P, P)]
                        act.activation(to, psT[b % 2][:, 0:D].rearrange("p (k n) -> p k n", k=2), ACT.Copy
                                       ).then_inc(turn_out, 1)
                    if b > 0 and proj is not None:
                        act.wait_ge(prod, BG * g + b + 1)
                        if b == 1:
                            act.wait_ge(stored[u], 16 * no * n + 16)
                        act.activation(y[u][:, b - 1, :], psY[(b - 1) % 2][:, 0:width], ACT.Copy
                                       ).then_inc(prod_out, 1)

            each_batch(act, body)

        @block.tensor
        def _(pe):
            pe.sem_inc(turn, 2 * BG)
            pe.sem_inc(prod, 1)
            if hT is not None:
                pe.sem_inc(hturned, 2)

            def turn_back(g, u):
                pe.wait_ge(hfixed, g + 1)
                pe.wait_ge(v, V0 + nv * g + 1 - nv)
                for b in range(BG):
                    for k in range(2):
                        at = (b % 2) * D + k * P
                        ins = pe.transpose(psH[:, b // 2, at:at + P], hfix[u][:, k, b * P:(b + 1) * P],
                                           cst["ident"][:])
                ins.then_inc(hturned, 1)

            if hT is not None:
                turn_back(0, 0)

            def body(g, u, n):
                if hT is not None and not (isinstance(g, int) and g == NG - 1):
                    turn_back(g + 1, 1 - u)
                if turns:
                    pe.wait_ge(v, V0 + nv * g + nv)
                for b in range(BG + 1 if turns else 0):
                    if b < BG:
                        pe.wait_ge(turn_out, BG * g + (b if b >= 2 else 1))
                        for k in range(2):
                            ins = pe.transpose(psT[b % 2][:, k * P:(k + 1) * P], row[u][:, b, k * P:(k + 1) * P],
                                               cst["ident"][:])
                        ins.then_inc(turn, 1)
                    if b > 0 and proj is not None:
                        pe.wait_ge(turn_out, BG * g + b + 1)
                        pe.wait_ge(prod_out, BG * g + (b - 1 if b > 2 else 1))
                        for k in range(2):
                            ins = pe.matmul(psY[(b - 1) % 2][:, 0:width], turned[(b - 1) % 2][:, k, :],
                                            proj[:, k, :], start=(k == 0), stop=(k == 1))
                        ins.then_inc(prod, 1)

            each_batch(pe, body)


def rows2(w):
    return w.rearrange("(k p) n -> p k n", p=P)


def stage_load(nc, name, pairs):
    with ExitStack() as ctx:
        done = Mem(nc, ctx).sem(f"{name}_done")
        block = ctx.enter_context(nc.Block())

        @block.sync
        def _(sp):
            for to, view in pairs:
                sp.dma_start(to if isinstance(to, bass.AP) else to[:], view).then_inc(done, 16)
            sp.wait_ge(done, 16 * len(pairs))


def make_plain(dve, link, g, bufs, pre, tmp, ps):
    link(dve.tensor_copy(pre[:], bufs[0][:]))


def turned_back(psH):
    return psH[:].rearrange("p a (b d) -> p (a b) d", b=2)[:, 0:BG, :]


def bias_and_prelu(dve, link, psH, pre, tmp, bias, slope, skip=None):
    link(dve.tensor_tensor(pre[:], turned_back(psH), bias[:].unsqueeze(1).to_broadcast([P, BG, D]), ALU.add))
    if skip is not None:
        link(dve.tensor_tensor(pre[:], pre[:], skip[:], ALU.add))
    link(dve.tensor_scalar(tmp[:], pre[:], 0.0, slope[:, 0:1], ALU.min, ALU.mult))
    link(dve.scalar_tensor_tensor(out=pre[:], in0=pre[:], scalar=0.0, in1=tmp[:], op0=ALU.max, op1=ALU.add))


GATES = (0, 1, 3, 2)
Q4 = 4 * C


def stage_lstm_inputs(nc, cst, io, xT, xp):
    with ExitStack() as ctx:
        m = Mem(nc, ctx)
        wih = m.sb("wih", [P, 2, 4 * D])
        bih, bhh, bias = m.sb("bih", [P, 8]), m.sb("bhh", [P, 8]), m.sb("lbias", [P, 8])
        stage = [m.sb(f"xp_stage{u}", [P, 2, Q4]) for u in range(2)]
        ps = [[m.ps(f"xp_ps{u}{k}", [P, 512]) for k in range(2)] for u in range(2)]
        w_in, b_ok = m.sem("xp_w_in"), m.sem("xp_b_ok")
        made, biased = m.sem("xp_made"), m.sem("xp_biased")
        stored = [m.sem(f"xp_stored{u}") for u in range(2)]
        block = ctx.enter_context(nc.Block())

        @block.sync
        def _(sp):
            sp.dma_start(wih[:], rows2(io["WihT"])).then_inc(w_in, 16)
            sp.dma_start(bih[:], io["b_ih"]).then_inc(w_in, 16)
            sp.dma_start(bhh[:], io["b_hh"]).then_inc(w_in, 16)
            for u in range(2):
                sp.sem_inc(stored[u], 16)
            with sp.Fori(0, L // 2) as r:
                for u in range(2):
                    sp.wait_ge(biased, 4 * r + 2 * u + 6)
                    sp.dma_start(xp[bass.ds(2 * r + u, 1)].rearrange("a p q -> (a p) q"),
                                 stage[u][:].rearrange("p k q -> p (k q)")).then_inc(stored[u], 16)
            for u in range(2):
                sp.wait_ge(stored[u], 16 * (L // 2) + 16)

        @block.tensor
        def _(pe):
            pe.wait_ge(w_in, 48)
            xs = xT[:, :, 0:N].rearrange("p k (c s) -> p k s c", s=L)
            with pe.Fori(0, L // 2) as r:
                for u in range(2):
                    for k in range(2):
                        pe.wait_ge(biased, 4 * r + 2 * u + k + 1)
                        for q, gate in enumerate(GATES):
                            col = gate * D + k * P
                            for kk in range(2):
                                ins = pe.matmul(ps[u][k][:, q * C:(q + 1) * C], wih[:, kk, col:col + P],
                                                xs[:, kk, bass.ds(2 * r + u, 1), :].rearrange("p a c -> p (a c)"),
                                                start=(kk == 0), stop=(kk == 1))
                        ins.then_inc(made, 1)

        @block.vector
        def _(dve):
            dve.sem_inc(biased, 4)
            dve.wait_ge(w_in, 48)
            dve.tensor_tensor(bias[:], bih[:], bhh[:], ALU.add).then_inc(b_ok, 1)
            dve.wait_ge(b_ok, 1)
            with dve.Fori(0, L // 2) as r:
                for u in range(2):
                    for k in range(2):
                        if k == 0:
                            dve.wait_ge(stored[u], 16 * r + 16)
                        dve.wait_ge(made, 4 * r + 2 * u + k + 1)
                        dve.tensor_tensor(stage[u][:, k, :].rearrange("p (q c) -> p q c", q=4),
                                          ps[u][k][:, 0:Q4].rearrange("p (q c) -> p q c", q=4),
                                          bias[:, 4 * k:4 * k + 4].unsqueeze(2).to_broadcast([P, 4, C]),
                                          ALU.add).then_inc(biased, 1)


def stage_sweeps(nc, cst, mem, xp, name, sweeps, skip=0, unless=None):
    R0, LS = skip // 2, L - skip
    whh, h, qc, gs, nxt, start, hist = (mem[k] for k in ("whh", "h", "qc", "gs", "nxt", "start", "hist"))
    with ExitStack() as ctx:
        m = Mem(nc, ctx)
        xin = [m.sb(f"{name}_xin{u}", [P, 2, Q4]) for u in range(2)]
        pr = [m.sb(f"{name}_pr{k}", [P, 2 * C]) for k in range(2)]
        tc = [m.sb(f"{name}_tc{k}", [P, C]) for k in range(2)]
        dif = m.sb(f"{name}_dif", [P, 4, C])
        far = m.sb(f"{name}_far", [P, 4])
        ps = [[m.ps(f"{name}_ps{u}{k}", [P, 512]) for k in range(2)] for u in range(2)]
        ps_far = m.ps(f"{name}_ps_far", [1, P])
        x_in = [m.sem(f"{name}_x_in{u}") for u in range(2)]
        gates = [m.sem(f"{name}_gates{k}") for k in range(2)]
        x_used = m.sem(f"{name}_x_used")
        acted = [m.sem(f"{name}_acted{k}") for k in range(2)]
        mixed = [m.sem(f"{name}_mixed{k}") for k in range(2)]
        c_ready = [m.sem(f"{name}_c_ready{k}") for k in range(2)]
        tc_ready = [m.sem(f"{name}_tc_ready{k}") for k in range(2)]
        h_ready = [m.sem(f"{name}_h_ready{k}") for k in range(2)]
        noted = [m.sem(f"{name}_noted{k}") for k in range(2)]
        shifted = m.sem(f"{name}_shifted")
        loaded = m.sem(f"{name}_loaded")
        judged, far_turned = m.sem(f"{name}_judged"), m.sem(f"{name}_far_turned")
        block = ctx.enter_context(nc.Block())

        def only_if_needed(eng, program):
            if unless is None:
                return program()
            done = eng.value_load(unless[0:1, 0:1], min_val=0, max_val=1)
            with eng.If(done < 1):
                program()

        @block.sync
        def _(sp):
            def program():
                with sp.Fori(0, sweeps) as w:
                    with sp.Fori(0, LS // 2) as r:
                        for u in range(2):
                            sp.wait_ge(x_used, w * LS + 2 * r + u + 1)
                            sp.dma_start(xin[u][:].rearrange("p k q -> p (k q)"),
                                         xp[bass.ds(2 * (r + R0) + u, 1)].rearrange("a p q -> (a p) q")
                                         ).then_inc(x_in[u], 16)
            only_if_needed(sp, program)

        @block.tensor
        def _(pe):
            def program():
                pe.sem_inc(x_used, 2)
                with pe.Fori(0, sweeps) as w:
                    with pe.Fori(0, LS // 2) as r:
                        for u in range(2):
                            pe.wait_ge(x_in[u], 16 * (w * (LS // 2) + r) + 16)
                            for half in range(2):
                                ins = pe.matmul(ps[u][half][:, 0:Q4], cst["ident"][:], xin[u][:, half, :],
                                                start=True, stop=False, skip_group_check=True)
                            ins.then_inc(x_used, 1)
                            pe.wait_ge(h_ready[0], w * (LS + 1) + 2 * r + u + 1)
                            for half in range(2):
                                for q, gate in enumerate(GATES):
                                    col = gate * D + half * P
                                    pe.matmul(ps[u][half][:, q * C:(q + 1) * C], whh[:, 0, col:col + P], h[:, 0, :],
                                              start=False, stop=False, skip_group_check=True)
                            pe.wait_ge(h_ready[1], w * (LS + 1) + 2 * r + u + 1)
                            for half in range(2):
                                for q, gate in enumerate(GATES):
                                    col = gate * D + half * P
                                    ins = pe.matmul(ps[u][half][:, q * C:(q + 1) * C], whh[:, 1, col:col + P],
                                                    h[:, 1, :], start=False, stop=(q == 3), skip_group_check=True)
                                ins.then_inc(gates[half], 1)
                pe.wait_ge(judged, 2)
                pe.transpose(ps_far[0:1, :], far[:, 0:1], cst["ident"][:]).then_inc(far_turned, 1)
            only_if_needed(pe, program)

        @block.scalar
        def _(act):
            def program():
                with act.Fori(0, sweeps) as w:
                    with act.Fori(0, LS // 2) as r:
                        for u in range(2):
                            s = w * LS + 2 * r + u
                            for k in range(2):
                                act.wait_ge(gates[k], s + 1)
                                act.activation(gs[:, k, 0:3 * C], ps[u][k][:, 0:3 * C], ACT.Sigmoid
                                               ).then_inc(acted[k], 1)
                                act.activation(qc[:, k, 0:C], ps[u][k][:, 3 * C:Q4], ACT.Tanh).then_inc(acted[k], 1)
                            for k in range(2):
                                act.wait_ge(c_ready[k], s + 1)
                                act.activation(tc[k][:], qc[:, k, C:2 * C], ACT.Tanh).then_inc(tc_ready[k], 1)
            only_if_needed(act, program)

        @block.gpsimd
        def _(pool):
            def program():
                hs = hist[:, :, 0:N].rearrange("p k (c s) -> p k s c", s=L)
                for k in range(2):
                    pool.sem_inc(noted[k], 1)
                with pool.Fori(0, sweeps) as w:
                    with pool.Fori(0, LS) as s:
                        for k in range(2):
                            pool.wait_ge(h_ready[k], w * (LS + 1) + s + 2)
                            pool.tensor_copy(hs[:, k, bass.ds(s + skip, 1), :].rearrange("p a c -> p (a c)"), h[:, k, :]
                                             ).then_inc(noted[k], 1)
            only_if_needed(pool, program)

        @block.vector
        def _(dve):
            def program():
                with dve.Fori(0, sweeps) as w:
                    dve.tensor_copy(start[:], nxt[:]).then_inc(loaded, 1)
                    dve.tensor_copy(qc[:, :, C:2 * C], nxt[:, 2:4, :]).then_inc(loaded, 1)
                    for k in range(2):
                        dve.wait_ge(noted[k], w * LS + 1)
                        dve.tensor_copy(h[:, k, :], nxt[:, k, :]).then_inc(h_ready[k], 1)
                    with dve.Fori(0, LS // 2) as r:
                        for u in range(2):
                            s = w * LS + 2 * r + u
                            for k in range(2):
                                dve.wait_ge(acted[k], 2 * s + 2)
                                dve.tensor_tensor(pr[k][:], gs[:, k, 0:2 * C], qc[:, k, :], ALU.mult
                                                  ).then_inc(mixed[k], 1)
                                dve.wait_ge(mixed[k], s + 1)
                                dve.tensor_tensor(qc[:, k, C:2 * C], pr[k][:, 0:C], pr[k][:, C:2 * C], ALU.add
                                                  ).then_inc(c_ready[k], 1)
                            for k in range(2):
                                dve.wait_ge(tc_ready[k], s + 1)
                                dve.wait_ge(noted[k], s + 1)
                                dve.tensor_tensor(h[:, k, :], gs[:, k, 2 * C:3 * C], tc[k][:], ALU.mult
                                                  ).then_inc(h_ready[k], 1)
                    for k in range(2):
                        dve.wait_ge(h_ready[k], w * (LS + 1) + LS + 1)
                        dve.wait_ge(c_ready[k], w * LS + LS)
                    for k in range(2):
                        dve.tensor_copy(nxt[:, k, 1:C], h[:, k, 0:C - 1]).then_inc(shifted, 1)
                        dve.tensor_copy(nxt[:, 2 + k, 1:C], qc[:, k, C:2 * C - 1]).then_inc(shifted, 1)
                    dve.wait_ge(shifted, 4 * w + 4)
                dve.tensor_tensor(dif[:], nxt[:], start[:], ALU.subtract).then_inc(loaded, 1)
                dve.wait_ge(loaded, 2 * sweeps + 1)
                dve.tensor_tensor(dif[:], dif[:], dif[:], ALU.mult).then_inc(judged, 1)
                dve.wait_ge(judged, 1)
                dve.tensor_reduce(far[:, 0:1], dif[:].rearrange("p k c -> p (k c)"), AX.X, ALU.max).then_inc(judged, 1)
                dve.wait_ge(far_turned, 1)
                dve.tensor_reduce(far[0:1, 1:2], ps_far[0:1, :], AX.X, ALU.max).then_inc(judged, 1)
                dve.wait_ge(judged, 3)
                dve.tensor_scalar(mem["settled"][:], far[0:1, 1:2], SETTLED * SETTLED, None, ALU.is_le
                                  ).then_inc(judged, 1)
            only_if_needed(dve, program)


def stage_gated_sums(nc, cst, io, hist):
    TC = 500
    NC_ = 13
    with ExitStack() as ctx:
        m = Mem(nc, ctx)
        wl, wlb = m.sb("wl", [P, 2, 2]), m.sb("wlb", [P, 2, 2, P])
        bl = m.sb("bl", [P, 2])
        fw, bw, nbw = m.sb("fw", [P, 2]), m.sb("bw", [P, 2]), m.sb("nbw", [P, 2])
        w, inc = m.sb("gw", [P, 2, NP_]), m.sb("inc", [P, 2, NP_])
        one = m.sb("one_row", [P, TC])
        l1 = m.sb("l1", [P, TC])
        gate = m.sb("gate", [P, TC])
        ps = [[m.ps(f"gs_ps{u}{l}", [P, 512]) for l in range(2)] for u in range(2)]
        w_in, v, logits = m.sem("gs_w_in"), m.sem("gs_v"), m.sem("gs_logits")
        spread = m.sem("gs_spread")
        block = ctx.enter_context(nc.Block())
        cols = [(i * TC, min(N, (i + 1) * TC)) for i in range(NC_)]

        @block.sync
        def _(sp):
            for to, frm in ((wl, io["W_lin"]), (bl, io["b_lin"].to_broadcast([P, 2])), (fw, io["fw"]), (bw, io["bw"])):
                sp.dma_start(to[:], frm).then_inc(w_in, 16)

        @block.tensor
        def _(pe):
            pe.wait_ge(spread, 5)
            for i, (a, b) in enumerate(cols):
                if i >= 2:
                    pe.wait_ge(v, 5 * (i - 2) + 2)
                for l in range(2):
                    for k in range(2):
                        ins = pe.matmul(ps[i % 2][l][:, 0:b - a], wlb[:, k, l, :], hist[:, k, a:b], start=(k == 0),
                                        stop=(k == 1))
                ins.then_inc(logits, 1)

        @block.vector
        def _(dve):
            dve.wait_ge(w_in, 64)
            for k in range(2):
                for l in range(2):
                    dve.tensor_copy(wlb[:, k, l, :], wl[:, k, l:l + 1].to_broadcast([P, P])).then_inc(spread, 1)
            dve.tensor_scalar(nbw[:], bw[:], -1.0, None, ALU.mult).then_inc(spread, 1)
            dve.memset(one[:], 1.0).then_inc(spread, 1)
            dve.wait_ge(spread, 6)
            for i, (a, b) in enumerate(cols):
                n = b - a
                dve.wait_ge(logits, i + 1)
                dve.tensor_scalar(l1[:, 0:n], ps[i % 2][1][:, 0:n], bl[:, 1:2], None, ALU.add).then_inc(v, 1)
                dve.wait_ge(v, 5 * i + 1)
                dve.scalar_tensor_tensor(out=gate[:, 0:n], in0=ps[i % 2][0][:, 0:n], scalar=bl[:, 0:1],
                                         in1=l1[:, 0:n], op0=ALU.add, op1=ALU.is_lt).then_inc(v, 1)
                dve.wait_ge(v, 5 * i + 2)
                dve.tensor_tensor(w[:, :, a:b], hist[:, :, a:b], gate[:, 0:n].unsqueeze(1).to_broadcast([P, 2, n]),
                                  ALU.mult).then_inc(v, 1)
                dve.wait_ge(v, 5 * i + 3)
                for k in range(2):
                    first = 0.0 if i == 0 else inc[:, k, a - 1:a]
                    dve.tensor_tensor_scan(inc[:, k, a:b], one[:, 0:n], w[:, k, a:b], first, ALU.mult, ALU.add
                                           ).then_inc(v, 1)
                dve.wait_ge(v, 5 * i + 5)
            at = [5 * NC_]

            def link(ins):
                at[0] += 1
                ins.then_inc(v, 1)
                dve.wait_ge(v, at[0])

            link(dve.tensor_tensor(w[:, :, 0:N], inc[:, :, 0:N], w[:, :, 0:N], ALU.subtract))
            for k in range(2):
                total = one[:, k:k + 1]
                link(dve.tensor_copy(total, inc[:, k, N - 1:N]))
                link(dve.tensor_scalar(inc[:, k, 0:N], inc[:, k, 0:N], total, nbw[:, k:k + 1], ALU.subtract, ALU.mult))
                link(dve.scalar_tensor_tensor(out=w[:, k, 0:N], in0=w[:, k, 0:N], scalar=fw[:, k:k + 1],
                                              in1=inc[:, k, 0:N], op0=ALU.mult, op1=ALU.add))
                link(dve.scalar_tensor_tensor(out=hist[:, k, 0:N], in0=hist[:, k, 0:N], scalar=2.0, in1=w[:, k, 0:N],
                                              op0=ALU.mult, op1=ALU.add))


def stage_clear(nc, name, views):
    with ExitStack() as ctx:
        done = Mem(nc, ctx).sem(f"{name}_done")
        block = ctx.enter_context(nc.Block())

        @block.vector
        def _(dve):
            for view in views:
                dve.memset(view, 0.0).then_inc(done, 1)
            dve.wait_ge(done, len(views))


CE = NIT * P


def stage_head_scores(nc, cst, io, proj):
    with ExitStack() as ctx:
        m = Mem(nc, ctx)
        wt, at = m.sb("hs_wt", [D // H8, H8, D]), m.sb("hs_at", [D // H8, 2, H8])
        ps = m.ps("hs_ps", [P, 2, 2 * H8])
        loaded, made, copied = m.sem("hs_loaded"), m.sem("hs_made"), m.sem("hs_copied")
        block = ctx.enter_context(nc.Block())

        @block.sync
        def _(sp):
            sp.dma_start(wt[:], io["headWT"]).then_inc(loaded, 16)
            sp.dma_start(at[:], io["headA"]).then_inc(loaded, 16)
            sp.dma_start(proj[:, :, 0:D], rows2(io["headW"])).then_inc(loaded, 16)
            sp.wait_ge(loaded, 48)

        @block.tensor
        def _(pe):
            pe.wait_ge(loaded, 48)
            for k in range(2):
                for s in range(2):
                    for hd in range(H8):
                        ins = pe.matmul(ps[:, k, s * H8 + hd:s * H8 + hd + 1], wt[:, hd, k * P:(k + 1) * P],
                                        at[:, 1 - s, hd:hd + 1], start=True, stop=True)
            ins.then_inc(made, 1)

        @block.vector
        def _(dve):
            dve.wait_ge(made, 1)
            dve.tensor_copy(proj[:, :, D:D + 2 * H8], ps[:]).then_inc(copied, 1)
            dve.wait_ge(copied, 1)


def stage_own_scores(nc, cst, io, s_seg, lines):
    R = 4
    with ExitStack() as ctx:
        m = Mem(nc, ctx)
        scores = m.sb("ow_scores", [P, NB, H8])
        ga = [m.sb(f"ow_ga{u}", [P, TIT, H8]) for u in range(R)]
        own, top = m.sb("ow_own", [P, CE]), m.sb("ow_top", [P, CE])
        node = m.sb("ow_node", [P, CE + 2], I32)
        cut = [m.sb(f"ow_cut{c}", [P, CE]) for c in range(2)]
        least = m.sb("ow_least", [P, NIT, 2])
        ends = m.sb("ow_ends", [P, 2])
        line = m.sb("ow_line", [1, 2, P])
        run, carry, init = m.sb("ow_run", [1, P]), m.sb("ow_carry", [1, P]), m.sb("ow_init", [P, 1])
        ps = [m.ps(f"ow_ps{u}", [P, P]) for u in range(R)]
        ps_line, ps_init = m.ps("ow_psl", [1, 2, P]), m.ps("ow_psi", [P, 1])
        own_in = [m.sem(f"ow_own_in{u}") for u in range(R)]
        turned, copied = m.sem("ow_turned"), m.sem("ow_copied")
        node_in, v, ends_turned, stored = m.sem("ow_node_in"), m.sem("ow_v"), m.sem("ow_ends_turned"), m.sem("ow_stored")
        issue, loaded, scattered = m.sem("ow_issue"), m.sem("ow_loaded"), m.sem("ow_scattered")
        block = ctx.enter_context(nc.Block())
        CUTS, ENDS, CARRY, DONE = 6, 9, 14, 16

        @block.sync
        def _(sp):
            sp.dma_start(scores[:], s_seg.rearrange("(b p) h -> p b h", p=P)).then_inc(loaded, 16)
            for j in range(TIT):
                sp.dma_start(node[j * H8:(j + 1) * H8, :], io["dst_pieces"][j:j + 1, :].to_broadcast([H8, CE + 2])
                             ).then_inc(node_in, 16)
            runs = cst["runs"].rearrange("(j i p) h -> i p j h", j=TIT, p=P)
            sp.wait_ge(scattered, 16 * NB)
            for u in range(R):
                sp.dma_start(ga[u][:], runs[u]).then_inc(own_in[u], 16)
            with sp.Fori(0, NIT // R - 1) as r:
                for u in range(R):
                    sp.wait_ge(turned, R * r + u + R + 1)
                    sp.dma_start(ga[u][:], runs[bass.ds(R * r + R + u, 1)].rearrange("a p j h -> (a p) j h")
                                 ).then_inc(own_in[u], 16)
            sp.wait_ge(node_in, 16 * TIT)
            to = lines[:, 0:3 * P].rearrange("(j i h) (c e) -> j c h i e", i=NIT, h=H8, c=3)
            sp.wait_ge(v, CUTS)
            for j in range(TIT):
                sp.dma_start(lines[:, 3 * P:3 * P + 2].rearrange("(j i h) c -> j h i c", i=NIT, h=H8)[j],
                             least[j * H8:(j + 1) * H8]).then_inc(stored, 16)
            for c, (frm, step) in enumerate(((top, DONE), (cut[0], CUTS), (cut[1], CUTS))):
                sp.wait_ge(v, step)
                for j in range(TIT):
                    sp.dma_start(to[j, c], frm[j * H8:(j + 1) * H8, :].rearrange("h (i e) -> h i e", e=P)
                                 ).then_inc(stored, 16)
            sp.wait_ge(stored, 16 * 4 * TIT)

        @block.gpsimd
        def _(pool):
            pool.wait_ge(loaded, 16)
            for b in range(NB):
                pool.indirect_dma_start(cst["runs"], bass.IndirectOffsetOnAxis(cst["start"][:, b:b + 1], 0),
                                        scores[:, b, :], None, bounds_check=EP - 1, oob_is_err=False
                                        ).then_inc(scattered, 16)

        @block.tensor
        def _(pe):
            pe.sem_inc(turned, R)
            with pe.Fori(0, NIT // R) as r:
                for u in range(R):
                    pe.wait_ge(copied, R * r + u + 1)
                    pe.wait_ge(own_in[u], 16 * r + 16)
                    pe.transpose(ps[u][:], ga[u][:].rearrange("p j h -> p (j h)"), cst["ident"][:]).then_inc(turned, 1)
            pe.wait_ge(v, ENDS)
            for c in range(2):
                ins = pe.transpose(ps_line[0:1, c, :], ends[:, c:c + 1], cst["ident"][:])
            ins.then_inc(ends_turned, 1)
            pe.wait_ge(v, CARRY)
            pe.matmul(ps_init[:], carry[0:1, :], cst["ones"][0:1, 0:1], start=True, stop=True).then_inc(ends_turned, 1)

        @block.scalar
        def _(act):
            act.sem_inc(copied, R)
            with act.Fori(0, NIT // R) as r:
                for u in range(R):
                    act.wait_ge(turned, R * r + u + R + 1)
                    act.sem_inc(issue, 1)
                    act.activation(own[:, bass.ds((R * r + u) * P, P)], ps[u][:], ACT.Copy).then_inc(copied, 1)

        @block.vector
        def _(dve):
            at = [0]

            def link(ins):
                at[0] += 1
                ins.then_inc(v, 1)
                dve.wait_ge(v, at[0])

            dve.wait_ge(node_in, 16 * TIT)
            for c, k in ((0, 0), (1, 2)):
                link(dve.tensor_tensor(cut[c][:], node[:, 1:CE + 1], node[:, k:CE + k], ALU.not_equal))
                link(dve.tensor_scalar(cut[c][:], cut[c][:], -BIG, None, ALU.mult))
            for c in range(2):
                link(dve.tensor_reduce(least[:, :, c], cut[c][:].rearrange("p (i e) -> p i e", e=P), AX.X, ALU.min))
            dve.wait_ge(copied, NIT + R)
            link(dve.tensor_tensor_scan(top[:], cut[0][:], own[:], -BIG, ALU.add, ALU.max))
            link(dve.tensor_copy(ends[:, 0:1], top[:, CE - 1:CE]))
            link(dve.tensor_reduce(ends[:, 1:2], cut[0][:], AX.X, ALU.min))
            dve.wait_ge(ends_turned, 1)
            lines_to_heads(dve, link, line, ps_line)
            by_head = line[:].rearrange("a c (h j) -> a c h j", h=H8)
            link(dve.memset(by_head[:, 1, :, 0:1], -BIG))
            link(dve.tensor_tensor_scan(run[:], line[:, 1, :], line[:, 0, :], -BIG, ALU.add, ALU.max))
            link(dve.memset(carry[:], -BIG))
            carry_forth(dve, link, carry, run)
            assert at[0] == CARRY, at[0]
            dve.wait_ge(ends_turned, 2)
            link(dve.tensor_copy(init[:], ps_init[:]))
            link(dve.tensor_tensor_scan(top[:], cut[0][:], own[:], init[:], ALU.add, ALU.max))
            assert at[0] == DONE, at[0]


def lines_to_heads(dve, link, line, ps_line):
    link(dve.tensor_copy(line[:].rearrange("a c (h j) -> a c h j", h=H8),
                         ps_line.rearrange("a c (j h) -> a c h j", h=H8)))


def carry_forth(dve, link, carry, run):
    link(dve.tensor_copy(carry[:].rearrange("a (j h) -> a h j", h=H8)[:, :, 1:TIT],
                         run[:].rearrange("a (h j) -> a h j", h=H8)[:, :, 0:TIT - 1]))


def stage_attention(nc, cst, io, table, lines, acc):
    G4, RB = 4, 4
    AHEAD = RB * TIT
    W = D + H8
    with ExitStack() as ctx:
        m = Mem(nc, ctx)
        rows = m.sb("at_rows", [P, RB * TIT, W])
        ids = [m.sb(f"at_ids{i}", [P, TIT], I32) for i in range(2)]
        own = [m.sb(f"at_own{i}", [P, 3 * P + 2]) for i in range(2)]
        zc, z, top, w = (m.sb(f"at_{n}", [P, P]) for n in ("zc", "z", "top", "w"))
        init = m.sb("at_init", [P, 2])
        line, run = m.sb("at_line", [1, 2, P]), m.sb("at_run", [1, P])
        carry = [m.sb(f"at_carry{rd}", [1, P]) for rd in range(2)]
        last = m.sb("at_last", [1, H8, 1])
        joined = m.sb("at_joined", [1, H8, 1])
        fade = m.sb("at_fade", [H8, 2])
        heads = m.sb("at_heads", [H8, 3 * P])
        ex = [m.sb(f"at_ex{i}", [P, TIT, H8]) for i in range(RB)]
        factor = m.sb("at_factor", [P, RB, 3])
        spread = m.sb("at_spread", [P, 2 * G4, H8, P // H8])
        onehot = m.sb("at_onehot", [P, 2 * G4, P])
        part = [m.ps(f"at_part{i}", [P, 3, 512]) for i in range(2)]
        ps_z = m.ps("at_ps_z", [P, 512])
        ps_line = m.ps("at_ps_line", [1, 2, 2, P])
        EXP, INIT, FADE = P, 2 * P, 2 * P + 2
        ids_in = [m.sem(f"at_ids_in{i}") for i in range(2)]
        own_in = [m.sem(f"at_own_in{i}") for i in range(2)]
        heads_in = m.sem("at_heads_in")
        rows_in = [m.sem(f"at_rows_in{i}") for i in range(RB)]
        v = m.sem("at_v")
        zc_ready, pe_turned = m.sem("at_zc_ready"), m.sem("at_pe_turned")
        exped, ex_ready = m.sem("at_exped"), m.sem("at_ex_ready")
        prepared = m.sem("at_prepared")
        weighted, spread_ready = m.sem("at_weighted"), m.sem("at_spread_ready")
        onehot_ready = m.sem("at_onehot_ready")
        summed, added = m.sem("at_summed"), m.sem("at_added")
        forth_done = m.sem("at_forth_done")
        faded = m.sem("at_faded")
        issue = m.sem("at_issue")
        block = ctx.enter_context(nc.Block())
        NV, ENDS, CARRIES, TURNS = 22, (3, 13), (10, 17), 6

        def tiles_in_groups(eng, program):
            with eng.Fori(0, NIT // RB - 1) as r:
                for u in range(RB):
                    program(RB * r + u, u, 2)
            for u in range(RB):
                program(NIT - RB + u, u, min(2, RB - 1 - u))

        @block.sync
        def _(sp):
            sp.dma_start(heads[:], io["head_spread"]).then_inc(heads_in, 16)

            def load(n, b):
                sp.dma_start(ids[b][:], io["idx"][bass.ds(n, 1)].rearrange("a p k -> (a p) k")
                             ).then_inc(ids_in[b], 16)
                sp.wait_ge(prepared, n + 1)
                sp.dma_start(own[b][:], lines[bass.ds(n * P, P), :]
                             ).then_inc(own_in[b], 16)

            for b in range(2):
                load(b, b)
            with sp.Fori(0, NIT // RB - 1) as r:
                for u in range(RB):
                    sp.wait_ge(rows_in[u], 16 * TIT * r + 16 * TIT)
                    load(RB * r + u + 2, u % 2)
            for u in range(RB - 2):
                sp.wait_ge(rows_in[u], 4 * TIT * NIT)
                load(NIT - RB + u + 2, u % 2)
            sp.wait_ge(heads_in, 16)

        @block.gpsimd
        def _(pool):
            with pool.Fori(0, NIT // RB) as r:
                for u in range(RB):
                    pool.wait_ge(ids_in[u % 2], 32 * r + 16 * (u // 2) + 16)
                    for t in range(TIT):
                        if t % G4 == 0:
                            pool.wait_ge(summed, AHEAD * r + TIT * u + t + G4)
                            pool.sem_inc(issue, 1)
                        pool.indirect_dma_start(rows[:, TIT * u + t, :], None, table,
                                                bass.IndirectOffsetOnAxis(ids[u % 2][:, t:t + 1], 0)
                                                ).then_inc(rows_in[u], 16)

        @block.scalar
        def _(act):
            def prepare(n, u, step):
                if step == 5:
                    act.wait_ge(rows_in[u], 4 * TIT * (n - u) + 16 * TIT)
                    act.wait_ge(pe_turned, TURNS * n + 1)
                    act.sem_inc(issue, 1)
                    act.activation(zc[:].rearrange("p (t h) -> p t h", h=H8), rows[:, TIT * u:TIT * (u + 1), D:W],
                                   ACT.Copy).then_inc(zc_ready, 1)
                if step == TIT + 1:
                    act.wait_ge(v, NV * n + NV + 2)
                    act.activation(fade[:, 1:2], fade[:, 0:1], ACT.Exp).then_inc(exped, 1)
                    act.activation(w[:], z[:], ACT.Exp).then_inc(exped, 1)
                if step == TIT + 4:
                    act.wait_ge(pe_turned, TURNS * n + TURNS + 1)
                    act.wait_ge(weighted, TIT * n + TIT)
                    act.activation(factor[:, u, :], ps_z[:, FADE:FADE + 3], ACT.Copy)
                    act.activation(ex[u][:].rearrange("p t h -> p (t h)"), ps_z[:, EXP:EXP + P], ACT.Copy
                                   ).then_inc(ex_ready, 1)

            for step in range(2 * TIT):
                prepare(0, 0, step)
            for step in range(TIT):
                prepare(1, 1, step)

            def group(n, u, left):
                act.wait_ge(ex_ready, n + 2)
                for t in range(TIT):
                    if t % G4 == 0:
                        act.wait_ge(summed, TIT * n + t + AHEAD - G4)
                        act.sem_inc(issue, 1)
                        at = t % (2 * G4)
                        act.activation(spread[:, at:at + G4], ex[u][:, t:t + G4, :].unsqueeze(3)
                                       .to_broadcast([P, G4, H8, P // H8]), ACT.Copy).then_inc(spread_ready, G4)
                    if left:
                        prepare(n + 1, (u + 1) % RB, TIT + t)
                    if left == 2:
                        prepare(n + 2, (u + 2) % RB, t)

            tiles_in_groups(act, group)

        @block.vector
        def _(dve):
            dve.memset(acc[:], 0.0).then_inc(added, 2)
            dve.memset(carry[1][:], -BIG).then_inc(v, 1)
            dve.memset(last[:], -BIG).then_inc(v, 1)
            dve.wait_ge(v, 2)
            dve.sem_inc(prepared, 2)
            dve.sem_inc(weighted, RB * TIT)

            def prepare(n, b, step):
                at = [{7: 0, 9: ENDS[0], 11: CARRIES[0], 13: ENDS[1], 15: CARRIES[1]}.get(step, 0)]

                def mark(ins):
                    at[0] += 1
                    ins.then_inc(v, 1)

                def link(ins):
                    mark(ins)
                    dve.wait_ge(v, NV * n + at[0] + 2)

                by_head = line[:].rearrange("a c (h j) -> a c h j", h=H8)
                run_by_head = run[:].rearrange("a (h j) -> a h j", h=H8)
                forth, back = own[b][:, P:2 * P], own[b][:, 2 * P:3 * P]
                if step == 7:
                    dve.wait_ge(own_in[b], 8 * (n - b) + 16)
                    dve.wait_ge(exped, 2 * n + 2)
                    dve.wait_ge(pe_turned, TURNS * n + 2)
                    link(dve.tensor_tensor(z[:], ps_z[:, 0:P], own[b][:, 0:P], ALU.add))
                    link(dve.scalar_tensor_tensor(out=z[:], in0=z[:], scalar=0.2, in1=z[:], op0=ALU.mult, op1=ALU.max))
                    mark(dve.tensor_tensor_scan(top[:], forth, z[:], -BIG, ALU.add, ALU.max))
                    assert at[0] == ENDS[0]
                if step == 9:
                    dve.wait_ge(pe_turned, TURNS * n + 3)
                    lines_to_heads(dve, link, line, ps_line[:, 0])
                    link(dve.tensor_tensor(joined[:], by_head[:, 1, :, 0:1], last[:], ALU.add))
                    mark(dve.tensor_tensor(by_head[:, 0, :, 0:1], by_head[:, 0, :, 0:1], joined[:], ALU.max))
                    mark(dve.tensor_copy(carry[0][:].rearrange("a (j h) -> a h j", h=H8)[:, :, 0:1], last[:]))
                    link(dve.memset(by_head[:, 1, :, 0:1], -BIG))
                    link(dve.tensor_tensor_scan(run[:], line[:, 1, :], line[:, 0, :], -BIG, ALU.add, ALU.max))
                    carry_forth(dve, mark, carry[0], run)
                    assert at[0] == CARRIES[0], at[0]
                if step == 11:
                    mark(dve.tensor_copy(last[:], run_by_head[:, :, TIT - 1:TIT]))
                    dve.wait_ge(pe_turned, TURNS * n + 4)
                    link(dve.tensor_copy(init[:, 0:1], ps_z[:, INIT:INIT + 1]))
                    assert at[0] == ENDS[1] - 1, at[0]
                    dve.tensor_tensor_scan(top[:], forth, z[:], init[:, 0:1], ALU.add, ALU.max).then_inc(forth_done, 1)
                    dve.wait_ge(forth_done, n + 1)
                    mark(dve.tensor_tensor_scan(top[:, ::-1], back[:, ::-1], top[:, ::-1], -BIG, ALU.add, ALU.max))
                if step == 13:
                    dve.wait_ge(pe_turned, TURNS * n + 5)
                    lines_to_heads(dve, link, line, ps_line[:, 1])
                    link(dve.memset(by_head[:, 1, :, TIT - 1:TIT], -BIG))
                    link(dve.tensor_tensor_scan(run[0:1, ::-1], line[0:1, 1, ::-1], line[0:1, 0, ::-1], -BIG, ALU.add,
                                                ALU.max))
                    mark(dve.tensor_copy(carry[1][:].rearrange("a (j h) -> a h j", h=H8)[:, :, 0:TIT - 1],
                                         run_by_head[:, :, 1:TIT]))
                    assert at[0] == CARRIES[1], at[0]
                if step == 15:
                    dve.wait_ge(pe_turned, TURNS * n + 6)
                    link(dve.tensor_copy(init[:, 1:2], ps_z[:, INIT + 1:INIT + 2]))
                    link(dve.tensor_tensor_scan(top[:, ::-1], back[:, ::-1], top[:, ::-1], init[:, 1:2], ALU.add,
                                                ALU.max))
                    dve.sem_inc(prepared, 1)
                    mark(dve.tensor_tensor(fade[:, 0:1], init[0:H8, 0:1], top[0:H8, 0:1], ALU.subtract))
                    link(dve.tensor_tensor(z[:], z[:], top[:], ALU.subtract))
                    mark(dve.tensor_scalar(fade[:, 0:1], fade[:, 0:1], 0.0, None, ALU.min))
                    assert at[0] == NV, at[0]

            def program(joint):
                for n in range(2):
                    for step in range(TIT):
                        prepare(n, n, step)
                dve.wait_ge(ex_ready, 2)

                def weigh_and_place(n, u, t):
                    rv = rows[:, TIT * u + t:TIT * u + t + G4, 0:D].rearrange("p t (h d) -> p t h d", h=H8)
                    dve.tensor_tensor(rv, rv, ex[u][:, t:t + G4, :].unsqueeze(3).to_broadcast([P, G4, H8, D // H8]),
                                      ALU.mult).then_inc(weighted, G4)
                    at = t % (2 * G4)
                    dve.wait_ge(summed, TIT * n + t + AHEAD - G4)
                    rel = cst["rel"][:, int(joint > 1), :]
                    dve.tensor_tensor(onehot[:, at:at + G4, :], cst["iota"][:].unsqueeze(1).to_broadcast([P, G4, P]),
                                      rel[:, bass.ds(TIT * n + t, G4)].unsqueeze(2).to_broadcast([P, G4, P]),
                                      ALU.is_equal).then_inc(onehot_ready, G4)

                weigh_and_place(0, 0, 0)

                def group(n, u, left):
                    for t in range(TIT):
                        if t % G4 == 0 and t + G4 < TIT:
                            weigh_and_place(n, u, t + G4)
                        elif t % G4 == 0 and left:
                            dve.wait_ge(ex_ready, n + 3)
                            weigh_and_place(n + 1, (u + 1) % RB, 0)
                        if t % (4 * joint) == 0:
                            _, first = nc.values_load_multi_w_load_instructions(
                                cst["first"][0:1, int(joint > 1), bass.ds((TIT // joint) * n + t // joint, 4)],
                                engines=[mybir.EngineType.DVE], min_val=0, max_val=NP_ - 1)
                        if left == 2:
                            prepare(n + 2, u % 2, t)
                        if t == joint - 1:
                            dve.wait_ge(ex_ready, n + 2)
                            dve.wait_ge(added, (TIT // joint) * n + 2)
                            a = acc[:, :, bass.ds(first[0], 1)]
                            dve.tensor_tensor(a, a, factor[:, u, :].unsqueeze(2), ALU.mult).then_inc(faded, 1)
                        if t % joint == joint - 1:
                            g = t // joint
                            dve.wait_ge(summed, TIT * n + t + AHEAD + 1)
                            dve.wait_ge(added, (TIT // joint) * n + g + 2)
                            dve.wait_ge(faded, n + 1)
                            a = acc[:, :, bass.ds(first[g % 4], P)]
                            dve.tensor_tensor(a, a, part[g % 2][:, :, 0:P], ALU.add).then_inc(added, 1)

                tiles_in_groups(dve, group)

            narrow_or_wide(cst, dve, program)

        @block.tensor
        def _(pe):
            def prepare(n, b, step):
                if step == 6:
                    pe.wait_ge(zc_ready, n + 1)
                    pe.wait_ge(ex_ready, n + 1)
                    pe.transpose(ps_z[:, 0:P], zc[:], cst["ident"][:]).then_inc(pe_turned, 1)
                for rd, at, back_at in ((0, 9, 11), (1, 13, 15)):
                    if step == at:
                        pe.wait_ge(v, NV * n + ENDS[rd] + 2)
                        pe.wait_ge(own_in[b], 8 * (n - b) + 16)
                        edge = (P - 1) * (1 - rd)
                        pe.transpose(ps_line[0:1, rd, 0, :], top[:, edge:edge + 1], cst["ident"][:])
                        pe.transpose(ps_line[0:1, rd, 1, :], own[b][:, 3 * P + rd:3 * P + rd + 1], cst["ident"][:]
                                     ).then_inc(pe_turned, 1)
                    if step == back_at:
                        pe.wait_ge(v, NV * n + CARRIES[rd] + 2)
                        pe.matmul(ps_z[:, INIT + rd:INIT + rd + 1], carry[rd][0:1, :], cst["ones"][0:1, 0:1],
                                  start=True, stop=True).then_inc(pe_turned, 1)
                if step == TIT + 3:
                    pe.wait_ge(exped, 2 * n + 4)
                    pe.transpose(ps_z[:, EXP:EXP + P], w[:], cst["ident"][:])
                    for k in range(3):
                        ins = pe.matmul(ps_z[:, FADE + k:FADE + k + 1], heads[:, k * P:(k + 1) * P], fade[:, 1:2],
                                        start=True, stop=True)
                    ins.then_inc(pe_turned, 1)

            def program(joint):
                for step in range(2 * TIT):
                    prepare(0, 0, step)
                for step in range(TIT):
                    prepare(1, 1, step)

                def group(n, u, left):
                    for t in range(TIT):
                        g = t // joint
                        if left:
                            prepare(n + 1, (u + 1) % 2, TIT + t)
                        if left == 2:
                            prepare(n + 2, u % 2, t)
                        pe.wait_ge(weighted, TIT * n + t + RB * TIT + 1)
                        pe.wait_ge(spread_ready, TIT * n + t + 1)
                        pe.wait_ge(onehot_ready, TIT * n + t + 1)
                        if t % joint == 0:
                            pe.wait_ge(added, (TIT // joint) * n + g + 1)
                        for k in range(3):
                            lhs = rows[:, TIT * u + t, k * P:(k + 1) * P] if k < 2 else \
                                spread[:, t % (2 * G4)].rearrange("p h r -> p (h r)")
                            ins = pe.matmul(part[g % 2][:, k, 0:P], lhs, onehot[:, t % (2 * G4), :], start=(t % joint == 0),
                                            stop=(t % joint == joint - 1))
                        ins.then_inc(summed, 1)

                tiles_in_groups(pe, group)

            pe.wait_ge(heads_in, 16)
            pe.sem_inc(pe_turned, 1)
            pe.sem_inc(exped, 2)
            pe.sem_inc(ex_ready, 1)
            pe.sem_inc(summed, AHEAD)
            narrow_or_wide(cst, pe, program)


def stage_experts(nc, cst, io, xT, x3, out):
    with ExitStack() as ctx:
        m = Mem(nc, ctx)
        w1, w2, w3 = (m.sb(f"ew{i}", [P, NEXP, 2, D]) for i in (1, 2, 3))
        b1, b2 = m.sb("eb1", [P, NEXP, 2]), m.sb("eb2", [P, NEXP, 2])
        b3 = m.sb("eb3", [1, NEXP, D])
        rw1, rb1, rw2, rb2 = m.sb("rw1", [P, 2, P]), m.sb("rb1", [P, 1]), m.sb("rw2", [P, NEXP]), m.sb("rb2", [1, NEXP])
        x = m.sb("ex_x", [P, 2, BC])
        rh = m.sb("ex_rh", [P, BC])
        h1, h2 = m.sb("ex_h1", [P, 2, BC]), m.sb("ex_h2", [P, 2, BC])
        tot = m.sb("ex_tot", [P, BG, D])
        lg, pr, oh1, oh2, key, wt = (m.sb(f"ex_{n}", [P, BG, NEXP]) for n in ("lg", "pr", "oh1", "oh2", "key", "wt"))
        s = [m.sb(f"ex_s{i}", [P, BG, 1]) for i in range(8)]
        psh = m.ps("ex_psh", [P, 4, 512])
        psy = [m.ps(f"ex_psy{i}", [P, 512]) for i in range(3)]
        psl = m.ps("ex_psl", [P, 512])
        w_in, x_in, stored = m.sem("ex_w_in"), m.sem("ex_x_in"), m.sem("ex_stored")
        fixed = m.sem("ex_fixed")
        up = m.sem("ex_up")
        act_up = m.sem("ex_act_up")
        lgs, v, ydone, yadd = m.sem("ex_lgs"), m.sem("ex_v"), m.sem("ex_ydone"), m.sem("ex_yadd")
        expd, mixed = m.sem("ex_expd"), m.sem("ex_mixed")
        block = ctx.enter_context(nc.Block())
        UP = 2 + NEXP * 8
        NV = 24
        NY = NEXP * BG

        @block.sync
        def _(sp):
            sp.sem_inc(stored, 16)
            for to, frm in ((w1[:], io["ew1"]), (w2[:], io["ew2"]), (w3[:], io["ew3"]), (b1[:], io["eb1"]),
                            (b2[:], io["eb2"]), (b3[:], io["eb3"]), (rw1[:], rows2(io["rw1"])), (rb1[:], io["rb1"]),
                            (rw2[:], io["rw2"]), (rb2[:], io["rb2"])):
                sp.dma_start(to, frm).then_inc(w_in, 16)
            with sp.Fori(0, NG) as g:
                sp.wait_ge(stored, 16 * g + 16)
                sp.dma_start(tot[:], batch(x3, g)).then_inc(x_in, 16)
                sp.wait_ge(yadd, NY * g + NY + 3)
                sp.dma_start(batch(out, g), tot[:]).then_inc(stored, 16)
            sp.wait_ge(stored, 16 * NG + 16)

        @block.tensor
        def _(pe):
            pe.wait_ge(w_in, 160)
            pe.sem_inc(up, 1)
            with pe.Fori(0, NG) as g:
                n = [0]

                def pair(lhs, src, need):
                    for c in range(2):
                        bank = n[0] % 4
                        pe.wait_ge(act_up, UP * g + max(n[0] - 2, 1))
                        for k in range(2):
                            ins = pe.matmul(psh[:, bank, 0:HC], lhs[k], src[:, k, c * HC:(c + 1) * HC],
                                            start=(k == 0), stop=(k == 1))
                        ins.then_inc(up, 1)
                        n[0] += 1

                pe.wait_ge(fixed, g + 1)
                pair([rw1[:, k, :] for k in range(2)], x, None)
                pe.wait_ge(act_up, UP * g + 2 + 1)
                pe.wait_ge(v, NV * g + 1)
                for b in range(BG):
                    pe.matmul(psl[:, b * NEXP:(b + 1) * NEXP], rh[:, b * P:(b + 1) * P], rw2[:], start=True,
                              stop=False)
                    ins = pe.matmul(psl[:, b * NEXP:(b + 1) * NEXP], cst["ones"][0:1, :], rb2[:], start=False, stop=True)
                ins.then_inc(lgs, 1)
                for e in range(NEXP):
                    for mm in range(2):
                        pair([w1[:, e, k, mm * P:(mm + 1) * P] for k in range(2)], x, None)
                    pe.wait_ge(act_up, UP * g + n[0] + 1)
                    for mm in range(2):
                        pair([w2[:, e, k, mm * P:(mm + 1) * P] for k in range(2)], h1, None)
                    pe.wait_ge(act_up, UP * g + n[0] + 1)
                    for b in range(BG):
                        y = e * BG + b
                        pe.wait_ge(yadd, NY * g + y + 1)
                        for k in range(2):
                            pe.matmul(psy[y % 3][:, 0:D], h2[:, k, b * P:(b + 1) * P], w3[:, e, k, :],
                                      start=(k == 0), stop=False)
                        pe.matmul(psy[y % 3][:, 0:D], cst["ones"][0:1, :], b3[0:1, e, :], start=False, stop=True
                                  ).then_inc(ydone, 1)

        @block.scalar
        def _(act):
            act.wait_ge(w_in, 160)
            act.sem_inc(act_up, 1)
            with act.Fori(0, NG) as g:
                n = [0]

                def relu(to, bias, free=None):
                    for c in range(2):
                        act.wait_ge(up, UP * g + n[0] + 2)
                        if free is not None:
                            act.wait_ge(*free)
                        act.activation(to[:, c * HC:(c + 1) * HC], psh[:, n[0] % 4, 0:HC], ACT.Relu, bias=bias
                                       ).then_inc(act_up, 1)
                        n[0] += 1

                act.wait_ge(up, UP * g + 1)
                act.activation(x[:], xT[:, :, bass.ds(g * BC, BC)], ACT.Copy).then_inc(fixed, 1)
                relu(rh[:], rb1[:, 0:1])
                for e in range(NEXP):
                    for mm in range(2):
                        relu(h1[:, mm, :], b1[:, e, mm:mm + 1])
                    if e == 0:
                        act.wait_ge(v, NV * g + 4)
                        act.activation(pr[:], lg[:], ACT.Exp).then_inc(expd, 1)
                        act.wait_ge(v, NV * g + 17)
                        act.activation(s[5][:], s[4][:], ACT.Exp).then_inc(expd, 1)
                    for mm in range(2):
                        relu(h2[:, mm, :], b2[:, e, mm:mm + 1],
                             free=(ydone, NY * g + BG * e) if e else (yadd, NY * g + 1))

        @block.vector
        def _(dve):
            dve.wait_ge(w_in, 160)
            dve.sem_inc(yadd, 3)
            dve.sem_inc(v, 1)
            with dve.Fori(0, NG) as g:
                at = [0]

                def link(ins):
                    at[0] += 1
                    ins.then_inc(v, 1)
                    dve.wait_ge(v, NV * g + at[0] + 1)

                def wide(t):
                    return t[:].to_broadcast([P, BG, NEXP])

                iota = cst["iota"][:, 0:NEXP].unsqueeze(1).to_broadcast([P, BG, NEXP])

                def pick(first, val, oh):
                    link(dve.tensor_tensor(key[:], pr[:], wide(val), ALU.not_equal))
                    link(dve.tensor_scalar(key[:], key[:], 64.0, None, ALU.mult))
                    link(dve.tensor_tensor(key[:], key[:], iota, ALU.add))
                    link(dve.tensor_reduce(first[:], key[:], AX.X, ALU.min))
                    link(dve.tensor_tensor(oh[:], iota, wide(first), ALU.is_equal))

                dve.wait_ge(lgs, g + 1)
                lv = psl[:, 0:BG * NEXP].rearrange("p (b e) -> p b e", b=BG)
                link(dve.tensor_copy(lg[:], lv))
                link(dve.tensor_reduce(s[0][:], lg[:], AX.X, ALU.max))
                link(dve.tensor_tensor(lg[:], lg[:], wide(s[0]), ALU.subtract))
                dve.wait_ge(expd, 2 * g + 1)
                link(dve.tensor_reduce(s[1][:], pr[:], AX.X, ALU.add))
                link(dve.reciprocal(s[1][:], s[1][:]))
                link(dve.tensor_tensor(pr[:], pr[:], wide(s[1]), ALU.mult))
                link(dve.tensor_reduce(s[2][:], pr[:], AX.X, ALU.max))
                pick(s[3], s[2], oh1)
                link(dve.scalar_tensor_tensor(out=pr[:], in0=oh1[:], scalar=-4.0, in1=pr[:], op0=ALU.mult,
                                              op1=ALU.add))
                link(dve.tensor_reduce(s[6][:], pr[:], AX.X, ALU.max))
                link(dve.tensor_tensor(s[4][:], s[6][:], s[2][:], ALU.subtract))
                link(dve.tensor_copy(s[7][:], s[2][:]))
                dve.wait_ge(expd, 2 * g + 2)
                pick(s[3], s[6], oh2)
                link(dve.tensor_scalar(s[0][:], s[5][:], 1.0, None, ALU.add))
                link(dve.reciprocal(s[0][:], s[0][:]))
                link(dve.tensor_tensor(oh2[:], oh2[:], wide(s[5]), ALU.mult))
                assert at[0] == NV
                dve.tensor_tensor(oh1[:], oh1[:], oh2[:], ALU.add).then_inc(mixed, 1)
                dve.wait_ge(mixed, 2 * g + 1)
                dve.tensor_tensor(wt[:], oh1[:], wide(s[0]), ALU.mult).then_inc(mixed, 1)
                dve.wait_ge(mixed, 2 * g + 2)
                dve.wait_ge(x_in, 16 * g + 16)
                for e in range(NEXP):
                    for b in range(BG):
                        y = e * BG + b
                        dve.wait_ge(ydone, NY * g + y + 1)
                        if e:
                            dve.wait_ge(yadd, NY * g + y - BG + 1 + 3)
                        dve.scalar_tensor_tensor(out=tot[:, b, :], in0=psy[y % 3][:, 0:D], scalar=wt[:, b, e:e + 1],
                                                 in1=tot[:, b, :], op0=ALU.mult, op1=ALU.add).then_inc(yadd, 1)


def make_edge_rows(dve, link, g, bufs, pre, tmp, psH):
    link(dve.tensor_copy(pre[:], turned_back(psH)))


def build(nc, io, out):
    def dram(name, shape, dt=F32):
        return nc.dram_tensor(name, shape, dt, kind="Internal").ap()

    Mem.semaphores = []
    with ExitStack() as ctx:
        m = Mem(nc, ctx)
        cst = {
            "ident": m.sb("ident", [P, P]), "iota": m.sb("iota", [P, P]), "ones": m.sb("ones", [P, P]),
            "rel": m.sb("rel", [P, 2, NT + 2]), "first": m.sb("first", [1, 2, NT], I32),
            "wide": m.sb("wide", [1, 2], I32),
            "slope": m.sb("slope", [P, 1]), "start": m.sb("run_start", [P, NB], I32), "runs": dram("runs", (EP, H8)),
        }
        cst["loads"] = [("slope", io["prelu_a"].to_broadcast([P, 1]))]
        stage_constants(nc, cst, io)
        tables = [dram(f"table{i}", (NP_, D)) for i in range(2)]
        xn_d, x1_d, x2_d, x3_d = (dram(n, (NP_, D)) for n in ("xn_d", "x1_d", "x2_d", "x3_d"))
        xp = dram("xp_d", (L, P, 2 * Q4))

        with ExitStack() as lctx:
            acc = Mem(nc, lctx).sb("acc", [P, 3, NP_ + P])
            hist = acc[:, 0:2, 0:NP_]
            with ExitStack() as gctx:
                gm = Mem(nc, gctx)
                w1, w2 = gm.sb("w1", [P, 2, D]), gm.sb("w2", [P, 2, D])
                b1, b2 = gm.sb("b1", [P, D]), gm.sb("b2", [P, D])
                stage_load(nc, "gw", [(w1, rows2(io["W1T"])), (w2, rows2(io["W2T"])),
                                      (b1, io["b1"].to_broadcast([P, D])), (b2, io["b2"].to_broadcast([P, D]))])
                stage_nodes(nc, cst, "n1", make_plain, 1, loads=[io["x"]], keep=xn_d, keep_row=True, proj=w1,
                            outs=[(tables[0], 0, D)])
                stage_gather_sum(nc, cst, "s1", tables[0], io["idx"], acc, parts=3)
                stage_run_starts(nc, cst, acc)
                stage_over_degree(nc, cst, "d1", acc, new=True)
                stage_nodes(nc, cst, "e1", make_edge_rows, 1, norm=False, keep=tables[1], hT=acc)
                stage_gather_sum(nc, cst, "s2", tables[1], io["idx"], acc)
                stage_over_degree(nc, cst, "d2", acc, new=False)

                def make_mid(dve, link, g, bufs, pre, tmp, psH):
                    bias_and_prelu(dve, link, psH, pre, tmp, b1, cst["slope"])

                stage_nodes(nc, cst, "n2", make_mid, 3, norm=False, hT=acc, proj=w2, outs=[(tables[0], 0, D)])
                stage_gather_sum(nc, cst, "s3", tables[0], io["idx"], acc)
                stage_over_degree(nc, cst, "d3", acc, new=False)
                stage_nodes(nc, cst, "e2", make_edge_rows, 1, norm=False, keep=tables[1], hT=acc)
                stage_gather_sum(nc, cst, "s4", tables[1], io["idx"], acc)
                stage_over_degree(nc, cst, "d4", acc, new=False)

                def make_x1(dve, link, g, bufs, pre, tmp, psH):
                    bias_and_prelu(dve, link, psH, pre, tmp, b2, cst["slope"], skip=bufs[1])
                    link(dve.tensor_tensor(pre[:], pre[:], bufs[0][:], ALU.add))

                stage_nodes(nc, cst, "n3", make_x1, 5, loads=[io["x"], xn_d], keep=x1_d, hT=acc, xT=hist)
            renew_semaphores(nc)
            stage_lstm_inputs(nc, cst, io, hist, xp)
            with ExitStack() as sctx:
                sm = Mem(nc, sctx)
                mem = {"whh": sm.sb("whh", [P, 2, 4 * D]), "h": sm.sb("h", [P, 2, C]), "qc": sm.sb("qc", [P, 2, 2 * C]),
                       "gs": sm.sb("gs", [P, 2, 3 * C]), "nxt": sm.sb("nxt", [P, 4, C]),
                       "start": sm.sb("start", [P, 4, C]), "settled": sm.sb("settled", [1, 1], I32), "hist": hist}
                stage_clear(nc, "lz", [mem["nxt"][:], hist[:, :, N:NP_]])
                stage_load(nc, "lw", [(mem["whh"], rows2(io["WhhT"]))])
                stage_sweeps(nc, cst, mem, xp, "sg", 1, skip=10)
                stage_sweeps(nc, cst, mem, xp, "sw", 1)
                stage_sweeps(nc, cst, mem, xp, "sx", C - 1, unless=mem["settled"])
            renew_semaphores(nc)
            stage_gated_sums(nc, cst, io, hist)
            with ExitStack() as actx:
                am = Mem(nc, actx)
                proj = am.sb("head_proj", [P, 2, D + 2 * H8])
                stage_head_scores(nc, cst, io, proj)
                h_t, s_seg = dram("h_t", (NP_, D + H8)), dram("s_seg", (NP_, H8))

                def make_x2(dve, link, g, bufs, pre, tmp, psH):
                    link(dve.tensor_tensor(pre[:], turned_back(psH), bufs[0][:], ALU.add))

                stage_nodes(nc, cst, "n4", make_x2, 1, loads=[x1_d], keep=x2_d, hT=hist, proj=proj,
                            outs=[(h_t, 0, D + H8), (s_seg, D + H8, D + 2 * H8)])
        with ExitStack() as ectx:
            em = Mem(nc, ectx)
            lines = dram("score_lines", (NT * H8, 3 * P + 2))
            stage_own_scores(nc, cst, io, s_seg, lines)
            acc = em.sb("acc_att", [P, 3, NP_ + P])
            x3T = acc[:, 0:2, 0:NP_]
            stage_attention(nc, cst, io, h_t, lines, acc)
            stage_over_sums(nc, cst, io, acc)
            stage_nodes(nc, cst, "n5", make_x2, 1, loads=[x2_d], keep=x3_d, hT=acc, xT=x3T)
            stage_experts(nc, cst, io, x3T, x3_d, out)


def layout(z):
    import numpy as np
    a = {k: np.asarray(v) for k, v in z.items()}
    src = np.concatenate([a["src"], np.zeros(EP - E, np.int32)]).reshape(NT, P)
    dst = np.concatenate([a["dst"], np.full(EP - E, NP_ - 1, np.int32)]).reshape(NT, P)
    tiles = lambda t: np.ascontiguousarray(t.reshape(NIT, TIT, P).transpose(0, 2, 1))
    row = lambda v: np.ascontiguousarray(v.reshape(1, -1))
    gate_cols = lambda v: np.ascontiguousarray(v.reshape(4, 2, P)[list(GATES)].transpose(2, 1, 0).reshape(P, 8))
    half_cols = lambda v: np.ascontiguousarray(v.reshape(-1, P).T)
    flat = dst.reshape(-1)
    ringed = np.concatenate([[-1], flat, [-1]]).astype(np.int32)
    piece = EP // TIT
    pieces = np.stack([ringed[j * piece:j * piece + piece + 2] for j in range(TIT)])
    halves = lambda w: np.ascontiguousarray(w.reshape(NEXP, 2, P, D).transpose(2, 0, 1, 3))
    cols2 = lambda b: np.ascontiguousarray(b.reshape(NEXP, 2, P).transpose(2, 0, 1))
    return {
        "x": np.concatenate([a["x"], np.zeros((NP_ - N, D), np.float32)]),
        "idx": tiles(src),
        "dstT": np.ascontiguousarray(dst.T),
        "prelu_a": a["L0_gnn_prelu_a"].reshape(1, 1),
        "W1T": np.ascontiguousarray(a["L0_gnn_W1"].T), "W2T": np.ascontiguousarray(a["L0_gnn_W2"].T),
        "WihT": np.ascontiguousarray(a["L0_ffn_W_ih"].T), "WhhT": np.ascontiguousarray(a["L0_ffn_W_hh"].T),
        "b_ih": gate_cols(a["L0_ffn_b_ih"]), "b_hh": gate_cols(a["L0_ffn_b_hh"]),
        "W_lin": np.ascontiguousarray(a["L0_ffn_W_lin"].reshape(2, 2, P).transpose(2, 1, 0)),
        "b_lin": row(a["L0_ffn_b_lin"]), "fw": half_cols(a["L0_ffn_fw_att"]), "bw": half_cols(a["L0_ffn_bw_att"]),
        "dst_pieces": pieces, "headW": np.ascontiguousarray(a["L1_gnn_W"].transpose(1, 0, 2).reshape(D, D)),
        "headWT": np.ascontiguousarray(a["L1_gnn_W"].transpose(2, 0, 1)),
        "headA": np.ascontiguousarray(a["L1_gnn_a"].reshape(H8, 2, D // H8).transpose(2, 1, 0)),
        "ew1": halves(a["L1_ffn_expert_w1"]), "ew2": halves(a["L1_ffn_expert_w2"]),
        "ew3": halves(a["L1_ffn_expert_w3"]), "eb1": cols2(a["L1_ffn_expert_b1"]), "eb2": cols2(a["L1_ffn_expert_b2"]),
        "eb3": np.ascontiguousarray(a["L1_ffn_expert_b3"][None]), "rw1": a["L1_ffn_router_w1"],
        "rb1": a["L1_ffn_router_b1"].reshape(P, 1), "rw2": a["L1_ffn_router_w2"], "rb2": row(a["L1_ffn_router_b2"]),
        "head_sel": (np.arange(P)[:, None] == 16 * (np.arange(D)[None] // 32)).astype(np.float32),
        "head_spread": np.concatenate([np.arange(D)[None] // 32 == np.arange(H8)[:, None],
                                       np.arange(P)[None] // 16 == np.arange(H8)[:, None]], 1).astype(np.float32),
        "b1": row(a["L0_gnn_b1"]), "b2": row(a["L0_gnn_b2"]),
    }


def kernel(**inputs):
    import numpy as np
    import concourse.bacc as bacc
    from concourse.bass_utils import run_bass_kernel_spmd

    nc = bacc.Bacc("TRN2", target_bir_lowering=False, num_devices=1)
    arrays = layout(inputs)
    io = {k: nc.dram_tensor(f"in_{k}", a.shape, mybir.dt.from_np(a.dtype), kind="ExternalInput").ap()
          for k, a in arrays.items()}
    out = nc.dram_tensor("out", (NP_, D), F32, kind="ExternalOutput").ap()
    build(nc, io, out)
    r = run_bass_kernel_spmd(nc, [{f"in_{k}": a for k, a in arrays.items()}], core_ids=[0])
    return r.results[0]["out"][0:N]
```
